# Optimizing a Trainium2 kernel written in Bass

```python
import numpy as np
import jax
import jax.numpy as jnp

def _softmax(x, axis=-1):
    return jax.nn.softmax(x, axis=axis)

def _gelu(x):
    return jax.nn.gelu(x, approximate=True)

def _silu(x):
    return jax.nn.silu(x)

def _sigmoid(x):
    return jax.nn.sigmoid(x)

def _layernorm(x, axis=-1, eps=1e-05):
    m = jnp.mean(x, axis=axis, keepdims=True)
    v = jnp.var(x, axis=axis, keepdims=True)
    return (x - m) / jnp.sqrt(v + eps)

def _scatter_add(tgt, idx, src, axis=0):
    return tgt.at[idx].add(src)

def _segment_sum(src, seg, n):
    return jax.ops.segment_sum(src, seg, n)
kernel_name = 'mk_macaron_d2_jaxref_r8_5292e3'

def setup_inputs(seed: int=0):
    np.random.seed(seed)
    _w = jnp.asarray

    def _L0_attn_setup():
        import jax, jax.numpy as jnp
        import numpy as np
        H_M, P_M, G_M, N_M, K_CONV, CHUNK = (128, 64, 8, 128, 4, 128)
        D_MODEL = 512
        D_INNER = H_M * P_M
        CONV_DIM = D_INNER + 2 * G_M * N_M
        PROJ_DIM = D_INNER + CONV_DIM + H_M
        EPS = 1e-05

        def segsum(x):
            l = x.shape[-1]
            xe = jnp.broadcast_to(x[..., None], x.shape + (l,))
            m1 = jnp.tril(jnp.ones((l, l), dtype=bool), -1)
            s = jnp.cumsum(jnp.where(m1, xe, 0.0), axis=-2)
            m2 = jnp.tril(jnp.ones((l, l), dtype=bool), 0)
            return jnp.where(m2, s, -jnp.inf)

        def causal_conv(x, w, bconv):
            k = w.shape[1]
            s = x.shape[1]
            xp = jnp.pad(x, ((0, 0), (k - 1, 0), (0, 0)))
            y = sum((xp[:, i:i + s, :] * w[:, i] for i in range(k)))
            return y + bconv
        key = jax.random.key(seed)
        ks = jax.random.split(key, 8)
        B_, S = (1, 256)
        sc = 0.02
        return {'x': jax.random.normal(ks[0], (B_, S, D_MODEL), dtype=jnp.float32), 'norm_w': jnp.ones((D_MODEL,), dtype=jnp.float32), 'in_proj_w': jax.random.normal(ks[1], (PROJ_DIM, D_MODEL), dtype=jnp.float32) * sc, 'conv_w': jax.random.normal(ks[2], (CONV_DIM, K_CONV), dtype=jnp.float32) * 0.2, 'conv_b': jnp.zeros((CONV_DIM,), dtype=jnp.float32), 'dt_bias': jax.random.uniform(ks[3], (H_M,), dtype=jnp.float32) * 0.1, 'A_log': jnp.log(1.0 + 15.0 * jax.random.uniform(ks[4], (H_M,), dtype=jnp.float32)), 'Dp': jnp.ones((H_M,), dtype=jnp.float32), 'gnorm_w': jnp.ones((D_INNER,), dtype=jnp.float32), 'out_proj_w': jax.random.normal(ks[5], (D_MODEL, D_INNER), dtype=jnp.float32) * sc}
    _L0_attn_in = _L0_attn_setup()

    def _L0_ffn_setup():
        import jax, jax.numpy as jnp
        import numpy as np
        GROUP = 64

        def dequant_q40(w, s, out_features, in_features):
            msb = w >> 4
            lsb = (w & 15 ^ 8) - 8
            g = jnp.concatenate([msb, lsb], axis=1).reshape(-1, GROUP)
            deq = g.astype(s.dtype) * s[:, None]
            return deq.reshape(out_features, in_features)
        key = jax.random.key(seed)
        ks = jax.random.split(key, 7)
        dim, hidden = (512, 1376)
        B, S = (2, 256)

        def packed(k, din, dout):
            return jax.random.randint(k, (din * dout // GROUP // 2, GROUP), -128, 128, dtype=jnp.int32)

        def scales(k, din, dout):
            return (jax.random.uniform(k, (din * dout // GROUP,), dtype=jnp.float32) + 0.5) * 0.01
        x = jax.random.normal(ks[0], (B, S, dim), dtype=jnp.float32)
        w1 = packed(ks[1], dim, hidden)
        s1 = scales(ks[2], dim, hidden)
        w2 = packed(ks[3], hidden, dim)
        s2 = scales(ks[4], hidden, dim)
        w3 = packed(ks[5], dim, hidden)
        s3 = scales(ks[6], dim, hidden)
        return {'x': x, 'w1': w1, 's1': s1, 'w2': w2, 's2': s2, 'w3': w3, 's3': s3}
    _L0_ffn_in = _L0_ffn_setup()

    def _L1_attn_setup():
        import jax, jax.numpy as jnp
        import numpy as np
        B, S, HID = (1, 256, 512)
        NH, NKV = (32, 8)
        HD = HID // NH
        GROUPS = NH // NKV
        ROPE_THETA = 10000.0

        def _rope_cos_sin(seq_len, head_dim, dtype=jnp.float32):
            inv_freq = 1.0 / ROPE_THETA ** (jnp.arange(0, head_dim, 2, dtype=jnp.float32) / head_dim)
            t = jnp.arange(seq_len, dtype=jnp.float32)
            freqs = jnp.outer(t, inv_freq)
            emb = jnp.concatenate([freqs, freqs], axis=-1)
            return (jnp.cos(emb).astype(dtype), jnp.sin(emb).astype(dtype))

        def _rotate_half(x):
            x1, x2 = jnp.split(x, 2, axis=-1)
            return jnp.concatenate([-x2, x1], axis=-1)

        def _apply_rope(x, cos, sin):
            return x * cos[None, None] + _rotate_half(x) * sin[None, None]
        key = jax.random.key(seed)
        k1, k2, k3, k4, k5 = jax.random.split(key, 5)
        return {'hidden_states': jax.random.normal(k1, (B, S, HID), jnp.float32), 'Wq': jax.random.normal(k2, (NH * HD, HID), jnp.float32) * 0.02, 'Wk': jax.random.normal(k3, (NKV * HD, HID), jnp.float32) * 0.02, 'Wv': jax.random.normal(k4, (NKV * HD, HID), jnp.float32) * 0.02, 'Wo': jax.random.normal(k5, (HID, NH * HD), jnp.float32) * 0.02}
    _L1_attn_in = _L1_attn_setup()

    def _L1_ffn_setup():
        import jax, jax.numpy as jnp
        import numpy as np
        HID, BOT, RDIM, NSLOT, K, VB = (512, 64, 48, 128, 8, 32)
        TAU_LOW, TAU_HIGH, EARLY_EXIT = (0.5, 2.0, 0.05)

        def _uncertainty(h, Wu1, bu1, Wu2, bu2):
            var = jnp.var(h, axis=-1)
            log_var = jnp.log1p(var)
            norm_var = log_var / (jnp.mean(log_var) + 1e-06)
            learned = (jax.nn.gelu(h @ Wu1.T + bu1) @ Wu2.T + bu2)[..., 0]
            return jnp.clip(norm_var * 0.5 + jax.nn.sigmoid(learned) * 2.5, 0.0, 5.0)
        key = jax.random.key(seed)
        ks = jax.random.split(key, 12)
        B, S = (2, 256)
        return {'hidden_states': jax.random.normal(ks[0], (B, S, HID), dtype=jnp.float32), 'Wq': jax.random.normal(ks[1], (BOT, HID), dtype=jnp.float32) / np.sqrt(HID), 'Wr': jax.random.normal(ks[2], (RDIM, BOT), dtype=jnp.float32) / np.sqrt(BOT), 'aux_keys': jax.random.normal(ks[3], (NSLOT, BOT), dtype=jnp.float32) * 0.01, 'aux_values': jax.random.normal(ks[4], (NSLOT, HID), dtype=jnp.float32) * 0.02, 'Wvd': jax.random.normal(ks[5], (VB, HID), dtype=jnp.float32) * 0.1 / np.sqrt(HID), 'Wvu': jax.random.normal(ks[6], (HID, VB), dtype=jnp.float32) * 0.1 / np.sqrt(VB), 'Wu1': jax.random.normal(ks[7], (HID // 4, HID), dtype=jnp.float32) / np.sqrt(HID), 'bu1': jnp.zeros((HID // 4,), dtype=jnp.float32), 'Wu2': jax.random.normal(ks[8], (1, HID // 4), dtype=jnp.float32) * 0.01, 'bu2': jnp.zeros((1,), dtype=jnp.float32), 'gate_w1': jnp.float32(0.5), 'gate_bias': jnp.float32(-1.0), 'log_rel': jnp.zeros((NSLOT,), dtype=jnp.float32)}
    _L1_ffn_in = _L1_ffn_setup()
    _d = {'L0_attn_x': _L0_attn_in['x'], 'L0_attn_norm_w': _L0_attn_in['norm_w'], 'L0_attn_in_proj_w': _L0_attn_in['in_proj_w'], 'L0_attn_conv_w': _L0_attn_in['conv_w'], 'L0_attn_conv_b': _L0_attn_in['conv_b'], 'L0_attn_dt_bias': _L0_attn_in['dt_bias'], 'L0_attn_A_log': _L0_attn_in['A_log'], 'L0_attn_Dp': _L0_attn_in['Dp'], 'L0_attn_gnorm_w': _L0_attn_in['gnorm_w'], 'L0_attn_out_proj_w': _L0_attn_in['out_proj_w'], 'L0_ffn_w1': _L0_ffn_in['w1'], 'L0_ffn_s1': _L0_ffn_in['s1'], 'L0_ffn_w2': _L0_ffn_in['w2'], 'L0_ffn_s2': _L0_ffn_in['s2'], 'L0_ffn_w3': _L0_ffn_in['w3'], 'L0_ffn_s3': _L0_ffn_in['s3'], 'L1_attn_Wq': _L1_attn_in['Wq'], 'L1_attn_Wk': _L1_attn_in['Wk'], 'L1_attn_Wv': _L1_attn_in['Wv'], 'L1_attn_Wo': _L1_attn_in['Wo'], 'L1_ffn_Wq': _L1_ffn_in['Wq'], 'L1_ffn_Wr': _L1_ffn_in['Wr'], 'L1_ffn_aux_keys': _L1_ffn_in['aux_keys'], 'L1_ffn_aux_values': _L1_ffn_in['aux_values'], 'L1_ffn_Wvd': _L1_ffn_in['Wvd'], 'L1_ffn_Wvu': _L1_ffn_in['Wvu'], 'L1_ffn_Wu1': _L1_ffn_in['Wu1'], 'L1_ffn_bu1': _L1_ffn_in['bu1'], 'L1_ffn_Wu2': _L1_ffn_in['Wu2'], 'L1_ffn_bu2': _L1_ffn_in['bu2'], 'L1_ffn_gate_w1': _L1_ffn_in['gate_w1'], 'L1_ffn_gate_bias': _L1_ffn_in['gate_bias'], 'L1_ffn_log_rel': _L1_ffn_in['log_rel']}
    _x0 = _d['L0_attn_x']
    _d['L0_attn_x'] = jax.random.normal(jax.random.fold_in(jax.random.key(seed), 1), (2, 512, 512), dtype=_x0.dtype)
    del _x0
    return _d

def reference(L0_attn_x, L0_attn_norm_w, L0_attn_in_proj_w, L0_attn_conv_w, L0_attn_conv_b, L0_attn_dt_bias, L0_attn_A_log, L0_attn_Dp, L0_attn_gnorm_w, L0_attn_out_proj_w, L0_ffn_w1, L0_ffn_s1, L0_ffn_w2, L0_ffn_s2, L0_ffn_w3, L0_ffn_s3, L1_attn_Wq, L1_attn_Wk, L1_attn_Wv, L1_attn_Wo, L1_ffn_Wq, L1_ffn_Wr, L1_ffn_aux_keys, L1_ffn_aux_values, L1_ffn_Wvd, L1_ffn_Wvu, L1_ffn_Wu1, L1_ffn_bu1, L1_ffn_Wu2, L1_ffn_bu2, L1_ffn_gate_w1, L1_ffn_gate_bias, L1_ffn_log_rel):

    def _L0_attn_ref(x, norm_w, in_proj_w, conv_w, conv_b, dt_bias, A_log, Dp, gnorm_w, out_proj_w):
        import jax, jax.numpy as jnp
        import numpy as np
        H_M, P_M, G_M, N_M, K_CONV, CHUNK = (128, 64, 8, 128, 4, 128)
        D_MODEL = 512
        D_INNER = H_M * P_M
        CONV_DIM = D_INNER + 2 * G_M * N_M
        PROJ_DIM = D_INNER + CONV_DIM + H_M
        EPS = 1e-05

        def segsum(x):
            l = x.shape[-1]
            xe = jnp.broadcast_to(x[..., None], x.shape + (l,))
            m1 = jnp.tril(jnp.ones((l, l), dtype=bool), -1)
            s = jnp.cumsum(jnp.where(m1, xe, 0.0), axis=-2)
            m2 = jnp.tril(jnp.ones((l, l), dtype=bool), 0)
            return jnp.where(m2, s, -jnp.inf)

        def causal_conv(x, w, bconv):
            k = w.shape[1]
            s = x.shape[1]
            xp = jnp.pad(x, ((0, 0), (k - 1, 0), (0, 0)))
            y = sum((xp[:, i:i + s, :] * w[:, i] for i in range(k)))
            return y + bconv
        b, s, _ = x.shape
        residual = x
        h = x * jax.lax.rsqrt(jnp.mean(x * x, axis=-1, keepdims=True) + EPS) * norm_w
        proj = jnp.einsum('bsd,od->bso', h, in_proj_w)
        gate = proj[..., :D_INNER]
        hBC = proj[..., D_INNER:D_INNER + CONV_DIM]
        dt = proj[..., D_INNER + CONV_DIM:]
        hBC = jax.nn.silu(causal_conv(hBC, conv_w, conv_b))
        hid = hBC[..., :D_INNER].reshape(b, s, H_M, P_M)
        B = hBC[..., D_INNER:D_INNER + G_M * N_M].reshape(b, s, G_M, N_M)
        C = hBC[..., D_INNER + G_M * N_M:].reshape(b, s, G_M, N_M)
        dt = jax.nn.softplus(dt + dt_bias)
        A = -jnp.exp(A_log)
        pad = -s % CHUNK
        D_res = Dp[None, None, :, None] * hid
        hid_dt = hid * dt[..., None]
        A_full = A[None, None, :] * dt

        def padseq(t):
            return jnp.pad(t, [(0, 0), (0, pad)] + [(0, 0)] * (t.ndim - 2))
        hid_dt, A_full, Bp, Cp = (padseq(hid_dt), padseq(A_full), padseq(B), padseq(C))
        S = s + pad
        c, l = (S // CHUNK, CHUNK)
        hc = hid_dt.reshape(b, c, l, H_M, P_M)
        Ac = A_full.reshape(b, c, l, H_M).transpose(0, 3, 1, 2)
        rep = H_M // G_M
        Bh = jnp.repeat(Bp.reshape(b, c, l, G_M, N_M), rep, axis=3)
        Ch = jnp.repeat(Cp.reshape(b, c, l, G_M, N_M), rep, axis=3)
        A_cs = jnp.cumsum(Ac, axis=-1)
        L = jnp.exp(segsum(Ac))
        M = jnp.einsum('bcihn,bcjhn->bcijh', Ch, Bh) * jnp.transpose(L, (0, 2, 3, 4, 1))
        Y_diag = jnp.einsum('bcijh,bcjhp->bcihp', M, hc)
        decay_states = jnp.exp(A_cs[..., -1:] - A_cs)
        states = jnp.einsum('bclhn,bhcl,bclhp->bchpn', Bh, decay_states, hc)
        A_last = jnp.pad(A_cs[..., -1], ((0, 0), (0, 0), (1, 0)))
        decay_chunk = jnp.exp(segsum(A_last))
        states_cat = jnp.concatenate([jnp.zeros_like(states[:, :1]), states], axis=1)
        prev_states = jnp.einsum('bhij,bjhpn->bihpn', decay_chunk, states_cat)[:, :-1]
        Y_off = jnp.einsum('bclhn,bchpn,bhcl->bclhp', Ch, prev_states, jnp.exp(A_cs))
        y = (Y_diag + Y_off).reshape(b, S, H_M, P_M)[:, :s] + D_res
        y = y.reshape(b, s, D_INNER)
        yg = y * jax.nn.silu(gate)
        gsz = D_INNER // G_M
        ygr = yg.reshape(b, s, G_M, gsz)
        ygr = ygr * jax.lax.rsqrt(jnp.mean(ygr * ygr, axis=-1, keepdims=True) + EPS)
        y = ygr.reshape(b, s, D_INNER) * gnorm_w
        out = jnp.einsum('bsd,od->bso', y, out_proj_w)
        return residual + out

    def _L0_ffn_ref(x, w1, s1, w2, s2, w3, s3):
        import jax, jax.numpy as jnp
        import numpy as np
        GROUP = 64

        def dequant_q40(w, s, out_features, in_features):
            msb = w >> 4
            lsb = (w & 15 ^ 8) - 8
            g = jnp.concatenate([msb, lsb], axis=1).reshape(-1, GROUP)
            deq = g.astype(s.dtype) * s[:, None]
            return deq.reshape(out_features, in_features)
        dim = x.shape[-1]
        hidden = w1.shape[0] * w1.shape[1] * 2 // dim
        W1 = dequant_q40(w1, s1, hidden, dim)
        W3 = dequant_q40(w3, s3, hidden, dim)
        W2 = dequant_q40(w2, s2, dim, hidden)
        a = jnp.einsum('bsd,hd->bsh', x, W1)
        b = jnp.einsum('bsd,hd->bsh', x, W3)
        h = jax.nn.silu(a) * b
        return jnp.einsum('bsh,dh->bsd', h, W2)

    def _L1_attn_ref(hidden_states, Wq, Wk, Wv, Wo):
        import jax, jax.numpy as jnp
        import numpy as np
        B, S, HID = (1, 256, 512)
        NH, NKV = (32, 8)
        HD = HID // NH
        GROUPS = NH // NKV
        ROPE_THETA = 10000.0

        def _rope_cos_sin(seq_len, head_dim, dtype=jnp.float32):
            inv_freq = 1.0 / ROPE_THETA ** (jnp.arange(0, head_dim, 2, dtype=jnp.float32) / head_dim)
            t = jnp.arange(seq_len, dtype=jnp.float32)
            freqs = jnp.outer(t, inv_freq)
            emb = jnp.concatenate([freqs, freqs], axis=-1)
            return (jnp.cos(emb).astype(dtype), jnp.sin(emb).astype(dtype))

        def _rotate_half(x):
            x1, x2 = jnp.split(x, 2, axis=-1)
            return jnp.concatenate([-x2, x1], axis=-1)

        def _apply_rope(x, cos, sin):
            return x * cos[None, None] + _rotate_half(x) * sin[None, None]
        bsz, q_len, _ = hidden_states.shape
        q = (hidden_states @ Wq.T).reshape(bsz, q_len, NH, HD).transpose(0, 2, 1, 3)
        k = (hidden_states @ Wk.T).reshape(bsz, q_len, NKV, HD).transpose(0, 2, 1, 3)
        v = (hidden_states @ Wv.T).reshape(bsz, q_len, NKV, HD).transpose(0, 2, 1, 3)
        cos, sin = _rope_cos_sin(q_len, HD, hidden_states.dtype)
        q = _apply_rope(q, cos, sin)
        k = _apply_rope(k, cos, sin)
        k = jnp.repeat(k, GROUPS, axis=1)
        v = jnp.repeat(v, GROUPS, axis=1)
        scale = 1.0 / jnp.sqrt(jnp.asarray(HD, hidden_states.dtype))
        logits = jnp.einsum('bhqd,bhkd->bhqk', q, k) * scale
        causal = jnp.tril(jnp.ones((q_len, q_len), dtype=bool))
        logits = jnp.where(causal[None, None], logits, jnp.finfo(logits.dtype).min)
        attn = jax.nn.softmax(logits, axis=-1)
        out = jnp.einsum('bhqk,bhkd->bhqd', attn, v)
        out = out.transpose(0, 2, 1, 3).reshape(bsz, q_len, NH * HD)
        return out @ Wo.T

    def _L1_ffn_ref(hidden_states, Wq, Wr, aux_keys, aux_values, Wvd, Wvu, Wu1, bu1, Wu2, bu2, gate_w1, gate_bias, log_rel):
        import jax, jax.numpy as jnp
        import numpy as np
        HID, BOT, RDIM, NSLOT, K, VB = (512, 64, 48, 128, 8, 32)
        TAU_LOW, TAU_HIGH, EARLY_EXIT = (0.5, 2.0, 0.05)

        def _uncertainty(h, Wu1, bu1, Wu2, bu2):
            var = jnp.var(h, axis=-1)
            log_var = jnp.log1p(var)
            norm_var = log_var / (jnp.mean(log_var) + 1e-06)
            learned = (jax.nn.gelu(h @ Wu1.T + bu1) @ Wu2.T + bu2)[..., 0]
            return jnp.clip(norm_var * 0.5 + jax.nn.sigmoid(learned) * 2.5, 0.0, 5.0)
        query = hidden_states @ Wq.T
        rq = query @ Wr.T
        rk = aux_keys @ Wr.T
        router_scores = jnp.einsum('bsr,nr->bsn', rq, rk) / np.sqrt(RDIM) + log_rel
        top_scores, top_idx = jax.lax.top_k(router_scores, K)
        sel_keys = aux_keys[top_idx]
        attn = jnp.einsum('bsd,bskd->bsk', query, sel_keys) / np.sqrt(BOT) + log_rel[top_idx]
        w = jax.nn.softmax(attn, axis=-1)
        sel_vals = aux_values[top_idx]
        aux_out = jnp.einsum('bsk,bskh->bsh', w, sel_vals)
        aux_out = aux_out @ Wvd.T @ Wvu.T
        u = _uncertainty(hidden_states, Wu1, bu1, Wu2, bu2)
        u_norm = jnp.clip((u - TAU_LOW) / (TAU_HIGH - TAU_LOW), 0.0, 1.0)
        gate = jax.nn.sigmoid(gate_w1 * u_norm + gate_bias)
        gate = jnp.where(gate < EARLY_EXIT, 0.0, gate)
        return hidden_states + gate[..., None] * aux_out
    x = L0_attn_x
    x = x + 0.5 * _L0_ffn_ref(_layernorm(x, axis=-1), L0_ffn_w1, L0_ffn_s1, L0_ffn_w2, L0_ffn_s2, L0_ffn_w3, L0_ffn_s3)
    x = x + _L0_attn_ref(_layernorm(x, axis=-1), L0_attn_norm_w, L0_attn_in_proj_w, L0_attn_conv_w, L0_attn_conv_b, L0_attn_dt_bias, L0_attn_A_log, L0_attn_Dp, L0_attn_gnorm_w, L0_attn_out_proj_w)
    x = x + 0.5 * _L0_ffn_ref(_layernorm(x, axis=-1), L0_ffn_w1, L0_ffn_s1, L0_ffn_w2, L0_ffn_s2, L0_ffn_w3, L0_ffn_s3)
    x = x + 0.5 * _L1_ffn_ref(_layernorm(x, axis=-1), L1_ffn_Wq, L1_ffn_Wr, L1_ffn_aux_keys, L1_ffn_aux_values, L1_ffn_Wvd, L1_ffn_Wvu, L1_ffn_Wu1, L1_ffn_bu1, L1_ffn_Wu2, L1_ffn_bu2, L1_ffn_gate_w1, L1_ffn_gate_bias, L1_ffn_log_rel)
    x = x + _L1_attn_ref(_layernorm(x, axis=-1), L1_attn_Wq, L1_attn_Wk, L1_attn_Wv, L1_attn_Wo)
    x = x + 0.5 * _L1_ffn_ref(_layernorm(x, axis=-1), L1_ffn_Wq, L1_ffn_Wr, L1_ffn_aux_keys, L1_ffn_aux_values, L1_ffn_Wvd, L1_ffn_Wvu, L1_ffn_Wu1, L1_ffn_bu1, L1_ffn_Wu2, L1_ffn_bu2, L1_ffn_gate_w1, L1_ffn_gate_bias, L1_ffn_log_rel)
    return x

_drawn_inputs = setup_inputs


def setup_inputs(seed=0):
    import zlib

    import numpy as np

    out = dict(_drawn_inputs(seed))
    spreads = {'L0_attn_norm_w': (1.0, 0.2),
     'L0_attn_conv_b': (0.0, 0.1),
     'L0_attn_Dp': (1.0, 0.2),
     'L0_attn_gnorm_w': (1.0, 0.2),
     'L1_ffn_bu1': (0.0, 0.8),
     'L1_ffn_log_rel': (0.0, 0.8)}
    factors = {'L0_attn_dt_bias': 8.0,
     'L0_attn_A_log': 7.989,
     'L1_attn_Wq': 8.0,
     'L1_attn_Wk': 8.0,
     'L1_attn_Wv': 7.463,
     'L1_attn_Wo': 7.551,
     'L1_ffn_Wq': 8.0,
     'L1_ffn_Wr': 8.0,
     'L1_ffn_aux_keys': 8.0,
     'L1_ffn_aux_values': 8.0,
     'L1_ffn_Wvd': 8.0,
     'L1_ffn_Wvu': 8.0,
     'L1_ffn_Wu1': 8.0,
     'L1_ffn_Wu2': 8.0}
    for name, (base, spread) in spreads.items():
        noise = np.random.default_rng([zlib.crc32(name.encode()), seed]).standard_normal(out[name].shape)
        drawn = base * np.exp(spread * noise) if base else spread * noise
        out[name] = jnp.asarray(drawn.astype(out[name].dtype))
    for name, factor in factors.items():
        out[name] = (out[name] * factor).astype(out[name].dtype)
    return out
```

```python
import math
from contextlib import ExitStack

import numpy as np

import concourse.bass as bass
from concourse import mybir
from concourse.alu_op_type import AluOpType as ALU

F32 = mybir.dt.float32
I32 = mybir.dt.int32
ACT = mybir.ActivationFunctionType
AX = mybir.AxisListType

P = 128
SEQS, SEQ, D = 2, 512, 512
TOK = SEQS * SEQ
NT = TOK // P
DT = D // P
EPS = 1e-5
HID = 1376
FT = -(-HID // P)
HEADS, HD, GROUPS, STATE, TAPS, CHUNK = 128, 64, 8, 128, 4, 128
INNER = HEADS * HD
HPG = HEADS // GROUPS
GW = HPG * HD
GT = GW // P
NCH = SEQ // CHUNK
NH, NKV, AHD = 32, 8, 16
BOT, RDIM, NSLOT, VB, UH = 64, 48, 128, 32, 128


class Chip:

    def __init__(self, nc, ctx, prefix):
        self.nc, self.ctx, self.prefix, self.sems = nc, ctx, prefix, []
        ctx.callback(self.leave)

    def leave(self):
        self.nc.clear_and_free_semaphores(self.sems)
        self.nc.all_engine_barrier()

    def sb(self, name, shape, dtype=F32):
        return self.ctx.enter_context(self.nc.sbuf_tensor(self.prefix + name, shape, dtype))

    def sem(self, name):
        self.sems.append(self.nc.alloc_semaphore(name=self.prefix + name))
        return self.sems[-1]


class Chain:

    def __init__(self, eng, sem, base=0):
        self.eng, self.sem, self.base, self.n = eng, sem, base, 0

    def step(self, ins):
        ins.then_inc(self.sem, 1)
        self.n += 1

    def wait(self):
        self.eng.wait_ge(self.sem, self.base + self.n)

    def link(self, ins):
        self.step(ins)
        self.wait()


def norm_transpose(nc, g, name, dst, xn, rms_w=None, var_out=None):
    x, ps, ident, nhalf = g["x"], g["ps"], g["ident"], g["nhalf"]
    with ExitStack() as ctx:
        c = Chip(nc, ctx, name)
        st = c.sb("st", [P, NT, 6])
        mv = c.sb("mv", [P, NT, 2])
        ve = c.sb("ve", [P, NT])
        rstd = c.sb("rstd", [P, NT])
        ss = c.sb("ss", [P, NT])
        sq = c.sb("sq", [P, 2, D])
        r2 = c.sb("r2", [P, NT])
        xr = c.sb("xr", [P, NT, D]) if rms_w is not None else xn
        var_ready, rstd_ready, xn_ready, ss_ready, r2_ready, xr_ready, t_done, t_used, dve, own, v2 = (
            c.sem(s) for s in ("var_ready", "rstd_ready", "xn_ready", "ss_ready", "r2_ready", "xr_ready",
                               "t_done", "t_used", "dve", "own", "v2"))
        with nc.Block() as block:
            @block.vector
            def _(e):
                ch = Chain(e, dve)
                for t in range(NT):
                    ch.step(e.bn_stats(st[:, t, :], x[:, t, :]))
                ch.wait()
                for t in range(NT):
                    ch.step(e.bn_aggr(mv[:, t, :], st[:, t, :]))
                ch.wait()
                e.tensor_scalar(ve[:], mv[:, :, 1], EPS, None, ALU.add).then_inc(var_ready, 1)
                e.wait_ge(rstd_ready, 1)
                for t in range(NT):
                    e.tensor_scalar(xn[:, t, :], x[:, t, :], mv[:, t, 0:1], rstd[:, t:t + 1],
                                    ALU.subtract, ALU.mult).then_inc(xn_ready, 1)
                if var_out is not None:
                    e.wait_ge(xn_ready, NT)
                    for t in range(NT):
                        ch.step(e.bn_stats(st[:, t, :], xn[:, t, :]))
                    ch.wait()
                    for t in range(NT):
                        ch.step(e.bn_aggr(mv[:, t, :], st[:, t, :]))
                    ch.wait()
                    ch.link(e.tensor_copy(var_out[:], mv[:, :, 1]))
                if rms_w is not None:
                    e.wait_ge(xn_ready, NT)
                    for t in range(NT):
                        ch.step(e.tensor_tensor(x[:, t, :], x[:, t, :], xn[:, t, :], ALU.add))
                    e.wait_ge(ss_ready, NT)
                    e.tensor_scalar(ve[:], ss[:], 1.0 / D, EPS, ALU.mult, ALU.add).then_inc(v2, 1)
                    e.wait_ge(r2_ready, 1)
                    for t in range(NT):
                        e.tensor_scalar(xr[:, t, :], xn[:, t, :], r2[:, t:t + 1], None,
                                        ALU.mult).then_inc(xr_ready, 1)
                    for t in range(NT):
                        e.wait_ge(t_done, t + 1)
                        w = rms_w[:, :].unsqueeze(2).to_broadcast([P, DT, P])
                        e.tensor_tensor(dst[:, :, t * P:(t + 1) * P],
                                        ps[t % 2][:, :].rearrange("p (a n) -> p a n", a=DT), w,
                                        ALU.mult).then_inc(t_used, 1)

            @block.gpsimd
            def _(e):
                e.wait_ge(var_ready, 1)
                e.tensor_tensor(rstd[:], ve[:], nhalf[:, 0:NT], ALU.pow).then_inc(rstd_ready, 1)
                if rms_w is not None:
                    e.wait_ge(v2, 1)
                    e.tensor_tensor(r2[:], ve[:], nhalf[:, 0:NT], ALU.pow).then_inc(r2_ready, 1)

            @block.scalar
            def _(e):
                if rms_w is not None:
                    for t in range(NT):
                        e.wait_ge(xn_ready, t + 1)
                        if t >= 2:
                            e.wait_ge(ss_ready, t - 1)
                        e.activation(sq[:, t % 2, :], xn[:, t, :], ACT.Square,
                                     accum_out=ss[:, t:t + 1]).then_inc(ss_ready, 1)
                else:
                    for t in range(NT):
                        e.wait_ge(t_done, t + 1)
                        e.copy(dst[:, :, t * P:(t + 1) * P],
                               ps[t % 2][:, :].rearrange("p (a n) -> p a n", a=DT)).then_inc(t_used, 1)

            @block.tensor
            def _(e):
                for t in range(NT):
                    e.wait_ge(xr_ready if rms_w is not None else xn_ready, t + 1)
                    if t >= 2:
                        e.wait_ge(t_used, t - 1)
                    for a in range(DT):
                        last = e.transpose(ps[t % 2][:, a * P:(a + 1) * P], xr[:, t, a * P:(a + 1) * P],
                                           ident[:])
                    last.then_inc(t_done, 1)


def q4_ffn(nc, g, name):
    x, ps, d = g["x"], g["ps"], g["dram"]
    with ExitStack() as ctx:
        c = Chip(nc, ctx, name)
        hT = c.sb("hT", [P, DT, TOK])
        with ExitStack() as pre:
            xn = pre.enter_context(nc.sbuf_tensor(name + "xn", [P, NT, D], F32))
            norm_transpose(nc, g, name + "n_", hT, xn)
        WC = DT * HID
        W1 = c.sb("W1", [P, DT, HID])
        W3 = c.sb("W3", [P, DT, HID])
        W2 = c.sb("W2", [P, FT, D])
        raw = c.sb("raw", [P, FT * D], I32)
        scl = c.sb("scl", [P, FT * D])
        shifts = c.sb("shifts", [P, 5, 2], I32)
        hh = c.sb("hh", [P, FT, SEQ])
        sil = c.sb("sil", [P, 2, SEQ])
        sh_in, raw_in, scl_in, shifted, weights, a_done, b_done, silued, hh_ready, o_done, o_used = (
            c.sem(s) for s in ("sh_in", "raw_in", "scl_in", "shifted", "weights", "a_done", "b_done",
                               "silued", "hh_ready", "o_done", "o_used"))
        FTAIL = HID - (FT - 1) * P

        def rows(f):
            return P if f < FT - 1 else FTAIL

        with nc.Block() as block:
            @block.sync
            def _(e):
                e.dma_start(shifts[:], d["shifts"]).then_inc(sh_in, 16)
                for m, w in enumerate(("w1", "w3")):
                    if m:
                        e.wait_ge(shifted, 1)
                        e.wait_ge(weights, 1)
                    for half in range(2):
                        e.dma_start(raw[64 * half:64 * half + 64, 0:WC],
                                    d[w].rearrange("p a n -> p (a n)")).then_inc(raw_in, 16)
                        e.dma_start(scl[64 * half:64 * half + 64, 0:WC],
                                    d["s" + w[1]][half].rearrange("a n -> (a n)").partition_broadcast(64)
                                    ).then_inc(scl_in, 16)
                e.wait_ge(weights, 2)
                r3 = raw[:, :].rearrange("p (f n) -> p f n", f=FT)
                s3 = scl[:, :].rearrange("p (f n) -> p f n", f=FT)
                full = (FT - 1) * P
                e.dma_start(r3[:, 0:FT - 1, :], d["w2"][0:full, :].rearrange("(f p) n -> p f n", p=P)
                            ).then_inc(raw_in, 16)
                e.dma_start(r3[0:FTAIL, FT - 1, :], d["w2"][full:HID, :]).then_inc(raw_in, 16)
                nb = HID // 32
                for q in range(4):
                    n = len(range(q, nb, 4))
                    src = d["s2"].rearrange("b n -> (b n)")
                    ap = bass.AP(tensor=src.tensor, offset=q * D, ap=[[0, 32], [4 * D, n], [1, D]])
                    e.dma_start(s3[32 * q:32 * q + 32, 0:n, :], ap).then_inc(scl_in, 16)

            @block.vector
            def _(e):
                e.wait_ge(sh_in, 16)
                for m in range(2):
                    e.wait_ge(raw_in, 32 * (m + 1))
                    e.tensor_scalar(raw[:, 0:WC], raw[:, 0:WC], shifts[:, 0, 0:1], shifts[:, 0, 1:2],
                                    ALU.logical_shift_left, ALU.arith_shift_right).then_inc(shifted, 1)
                    e.wait_ge(shifted, m + 1)
                    e.wait_ge(scl_in, 32 * (m + 1))
                    e.tensor_tensor((W1, W3)[m][:, :, :].rearrange("p a n -> p (a n)"), raw[:, 0:WC],
                                    scl[:, 0:WC], ALU.mult).then_inc(weights, 1)
                e.wait_ge(raw_in, 96)
                for k in range(4):
                    for f0, f1, r in ((0, FT - 1, P), (FT - 1, FT, FTAIL)):
                        v = raw[0:r, :].rearrange("p (f n k) -> p f n k", f=FT, k=4)[:, f0:f1, :, k]
                        e.tensor_scalar(v, v, shifts[0:r, k + 1, 0:1], shifts[0:r, k + 1, 1:2],
                                        ALU.logical_shift_left, ALU.arith_shift_right).then_inc(shifted, 1)
                e.wait_ge(shifted, 10)
                e.wait_ge(scl_in, 128)
                w2f = W2[:, :, :].rearrange("p f n -> p (f n)")
                n = (FT - 1) * D
                e.tensor_tensor(w2f[:, 0:n], raw[:, 0:n], scl[:, 0:n], ALU.mult).then_inc(weights, 1)
                e.tensor_tensor(w2f[0:FTAIL, n:], raw[0:FTAIL, n:], scl[0:FTAIL, n:],
                                ALU.mult).then_inc(weights, 1)
                for h in range(SEQS):
                    for f in range(FT):
                        n, r = h * FT + f, rows(f)
                        e.wait_ge(silued, n + 1)
                        e.wait_ge(b_done, n + 1)
                        if h:
                            e.wait_ge(o_done, 4)
                        e.tensor_tensor(hh[0:r, f, :], ps[2 + n % 2][0:r, :], sil[0:r, n % 2, :],
                                        ALU.mult).then_inc(hh_ready, 1)
                    for t in range(4):
                        n = 4 * h + t
                        e.wait_ge(o_done, n + 1)
                        e.scalar_tensor_tensor(x[:, n, :], ps[4 + n % 2][:, :], 0.5, x[:, n, :],
                                               ALU.mult, ALU.add).then_inc(o_used, 1)

            @block.scalar
            def _(e):
                for n in range(SEQS * FT):
                    r = rows(n % FT)
                    e.wait_ge(a_done, n + 1)
                    if n >= 2:
                        e.wait_ge(hh_ready, n - 1)
                    e.activation(sil[0:r, n % 2, :], ps[n % 2][0:r, :], ACT.Silu).then_inc(silued, 1)

            @block.tensor
            def _(e):
                for h in range(SEQS):
                    for f in range(FT):
                        n, r = h * FT + f, rows(f)
                        if n == 0:
                            e.wait_ge(weights, 1)
                        if n >= 2:
                            e.wait_ge(silued, n - 1)
                        for a in range(DT):
                            last = e.matmul(ps[n % 2][0:r, :], W1[:, a, f * P:f * P + r],
                                            hT[:, a, h * SEQ:(h + 1) * SEQ], start=a == 0, stop=a == DT - 1)
                        last.then_inc(a_done, 1)
                        if n == 0:
                            e.wait_ge(weights, 2)
                        if n >= 2:
                            e.wait_ge(hh_ready, n - 1)
                        for a in range(DT):
                            last = e.matmul(ps[2 + n % 2][0:r, :], W3[:, a, f * P:f * P + r],
                                            hT[:, a, h * SEQ:(h + 1) * SEQ], start=a == 0, stop=a == DT - 1)
                        last.then_inc(b_done, 1)
                    e.wait_ge(weights, 4)
                    e.wait_ge(hh_ready, FT * (h + 1))
                    for t in range(4):
                        n = 4 * h + t
                        if n >= 2:
                            e.wait_ge(o_used, n - 1)
                        for f in range(FT):
                            r = rows(f)
                            last = e.matmul(ps[4 + n % 2][:, :], hh[0:r, f, t * P:(t + 1) * P], W2[0:r, f, :],
                                            start=f == 0, stop=f == FT - 1)
                        last.then_inc(o_done, 1)


def routed_ffn(nc, g, name):
    x, ps, d, ident, ones, nhalf = g["x"], g["ps"], g["dram"], g["ident"], g["ones"], g["nhalf"]
    with ExitStack() as ctx:
        c = Chip(nc, ctx, name)
        hT = c.sb("hT", [P, DT, TOK])
        xn = c.sb("xn", [P, NT, D])
        var = c.sb("var", [P, NT])
        norm_transpose(nc, g, name + "n_", hT, xn, var_out=var)
        WqT = c.sb("WqT", [P, DT, BOT])
        Wu1T = c.sb("Wu1T", [P, DT, UH])
        WvdT = c.sb("WvdT", [P, DT, VB])
        avT = c.sb("avT", [P, DT, NSLOT])
        WrT = c.sb("WrT", [BOT, RDIM])
        akT = c.sb("akT", [BOT, NSLOT])
        WvuT = c.sb("WvuT", [VB, D])
        lrel = c.sb("lrel", [P, NSLOT])
        sc = c.sb("sc", [P, 4])
        sc2 = c.sb("sc2", [P, 3])
        qT = c.sb("qT", [BOT, TOK])
        rqT = c.sb("rqT", [RDIM, TOK])
        rkT = c.sb("rkT", [RDIM, NSLOT])
        vd = c.sb("vd", [NSLOT, VB])
        u = c.sb("u", [UH, TOK])
        u2 = c.sb("u2", [UH, TOK])
        u3 = c.sb("u3", [UH, TOK])
        rs = c.sb("rs", [P, NT, NSLOT])
        at = c.sb("at", [P, NT, NSLOT])
        rep = c.sb("rep", [P, NT, NSLOT])
        top = c.sb("top", [P, NT, 8])
        mx = c.sb("mx", [P, NT])
        den = c.sb("den", [P, NT])
        wT = c.sb("wT", [NSLOT, TOK])
        lowT = c.sb("lowT", [VB, TOK])
        lv = c.sb("lv", [P, NT])
        lvs = c.sb("lvs", [P, 1])
        s1 = c.sb("s1", [P, NT])
        s2 = c.sb("s2", [P, NT])
        gate = c.sb("gate", [P, NT])
        msk = c.sb("msk", [P, NT])
        w_in, q_mm, q_sb, rk_mm, rk_sb, rq_mm, rq_sb, vd_mm, vd_sb, u_mm, u_sb, gelu, lr_mm, sc_mm, picked, neg, \
            exped, norm, t_mm, t_sb, low_mm, low_sb, o_mm, o_used, dve, lvr, lv_mm, act, tanhed, ez, fin = (
                c.sem(s) for s in ("w_in", "q_mm", "q_sb", "rk_mm", "rk_sb", "rq_mm", "rq_sb", "vd_mm", "vd_sb",
                                   "u_mm", "u_sb", "gelu", "lr_mm", "sc_mm", "picked", "neg", "exped", "norm",
                                   "t_mm", "t_sb", "low_mm", "low_sb", "o_mm", "o_used", "dve", "lvr", "lv_mm",
                                   "act", "tanhed", "ez", "fin"))
        loads = [(WqT, "rWqT"), (Wu1T, "Wu1T"), (WvdT, "WvdT"), (avT, "avT")]
        small = [(WrT, "WrT"), (akT, "akT"), (WvuT, "WvuT")]
        NL = 16 * (len(loads) + len(small) + 3 + 3)
        BIG = 1e30
        C0 = math.sqrt(2.0 / math.pi)

        with nc.Block() as block:
            @block.sync
            def _(e):
                for dst, src in loads:
                    e.dma_start(dst[:], d[src].rearrange("(a p) n -> p a n", p=P)).then_inc(w_in, 16)
                for dst, src in small:
                    e.dma_start(dst[:], d[src]).then_inc(w_in, 16)
                e.dma_start(lrel[:], d["lrel"].partition_broadcast(P)).then_inc(w_in, 16)
                e.dma_start(sc[:, 0:1], d["bu1"]).then_inc(w_in, 16)
                e.dma_start(sc[:, 1:2], d["Wu2"]).then_inc(w_in, 16)
                for n, s in enumerate(("bu2", "gate_w1", "gate_bias")):
                    e.dma_start(sc2[:, n:n + 1], d[s].partition_broadcast(P)).then_inc(w_in, 16)

            @block.tensor
            def _(e):
                e.wait_ge(w_in, NL)
                for h in range(2):
                    for a in range(DT):
                        last = e.matmul(ps[h][0:BOT, :], WqT[:, a, :], hT[:, a, h * 512:h * 512 + 512],
                                        start=a == 0, stop=a == DT - 1)
                    last.then_inc(q_mm, 1)
                e.matmul(ps[2][0:RDIM, 0:NSLOT], WrT[:], akT[:], start=True, stop=True).then_inc(rk_mm, 1)
                for a in range(DT):
                    last = e.matmul(ps[3][:, 0:VB], avT[:, a, :], WvdT[:, a, :], start=a == 0, stop=a == DT - 1)
                last.then_inc(vd_mm, 1)
                for h in range(2):
                    for a in range(DT):
                        last = e.matmul(ps[4 + h][:, :], Wu1T[:, a, :], hT[:, a, h * 512:h * 512 + 512],
                                        start=a == 0, stop=a == DT - 1)
                    last.then_inc(u_mm, 1)
                for h in range(2):
                    e.wait_ge(q_sb, h + 1)
                    e.matmul(ps[6 + h][0:RDIM, :], WrT[:], qT[:, h * 512:h * 512 + 512],
                             start=True, stop=True).then_inc(rq_mm, 1)
                e.wait_ge(rk_sb, 1)
                for t in range(NT):
                    e.wait_ge(rq_sb, t // 4 + 1)
                    if t < 2:
                        e.wait_ge(vd_sb, 1)
                        e.wait_ge(q_sb, 2)
                    else:
                        e.wait_ge(dve, 2 * (t - 1))
                    e.matmul(ps[t % 2][:, 0:NSLOT], rqT[:, t * P:(t + 1) * P], rkT[:], start=True, stop=True)
                    e.matmul(ps[2 + t % 2][:, 0:NSLOT], qT[:, t * P:(t + 1) * P], akT[:],
                             start=True, stop=True).then_inc(sc_mm, 1)
                e.wait_ge(lvr, 1)
                e.wait_ge(u_sb, 2)
                e.matmul(ps[4][:, 0:1], ones[:], lvs[:], start=True, stop=True).then_inc(lv_mm, 1)
                e.wait_ge(gelu, 1)
                for t in range(NT):
                    last = e.matmul(ps[5][:, t:t + 1], u[:, t * P:(t + 1) * P], sc[:, 1:2], start=True, stop=True)
                last.then_inc(lr_mm, 1)
                e.wait_ge(norm, NT)
                e.wait_ge(rq_sb, 2)
                for h in range(2):
                    for t in range(4):
                        n = 4 * h + t
                        last = e.transpose(ps[6 + h][:, t * P:(t + 1) * P], at[:, n, :], ident[:])
                    last.then_inc(t_mm, 1)
                e.wait_ge(dve, 2 * NT)
                for h in range(2):
                    e.wait_ge(t_sb, h + 1)
                    e.matmul(ps[h][0:VB, :], vd[:], wT[:, h * 512:h * 512 + 512],
                             start=True, stop=True).then_inc(low_mm, 1)
                for t in range(NT):
                    e.wait_ge(low_sb, t // 4 + 1)
                    if t >= 2:
                        e.wait_ge(o_used, t - 1)
                    e.matmul(ps[2 + t % 2][:, :], lowT[:, t * P:(t + 1) * P], WvuT[:],
                             start=True, stop=True).then_inc(o_mm, 1)

            @block.scalar
            def _(e):
                for h in range(2):
                    e.wait_ge(q_mm, h + 1)
                    e.copy(qT[:, h * 512:h * 512 + 512], ps[h][0:BOT, :]).then_inc(q_sb, 1)
                e.wait_ge(rk_mm, 1)
                e.copy(rkT[:], ps[2][0:RDIM, 0:NSLOT]).then_inc(rk_sb, 1)
                e.wait_ge(vd_mm, 1)
                e.copy(vd[:], ps[3][:, 0:VB]).then_inc(vd_sb, 1)
                for h in range(2):
                    e.wait_ge(u_mm, h + 1)
                    e.activation(u[:, h * 512:h * 512 + 512], ps[4 + h][:, :], ACT.Identity,
                                 bias=sc[:, 0:1]).then_inc(u_sb, 1)
                for h in range(2):
                    e.wait_ge(rq_mm, h + 1)
                    e.copy(rqT[:, h * 512:h * 512 + 512], ps[6 + h][0:RDIM, :]).then_inc(rq_sb, 1)
                e.activation(lv[:], var[:], ACT.Ln, bias=1.0, accum_out=lvs[:]).then_inc(lvr, 1)
                e.wait_ge(act, 1)
                e.activation(u3[:], u3[:], ACT.Tanh, scale=C0).then_inc(tanhed, 1)
                for t in range(NT):
                    e.wait_ge(neg, t + 1)
                    e.activation(at[:, t, :], at[:, t, :], ACT.Exp, bias=mx[:, t:t + 1],
                                 accum_out=den[:, t:t + 1]).then_inc(exped, 1)
                e.wait_ge(act, 2)
                e.activation(s1[:], s1[:], ACT.Exp, scale=-1.0).then_inc(ez, 1)
                e.wait_ge(act, 3)
                e.activation(gate[:], gate[:], ACT.Exp, scale=-1.0).then_inc(ez, 1)
                for h in range(2):
                    e.wait_ge(t_mm, h + 1)
                    e.copy(wT[:, h * 512:h * 512 + 512], ps[6 + h][:, :]).then_inc(t_sb, 1)
                for h in range(2):
                    e.wait_ge(low_mm, h + 1)
                    e.copy(lowT[:, h * 512:h * 512 + 512], ps[h][0:VB, :]).then_inc(low_sb, 1)

            @block.vector
            def _(e):
                ch = Chain(e, fin)
                e.wait_ge(u_sb, 2)
                ch.link(e.tensor_tensor(u2[:], u[:], u[:], ALU.mult))
                ch.link(e.tensor_scalar(u2[:], u2[:], 0.044715, 1.0, ALU.mult, ALU.add))
                e.tensor_tensor(u3[:], u2[:], u[:], ALU.mult).then_inc(act, 1)
                for t in range(NT):
                    e.wait_ge(sc_mm, t + 1)
                    e.scalar_tensor_tensor(rs[:, t, :], ps[t % 2][:, 0:NSLOT], RDIM ** -0.5, lrel[:],
                                           ALU.mult, ALU.add).then_inc(dve, 1)
                    e.scalar_tensor_tensor(at[:, t, :], ps[2 + t % 2][:, 0:NSLOT], BOT ** -0.5, lrel[:],
                                           ALU.mult, ALU.add).then_inc(dve, 1)
                e.wait_ge(dve, 2 * NT)
                for t in range(NT):
                    ch.step(e.max(out=top[:, t, :], in_=rs[:, t, :]))
                ch.wait()
                for t in range(NT):
                    ch.step(e.match_replace(out=rep[:, t, :], in_to_replace=top[:, t, :], in_values=rs[:, t, :],
                                            imm_value=-3.0e38))
                ch.wait()
                for t in range(NT):
                    ch.step(e.tensor_tensor(rs[:, t, :], rs[:, t, :], rep[:, t, :], ALU.not_equal))
                ch.wait()
                for t in range(NT):
                    ch.step(e.tensor_scalar(rep[:, t, :], rs[:, t, :], -1.0, BIG, ALU.add, ALU.mult))
                    ch.step(e.tensor_tensor(at[:, t, :], at[:, t, :], rs[:, t, :], ALU.mult))
                ch.wait()
                for t in range(NT):
                    ch.step(e.tensor_tensor(at[:, t, :], at[:, t, :], rep[:, t, :], ALU.add))
                ch.wait()
                for t in range(NT):
                    ch.link(e.tensor_reduce(mx[:, t:t + 1], at[:, t, :], AX.X, ALU.max))
                    e.tensor_scalar(mx[:, t:t + 1], mx[:, t:t + 1], -1.0, None, ALU.mult).then_inc(neg, 1)
                e.wait_ge(tanhed, 1)
                ch.step(e.tensor_scalar(u3[:], u3[:], 1.0, 0.5, ALU.add, ALU.mult))
                ch.wait()
                e.tensor_tensor(u[:], u[:], u3[:], ALU.mult).then_inc(gelu, 1)
                e.wait_ge(exped, NT)
                ch.link(e.reciprocal(den[:], den[:]))
                for t in range(NT):
                    e.tensor_scalar(at[:, t, :], at[:, t, :], den[:, t:t + 1], None, ALU.mult).then_inc(norm, 1)
                e.wait_ge(lv_mm, 1)
                ch.link(e.tensor_scalar(lvs[:], ps[4][:, 0:1], 1.0 / TOK, 1e-6, ALU.mult, ALU.add))
                ch.link(e.reciprocal(lvs[:], lvs[:]))
                ch.step(e.tensor_scalar(s2[:], lv[:], lvs[:], 0.5, ALU.mult, ALU.mult))
                e.wait_ge(lr_mm, 1)
                e.tensor_scalar(s1[:], ps[5][:, 0:NT], sc2[:, 0:1], None, ALU.add).then_inc(act, 1)
                e.wait_ge(ez, 1)
                ch.link(e.tensor_scalar(s1[:], s1[:], 1.0, None, ALU.add))
                ch.link(e.reciprocal(s1[:], s1[:]))
                ch.link(e.scalar_tensor_tensor(s1[:], s1[:], 2.5, s2[:], ALU.mult, ALU.add))
                ch.link(e.tensor_scalar(s1[:], s1[:], 0.0, 5.0, ALU.max, ALU.min))
                ch.link(e.tensor_scalar(s1[:], s1[:], -0.5, 1.0 / 1.5, ALU.add, ALU.mult))
                ch.link(e.tensor_scalar(s1[:], s1[:], 0.0, 1.0, ALU.max, ALU.min))
                e.tensor_scalar(gate[:], s1[:], sc2[:, 1:2], sc2[:, 2:3], ALU.mult, ALU.add).then_inc(act, 1)
                e.wait_ge(ez, 2)
                ch.link(e.tensor_scalar(gate[:], gate[:], 1.0, None, ALU.add))
                ch.link(e.reciprocal(gate[:], gate[:]))
                ch.link(e.tensor_scalar(msk[:], gate[:], 0.05, 0.5, ALU.is_ge, ALU.mult))
                ch.link(e.tensor_tensor(gate[:], gate[:], msk[:], ALU.mult))
                for t in range(NT):
                    ch.step(e.scalar_tensor_tensor(x[:, t, :], xn[:, t, :], 0.5, x[:, t, :], ALU.mult, ALU.add))
                ch.wait()
                for t in range(NT):
                    e.wait_ge(o_mm, t + 1)
                    e.scalar_tensor_tensor(x[:, t, :], ps[2 + t % 2][:, :], gate[:, t:t + 1], x[:, t, :],
                                           ALU.mult, ALU.add).then_inc(o_used, 1)


def attention(nc, g, name):
    x, ps, psum, d, ident = g["x"], g["ps"], g["psum"], g["dram"], g["ident"]
    QT = SEQ // P
    PAIRS = NH // 2
    M = QT * PAIRS
    NP = 2 * DT
    SCALE = AHD ** -0.5
    with ExitStack() as ctx:
        c = Chip(nc, ctx, name)
        hT = c.sb("hT", [P, DT, TOK])
        with ExitStack() as pre:
            xn = pre.enter_context(nc.sbuf_tensor(name + "xn", [P, NT, D], F32))
            norm_transpose(nc, g, name + "n_", hT, xn)
        wq, wk, wo = (c.sb(n, [P, DT, D]) for n in ("wq", "wk", "wo"))
        wv = c.sb("wv", [P, DT, NKV * AHD])
        cos, sin, rot = c.sb("cos", [P, SEQ]), c.sb("sin", [P, SEQ]), c.sb("rot", [P, P])
        par, cmask = c.sb("par", [P, 2]), c.sb("cmask", [P, P])
        hb = c.sb("hb", [P, DT, SEQ])
        raw = c.sb("raw", [P, 2, SEQ])
        t0, t1 = c.sb("t0", [P, SEQ]), c.sb("t1", [P, SEQ])
        q = c.sb("q", [P, DT, SEQ])
        kk = c.sb("kk", [P, 2, DT, SEQ])
        v = c.sb("v", [P, QT, NKV * AHD])
        pr = c.sb("pr", [P, 2, 2, SEQ])
        pt = c.sb("pt", [P, 2, 2, SEQ])
        mx = c.sb("mx", [P, 2, 2])
        nm = c.sb("nm", [P, 2, 2])
        den = c.sb("den", [P, 2, NH])
        rden = c.sb("rden", [P, NH])
        on = c.sb("on", [P, D])
        oT = c.sb("oT", [P, DT, P])
        w_in, hb_ready, proj, raw_ready, rotated, roped, scores, negmax, exped, turned, pt_act, pt_dve, pv, \
            normed, o_turned, oT_ready, out_mm, x_done, dve = (
                c.sem(s) for s in ("w_in", "hb_ready", "proj", "raw_ready", "rotated", "roped", "scores",
                                   "negmax", "exped", "turned", "pt_act", "pt_dve", "pv", "normed", "o_turned",
                                   "oT_ready", "out_mm", "x_done", "dve"))
        NV = NP + QT
        CR = 2

        with nc.Block() as block:
            @block.sync
            def _(e):
                for dst, src in ((wq, "wq"), (wk, "wk"), (wv, "wv"), (wo, "wo")):
                    e.dma_start(dst[:], d[src].rearrange("(a p) n -> p a n", p=P)).then_inc(w_in, 16)
                for dst, src in ((cos, "cos"), (sin, "sin"), (rot, "rot"), (par, "parity"), (cmask, "causal_add")):
                    e.dma_start(dst[:], d[src]).then_inc(w_in, 16)

            @block.gpsimd
            def _(e):
                with e.Fori(0, SEQS) as b:
                    e.wait_ge(raw_ready, b * NV + CR)
                    e.tensor_copy(hb[:], hT[:, :, bass.ds(b * SEQ, SEQ)]).then_inc(hb_ready, 1)

            @block.tensor
            def _(e):
                e.sem_inc(pv, CR)
                e.sem_inc(turned, CR)
                e.sem_inc(o_turned, 1)
                e.sem_inc(out_mm, 1)
                e.wait_ge(w_in, 9 * 16)
                with e.Fori(0, SEQS) as b:
                    e.wait_ge(hb_ready, b + 1)

                    def project(n):
                        e.wait_ge(raw_ready, b * NV + n - 1 + CR)
                        bank = 4 + n % 2
                        if n < NP:
                            w = wq if n < DT else wk
                            for a in range(DT):
                                last = e.matmul(ps[bank], w[:, a, (n % DT) * P:(n % DT + 1) * P], hb[:, a, :],
                                                start=a == 0, stop=a == DT - 1)
                        else:
                            t = n - NP
                            for a in range(DT):
                                last = e.matmul(psum[:, bank, 0:NKV * AHD], hb[:, a, t * P:(t + 1) * P],
                                                wv[:, a, :], start=a == 0, stop=a == DT - 1)
                        last.then_inc(proj, 1)

                    def rotate(n):
                        e.wait_ge(raw_ready, b * NV + n + 1 + CR)
                        e.wait_ge(roped, b * NP + n - 1 + CR)
                        e.matmul(ps[6 + n % 2], rot[:], raw[:, n % 2, :], start=True, stop=True).then_inc(rotated, 1)

                    e.wait_ge(x_done, b * QT + 1)
                    project(0)
                    for n in range(1, NV):
                        project(n)
                        if n - 1 < NP:
                            rotate(n - 1)
                    e.wait_ge(roped, b * NP + NP + CR)
                    e.wait_ge(raw_ready, b * NV + NV + CR)

                    def score(m):
                        qt, u = divmod(m, PAIRS)
                        e.wait_ge(exped, b * M + m - 1 + CR)
                        T, r = divmod(u, 4)
                        n = P * (qt + 1)
                        for h in range(2):
                            last = e.matmul(psum[:, 2 * (m % 2) + h, 0:n],
                                            q[32 * r:32 * r + 32, T, qt * P:(qt + 1) * P],
                                            kk[32 * r:32 * r + 32, h, T, 0:n], start=True, stop=True)
                        last.then_inc(scores, 1)

                    def turn(m):
                        qt, u = divmod(m, PAIRS)
                        e.wait_ge(exped, b * M + m + 1 + CR)
                        e.wait_ge(pt_act, b * M + m + CR)
                        e.wait_ge(pt_dve, b * M + m + CR)
                        for h in range(2):
                            for t in range(qt + 1):
                                last = e.transpose(psum[:, 4 + h, t * P:(t + 1) * P],
                                                   pr[:, m % 2, h, t * P:(t + 1) * P], ident[:])
                        last.then_inc(turned, 1)

                    def weigh(m):
                        qt, u = divmod(m, PAIRS)
                        e.wait_ge(pt_act, b * M + m + 1 + CR)
                        e.wait_ge(pt_dve, b * M + m + 1 + CR)
                        if u == 0:
                            e.wait_ge(normed, b * QT + qt + CR)
                        for h in range(2):
                            kv = (2 * u + h) // (NH // NKV)
                            col = (2 * u + h) * AHD
                            for t in range(qt + 1):
                                last = e.matmul(psum[:, 6, col:col + AHD], pt[:, m % 2, h, t * P:(t + 1) * P],
                                                v[:, t, kv * AHD:(kv + 1) * AHD], start=t == 0, stop=t == qt)
                        last.then_inc(pv, 1)

                    def o_turn(qt):
                        e.wait_ge(normed, b * QT + qt + 1 + CR)
                        e.wait_ge(x_done, b * QT + qt + 1)
                        for a in range(DT):
                            last = e.transpose(psum[:, 7, a * P:(a + 1) * P], on[:, a * P:(a + 1) * P], ident[:])
                        last.then_inc(o_turned, 1)

                    def o_mul(qt):
                        e.wait_ge(oT_ready, b * QT + qt + 1 + CR)
                        for a in range(DT):
                            last = e.matmul(ps[7], oT[:, a, :], wo[:, a, :], start=a == 0, stop=a == DT - 1)
                        last.then_inc(out_mm, 1)

                    score(0)
                    score(1)
                    for m in range(M + 4):
                        if m < M:
                            turn(m)
                        if 1 <= m <= M:
                            weigh(m - 1)
                        if m + 2 < M:
                            score(m + 2)
                        if m % PAIRS == 1 and m > 1:
                            o_turn(m // PAIRS - 1)
                        if m % PAIRS == 3 and m > 3:
                            o_mul(m // PAIRS - 1)

            @block.scalar
            def _(e):
                e.sem_inc(raw_ready, CR)
                e.sem_inc(exped, CR)
                e.sem_inc(pt_act, CR)
                e.sem_inc(oT_ready, CR)
                with e.Fori(0, SEQS) as b:
                    for n in range(NV):
                        e.wait_ge(proj, b * NV + n + 1)
                        if n < NP:
                            e.wait_ge(roped, b * NP + n - 1 + CR)
                            e.copy(raw[:, n % 2, :], ps[4 + n % 2]).then_inc(raw_ready, 1)
                        else:
                            e.copy(v[:, n - NP, :], psum[:, 4 + n % 2, 0:NKV * AHD]).then_inc(raw_ready, 1)

                    def evacuate(m):
                        n = P * (m // PAIRS + 1)
                        e.wait_ge(turned, b * M + m + 1 + CR)
                        e.wait_ge(pv, b * M + m - 1 + CR)
                        e.copy(pt[:, m % 2, 0, 0:n], psum[:, 4, 0:n]).then_inc(pt_act, 1)

                    for m in range(M + 4):
                        if m < M:
                            n = P * (m // PAIRS + 1)
                            e.wait_ge(negmax, b * M + m + 1)
                            e.wait_ge(turned, b * M + m - 1 + CR)
                            if m % PAIRS == 0:
                                e.wait_ge(normed, b * QT + m // PAIRS - 1 + CR)
                            for h in range(2):
                                hd = 2 * (m % PAIRS) + h
                                last = e.activation(pr[:, m % 2, h, 0:n], psum[:, 2 * (m % 2) + h, 0:n], ACT.Exp,
                                                    bias=nm[:, m % 2, h:h + 1], scale=SCALE,
                                                    accum_out=den[:, (m // PAIRS) % 2, hd:hd + 1])
                            last.then_inc(exped, 1)
                        if 1 <= m <= M:
                            evacuate(m - 1)
                        if m % PAIRS == 2 and m > 2:
                            qt = m // PAIRS - 1
                            e.wait_ge(o_turned, b * QT + qt + 1 + 1)
                            e.wait_ge(out_mm, b * QT + qt + 1)
                            e.copy(oT[:], psum[:, 7, :].rearrange("p (a n) -> p a n", a=DT)).then_inc(oT_ready, 1)

            @block.vector
            def _(e):
                e.sem_inc(roped, CR)
                e.sem_inc(pt_dve, CR)
                e.sem_inc(normed, CR)
                e.sem_inc(x_done, 1)
                e.wait_ge(w_in, 9 * 16)
                NC = DT * 2 + DT * 4 + M * 2 + QT
                with e.Fori(0, SEQS) as b:
                    ch = Chain(e, dve, b * NC)
                    for n in range(NP):
                        T = n % DT
                        e.wait_ge(raw_ready, b * NV + n + 1 + CR)
                        ch.step(e.tensor_tensor(t0[:], raw[:, n % 2, :], cos[:], ALU.mult))
                        e.wait_ge(rotated, b * NP + n + 1)
                        ch.link(e.tensor_tensor(t1[:], ps[6 + n % 2], sin[:], ALU.mult))
                        if n < DT:
                            e.tensor_tensor(q[:, T, :], t0[:], t1[:], ALU.add).then_inc(roped, 1)
                            e.wait_ge(roped, b * NP + n + 1 + CR)
                        else:
                            ch.link(e.tensor_tensor(t0[:], t0[:], t1[:], ALU.add))
                            ch.step(e.tensor_scalar(kk[:, 0, T, :], t0[:], par[:, 0:1], None, ALU.mult))
                            e.tensor_scalar(kk[:, 1, T, :], t0[:], par[:, 1:2], None, ALU.mult).then_inc(roped, 1)
                            e.wait_ge(roped, b * NP + n + 1 + CR)

                    def peak(m):
                        n = P * (m // PAIRS + 1)
                        s = psum[:, 2 * (m % 2):2 * (m % 2) + 2, :]
                        e.wait_ge(scores, b * M + m + 1)
                        ch.link(e.tensor_tensor(s[:, :, n - P:n], s[:, :, n - P:n],
                                                cmask[:, :].unsqueeze(1).to_broadcast([P, 2, P]), ALU.add))
                        ch.link(e.tensor_reduce(mx[:, m % 2, :], s[:, :, 0:n], AX.X, ALU.max))
                        e.wait_ge(exped, b * M + m - 1 + CR)
                        e.tensor_scalar(nm[:, m % 2, :], mx[:, m % 2, :], -SCALE, None, ALU.mult).then_inc(negmax, 1)

                    def evacuate(m):
                        n = P * (m // PAIRS + 1)
                        e.wait_ge(turned, b * M + m + 1 + CR)
                        e.wait_ge(pv, b * M + m - 1 + CR)
                        e.tensor_copy(pt[:, m % 2, 1, 0:n], psum[:, 5, 0:n]).then_inc(pt_dve, 1)

                    def normalize(qt):
                        e.wait_ge(pv, b * M + PAIRS * (qt + 1) + CR)
                        e.wait_ge(o_turned, b * QT + qt + 1)
                        ch.link(e.reciprocal(rden[:], den[:, qt % 2, :]))
                        e.tensor_tensor(on[:, :].rearrange("p (h n) -> p h n", h=NH),
                                        psum[:, 6, :].rearrange("p (h n) -> p h n", h=NH),
                                        rden[:, :].unsqueeze(2).to_broadcast([P, NH, AHD]), ALU.mult
                                        ).then_inc(normed, 1)

                    peak(0)
                    for m in range(M + 5):
                        if m + 1 < M:
                            peak(m + 1)
                        if m < M:
                            evacuate(m)
                        if m % PAIRS == 0 and m > 0:
                            normalize(m // PAIRS - 1)
                        if m % PAIRS == 4 and m > 4:
                            qt = m // PAIRS - 1
                            e.wait_ge(out_mm, b * QT + qt + 1 + 1)
                            xv = x[:, bass.ds(b * QT + qt, 1), :].squeeze(1)
                            e.tensor_tensor(xv, xv, ps[7], ALU.add).then_inc(x_done, 1)
                    assert ch.n == NC


def mamba(nc, g, name):
    x, ps, psum, d, ident, ones, nhalf = (g[n] for n in ("x", "ps", "psum", "dram", "ident", "ones", "nhalf"))
    STEPS = SEQS * GROUPS
    NB = 2 + GT
    with ExitStack() as ctx:
        c_ = Chip(nc, ctx, name)
        hT = c_.sb("hT", [P, DT, TOK])
        TS = c_.sb("TS", [P, SEQS * NCH, 3, HEADS])
        a_dram = nc.dram_tensor(name + "a_dram", (HEADS, TOK), F32, kind="Internal").ap()
        e_dram = nc.dram_tensor(name + "e_dram", (HEADS, TOK), F32, kind="Internal").ap()
        nw = c_.sb("nw", [P, DT])
        nw_in = c_.sem("nw_in")
        with nc.Block() as block:
            @block.sync
            def _(e):
                e.dma_start(nw[:], d["norm_w"]).then_inc(nw_in, 16)
                e.wait_ge(nw_in, 16)
        with ExitStack() as pre:
            xn = pre.enter_context(nc.sbuf_tensor(name + "xn", [P, NT, D], F32))
            norm_transpose(nc, g, name + "n_", hT, xn, rms_w=nw)
        with ExitStack() as pre:
            time_steps(nc, g, Chip(nc, pre, name + "t_"), hT, TS, a_dram, e_dram)

        hw = c_.sb("hw", [P, 5, DT, P])
        gw = c_.sb("gw", [P, 4, DT, P])
        wo = c_.sb("wo", [P, GT, D])
        causal = c_.sb("causal", [P, P])
        cw = c_.sb("cw", [P, NB, TAPS + 1])
        dgn = c_.sb("dgn", [P, GT, 2])
        ts = c_.sb("ts", [P, NCH, 3, HPG])
        hid = c_.sb("hid", [P, 2, GT, SEQ])
        bc = c_.sb("bc", [P, 2, 2, SEQ])
        gate = c_.sb("gate", [P, GT, SEQ])
        z = c_.sb("z", [P, GT, SEQ])
        L = c_.sb("L", [P, 2, HPG, P])
        hc = c_.sb("hc", [P, GW])
        hcw = c_.sb("hcw", [P, GW])
        Eb = c_.sb("Eb", [P, 2, GT, P])
        yo = c_.sb("yo", [P, GT, P])
        prev = c_.sb("prev", [STATE, GW])
        eL = c_.sb("eL", [P, 2, HPG])
        cb = c_.sb("cb", [P, NCH, P])
        bt = c_.sb("bt", [P, NCH, STATE])
        sv, rstd = c_.sb("sv", [P, 4]), c_.sb("rstd", [P, 4])

        names = ("const_in", "ring_full", "wo_in", "cw_in", "acc", "hid_ready", "turned", "hc_ready",
                 "hcw_ready", "subbed", "exped", "m_ready", "eL_ready", "ssd", "prev_ready", "combined", "dskip",
                 "gated", "squared", "sum_mm", "sum_ready", "rstd_ready", "dgn_in", "dve")
        s = {n: c_.sem(n) for n in names}
        ring_free = [c_.sem(f"ring_free{i}") for i in range(2)]
        hw_in = [c_.sem(f"hw_in{i}") for i in range(5)]
        gw_in = [c_.sem(f"gw_in{i}") for i in range(4)]
        L_in = [c_.sem(f"L_in{i}") for i in range(2)]
        E_in = [c_.sem(f"E_in{i}") for i in range(2)]
        CONST_IN = 16

        class Step:

            def __init__(self, k, grp, b, grp_next):
                self.k, self.grp, self.b, self.grp_next = k, grp, b, grp_next
                self.first = isinstance(k, int) and k == 0
                self.last = isinstance(k, int) and k == STEPS - 1
                self.par = b

        CBT, BTR, HB0, OUT, HB1, GATE = 0, 1, 2, 7, 11, 16

        def use(st, pos):
            if st.first:
                n = 10 + pos - (4 if pos >= HB1 else 0)
                return n, n % 2
            if st.last:
                n = 6 + 24 * st.k + pos - (5 if pos >= OUT else 0) - (5 if pos >= GATE else 0)
                return n, n % 2
            return st.k * 24 + (6 + pos), pos % 2

        def slot_count(st, pos):
            n, bank = use(st, pos)
            return n // 2 if isinstance(n, int) else st.k * 12 + (6 + pos) // 2

        def freed(st, pos):
            return ring_free[use(st, pos)[1]], slot_count(st, pos) + 1

        def filled(st, pos):
            return use(st, pos)[0] + 1

        END = 6 + 24 * (STEPS - 1) + GATE - 10 + GT
        LAST_CONV = 10 + 1 - 12
        LAST_GATE = 14 + 1 - 12

        def run(eng, body):
            body(Step(0, 0, 0, 0))
            with eng.Fori(0, (STEPS - 2) // 2) as j:
                body(Step(j * 2 + 1, j, 1, j + 1))
                body(Step(j * 2 + 2, j + 1, 0, j + 1))
            body(Step(STEPS - 1, GROUPS - 1, 1, None))

        with nc.Block() as block:
            @block.sync
            def _(e):
                def part(name, v):
                    return d[name][bass.ds(v, 1)].squeeze(0) if not isinstance(v, int) else d[name][v]

                e.dma_start(cw[:], d["conv"][0]).then_inc(s["cw_in"], 16)
                e.dma_start(causal[:], d["causal01"]).then_inc(s["const_in"], 16)

                def hidden(grp, i):
                    G = GROUPS * GT
                    return part("win", (grp + (2 * G + i * GROUPS)) if i < 2 else (grp * GT + (G + i - 2)))

                def load_hidden(grp, i):
                    e.dma_start(hw[:, i % 5], hidden(grp, i)).then_inc(hw_in[i % 5], 16)

                for i in range(NB):
                    if i >= 5:
                        e.wait_ge(s["ring_full"], i - 4)
                    load_hidden(0, i)

                def body(st):
                    k = st.k
                    if not st.last:
                        if st.first:
                            e.wait_ge(ring_free[1], NB // 2)
                        else:
                            e.wait_ge(ring_free[1], k * 12 + LAST_CONV)
                        e.dma_start(cw[:], part("conv", st.grp_next)).then_inc(s["cw_in"], 16)
                        for i in range(NB):
                            if i >= 5:
                                e.wait_ge(s["ring_full"], filled(st, HB0 + i - 5))
                            elif st.first:
                                e.wait_ge(s["ring_full"], i + 6)
                            else:
                                e.wait_ge(s["ring_full"], k * 24 + (6 + HB1 + i + 1 - 24))
                            load_hidden(st.grp_next, i)
                    if not st.first:
                        e.wait_ge(s["squared"], k * GT)
                    e.dma_start(dgn[:], part("dgn", st.grp)).then_inc(s["dgn_in"], 16)
                    for i in range(GT):
                        if i >= 4:
                            e.wait_ge(s["ring_full"], filled(st, GATE + i - 4))
                        elif not st.first:
                            e.wait_ge(s["ring_full"], k * 24 + (6 + GATE + i + 5 - 24))
                        e.dma_start(gw[:, i % 4], part("win", st.grp * GT + i)).then_inc(gw_in[i % 4], 16)
                        if i == 3 and st.b == 0:
                            if not st.first:
                                e.wait_ge(s["ring_full"], filled(st, OUT + 3))
                            e.dma_start(wo[:], part("wout", st.grp)).then_inc(s["wo_in"], 16)

                run(e, body)

            @block.tensor
            def _(e):
                def bank_for(st, pos):
                    n, bank = use(st, pos)
                    e.wait_ge(ring_free[bank], slot_count(st, pos))
                    return bank

                def project(w, rhs_b, bank):
                    for a in range(DT):
                        last = e.matmul(ps[bank], w[:, a, :], hT[:, a, rhs_b * SEQ:(rhs_b + 1) * SEQ],
                                        start=a == 0, stop=a == DT - 1)
                    last.then_inc(s["ring_full"], 1)

                for i in range(NB):
                    e.wait_ge(hw_in[i % 5], 16 * (i // 5 + 1))
                    if i >= 2:
                        e.wait_ge(ring_free[i % 2], i // 2)
                    project(hw[:, i % 5], 0, i % 2)

                def out_product(k, b, pos_bank):
                    e.wait_ge(s["squared"], k * GT)
                    e.wait_ge(s["combined"], k * NCH)
                    for t in range(4):
                        for i in range(GT):
                            last = e.matmul(psum[:, 6, t:t + 1], gate[:, i, t * P:(t + 1) * P], ones[:, 0:1],
                                            start=i == 0, stop=i == GT - 1)
                    last.then_inc(s["sum_mm"], 1)
                    for t in range(4):
                        bank = pos_bank(t)
                        for i in range(GT):
                            last = e.matmul(ps[bank], z[:, i, t * P:(t + 1) * P], wo[:, i, :],
                                            start=i == 0, stop=i == GT - 1)
                        last.then_inc(s["ring_full"], 1)

                def body(st):
                    k, par = st.k, st.par
                    q = k * NCH
                    e.wait_ge(s["hid_ready"], k * NB + 2)
                    bank = bank_for(st, CBT)
                    for c in range(NCH):
                        cs = slice(c * P, (c + 1) * P)
                        last = e.matmul(psum[:, bank, cs], bc[:, par, 0, cs], bc[:, par, 1, cs], start=True, stop=True)
                    last.then_inc(s["ring_full"], 1)
                    bank = bank_for(st, BTR)
                    for c in range(NCH):
                        cs = slice(c * P, (c + 1) * P)
                        last = e.transpose(psum[:, bank, cs], bc[:, par, 0, cs], ident[:])
                    last.then_inc(s["ring_full"], 1)
                    for c in range(NCH):
                        cs = slice(c * P, (c + 1) * P)
                        if c == 0:
                            e.wait_ge(s["hid_ready"], k * NB + NB)
                            if not st.first:
                                e.wait_ge(s["hc_ready"], q)
                        else:
                            e.wait_ge(s["prev_ready"], k * 3 + c)
                        for i in range(GT):
                            last = e.transpose(psum[:, 2 + i // 4, (i % 4) * P:(i % 4 + 1) * P],
                                               hid[:, par, i, cs], ident[:])
                        last.then_inc(s["turned"], 1)
                        if c < 2 and not st.last:
                            for i in range(5 * c, 5 * c + 5):
                                e.wait_ge(hw_in[i % 5], (k + 1) * 32 + 16 * (i // 5 + 1))
                                bank = bank_for(st, HB0 + i if c == 0 else HB1 + i - 5)
                                project(hw[:, i % 5], 1 - par, bank)
                        if c >= 2:
                            for i in range(4 * c - 8, 4 * c - 4):
                                e.wait_ge(gw_in[i % 4], k * 32 + 16 * (i // 4 + 1))
                                bank = bank_for(st, GATE + i)
                                project(gw[:, i % 4], par, bank)
                        if c == 0 and not st.first:
                            e.wait_ge(s["wo_in"], (st.grp + 1) * 16 if st.b else st.grp * 16)
                            out_product(k, st.b, lambda t: bank_for(st, OUT + t))
                        if not (st.first and c == 0):
                            e.wait_ge(s["combined"], q + c)
                        if c:
                            if c == 1 and not st.first:
                                e.wait_ge(s["sum_ready"], k)
                            e.wait_ge(s["prev_ready"], k * 3 + c)
                            for i in range(GT):
                                e.matmul(psum[:, 6 + i // 4, (i % 4) * P:(i % 4 + 1) * P],
                                         prev[:, i * P:(i + 1) * P], bc[:, par, 1, cs], start=True, stop=True)
                        e.wait_ge(s["hc_ready"], q + c + 1)
                        if c < 3:
                            e.wait_ge(s["hcw_ready"], k * 3 + c + 1)
                            e.wait_ge(*freed(st, BTR))
                            for i in range(2):
                                e.matmul(ps[2 + i], bt[:, c, :], hcw[:, i * 512:i * 512 + 512],
                                         start=True, stop=True)
                        e.wait_ge(s["m_ready"], q + c + 1)
                        for h in range(HPG):
                            i = h // 2
                            lo = HD * (h % 2)
                            last = e.matmul(psum[lo:lo + HD, 4 + i // 4, (i % 4) * P:(i % 4 + 1) * P],
                                            hc[:, h * HD:(h + 1) * HD], L[:, c % 2, h, :], start=True, stop=True)
                        last.then_inc(s["ssd"], 1)

                run(e, body)
                e.wait_ge(s["wo_in"], GROUPS * 16)

                def tail_bank(t):
                    n = END + t
                    e.wait_ge(ring_free[n % 2], n // 2)
                    return n % 2

                out_product(STEPS, 0, tail_bank)

            @block.scalar
            def _(e):
                a3 = a_dram.rearrange("h t -> (h t)")
                e3 = e_dram.rearrange("h t -> (h t)")

                def load_decays(st_k, grp, b, c):
                    off = grp * (HPG * TOK) + (b * SEQ + c * P)
                    ap = bass.AP(tensor=a3.tensor, offset=off, ap=[[0, P], [TOK, HPG], [1, P]])
                    e.dma_start(L[:, c % 2], ap).then_inc(L_in[c % 2], 16)

                def load_starts(grp, b, c):
                    for half in range(2):
                        off = grp * (HPG * TOK) + (half * TOK + b * SEQ + c * P)
                        ap = bass.AP(tensor=e3.tensor, offset=off, ap=[[0, HD], [2 * TOK, GT], [1, P]])
                        e.dma_start(Eb[HD * half:HD * half + HD, c % 2], ap).then_inc(E_in[c % 2], 16)

                def target(par, i):
                    return bc[:, par, i, :] if i < 2 else hid[:, par, i - 2, :]

                def newest_tap(par, i, bank):
                    e.activation(target(par, i), ps[bank], ACT.Identity, bias=cw[:, i, TAPS:TAPS + 1],
                                 scale=cw[:, i, TAPS - 1:TAPS]).then_inc(s["acc"], 1)

                def silu(par, i, convolved):
                    e.wait_ge(*convolved)
                    t = target(par, i)
                    e.activation(t, t, ACT.Silu).then_inc(s["hid_ready"], 1)

                load_decays(0, 0, 0, 0)
                e.wait_ge(s["cw_in"], 16)
                for i in range(NB):
                    e.wait_ge(s["ring_full"], i + 1)
                    newest_tap(0, i, i % 2)
                for i in range(NB):
                    silu(0, i, (ring_free[i % 2], i // 2 + 1))

                def square(k, i):
                    e.wait_ge(s["gated"], k * GT + (i - GT + 1))
                    e.activation(gate[:, i, :], z[:, i, :], ACT.Square)
                    e.activation(z[:, i, :], z[:, i, :], ACT.Copy, scale=dgn[:, i, 1:2]).then_inc(s["squared"], 1)

                def hidden_tile(st, i):
                    k = st.k
                    n, bank = use(st, HB0 + i if i < 5 else HB1 + i - 5)
                    e.wait_ge(s["ring_full"], n + 1)
                    if i >= 2 and not st.first:
                        e.wait_ge(s["dskip"], k * GT + (i - 2 - GT + 1))
                    newest_tap(1 - st.par, i, bank)
                    if i < 4 and not st.first:
                        square(k, 2 * i)
                        square(k, 2 * i + 1)

                def body(st):
                    k, par = st.k, st.par
                    q = k * NCH
                    if not st.last:
                        e.wait_ge(s["cw_in"], k * 16 + 32)
                    n, bank = use(st, BTR)
                    e.wait_ge(s["ring_full"], n + 1)
                    if not st.first:
                        e.wait_ge(s["ssd"], q)
                    e.copy(bt[:, :, :].rearrange("p c n -> p (c n)"), ps[bank]).then_inc(ring_free[bank], 1)
                    for c in range(NCH):
                        if c in (1, 2):
                            e.wait_ge(L_in[c % 2], k * 32 + 16 * (c // 2 + 1))
                            if not st.first:
                                e.wait_ge(s["prev_ready"], k * 3 + (c - 2))
                            e.activation(eL[:, c - 1, :], L[:, c % 2, :, P - 1], ACT.Exp).then_inc(s["eL_ready"], 1)
                        if c == 0:
                            for i in range(0 if st.last else 2):
                                hidden_tile(st, i)
                        e.wait_ge(s["subbed"], q + c + 1)
                        Lc = L[:, c % 2].rearrange("p h i -> p (h i)")
                        e.activation(Lc, Lc, ACT.Exp).then_inc(s["exped"], 1)
                        if not (st.last and c == 3):
                            if not (st.first and c == 0):
                                e.wait_ge(s["ssd"], q + c)
                                e.wait_ge(s["combined"], q + c)
                            if c < 3:
                                load_decays(k, st.grp, st.b, c + 1)
                                load_starts(st.grp, st.b, c + 1)
                            else:
                                load_decays(k, st.grp_next, 1 - st.b, 0)
                        if c < 2:
                            if not st.last:
                                for i in range(5 * c or 2, 5 * c + 5):
                                    hidden_tile(st, i)
                                for i in range(5 * c, 5 * c + 5):
                                    silu(1 - par, i, freed(st, HB0 + i if c == 0 else HB1 + i - 5))
                            elif c == 0:
                                for i in range(GT):
                                    square(k, i)
                        else:
                            for i in range(4 * c - 8, 4 * c - 4):
                                n, bank = use(st, GATE + i)
                                e.wait_ge(s["ring_full"], n + 1)
                                if not st.first:
                                    e.wait_ge(s["sum_mm"], k)
                                e.activation(gate[:, i, :], ps[bank], ACT.Silu).then_inc(ring_free[bank], 1)

                run(e, body)
                for i in range(GT):
                    square(STEPS, i)

            @block.gpsimd
            def _(e):
                def gate_products(k, gates):
                    e.wait_ge(ring_free[1], gates)
                    for i in range(GT):
                        e.wait_ge(s["dskip"], k * GT + (i - GT + 1))
                        e.tensor_tensor(z[:, i, :], z[:, i, :], gate[:, i, :], ALU.mult).then_inc(s["gated"], 1)

                def inverse_norm(k):
                    e.wait_ge(s["sum_ready"], k)
                    e.tensor_tensor(rstd[:], sv[:], nhalf[:, 0:4], ALU.pow).then_inc(s["rstd_ready"], 1)

                def body(st):
                    k = st.k
                    if not st.first:
                        gate_products(k, k * 12 + LAST_GATE)
                    for c in range(3):
                        e.wait_ge(s["hc_ready"], k * NCH + (c + 1))
                        if not (st.first and c == 0):
                            e.wait_ge(s["ssd"], k * NCH + c)
                        e.tensor_tensor(hcw[:, :].rearrange("p (h n) -> p h n", h=HPG),
                                        hc[:, :].rearrange("p (h n) -> p h n", h=HPG),
                                        ts[:, c, 2, :].unsqueeze(2).to_broadcast([P, HPG, HD]),
                                        ALU.mult).then_inc(s["hcw_ready"], 1)
                        if c == 0 and not st.first:
                            inverse_norm(k)

                run(e, body)
                gate_products(STEPS, END // 2)
                inverse_norm(STEPS)

            @block.vector
            def _(e):
                def convolve(par, i, bank, k1):
                    t = bc[:, par, i, :] if i < 2 else hid[:, par, i - 2, :]
                    e.wait_ge(s["acc"], k1 * NB + i + 1)
                    for n in (1, 2, 3):
                        ins = e.scalar_tensor_tensor(t[:, n:], ps[bank][:, :SEQ - n], cw[:, i, 3 - n:4 - n], t[:, n:],
                                                     ALU.mult, ALU.add)
                        if n < 3:
                            ch.link(ins)
                    ins.then_inc(ring_free[bank], 1)

                def masked_products(st):
                    n, bank = use(st, CBT)
                    e.wait_ge(s["ring_full"], n + 1)
                    ins = e.tensor_tensor(cb[:], ps[bank].rearrange("p (c i) -> p c i", c=NCH),
                                          causal[:, :].unsqueeze(1).to_broadcast([P, NCH, P]), ALU.mult)
                    ins.then_inc(ring_free[bank], 1)

                def combine(st_first, q, k, c, z_free=None):
                    e.wait_ge(s["ssd"], q + c + 1)
                    yd = psum[:, 4:6, :].rearrange("p b (i n) -> p (b i) n", i=4)
                    zo = psum[:, 6:8, :].rearrange("p b (i n) -> p (b i) n", i=4)
                    zc = z[:, :, c * P:(c + 1) * P]
                    if c == 0:
                        if not st_first:
                            e.wait_ge(s["ring_full"], z_free)
                        e.tensor_copy(zc, yd).then_inc(s["combined"], 1)
                    else:
                        e.wait_ge(E_in[c % 2], k * (64 if c % 2 else 32) + (64 if c == 3 else 32))
                        ch.link(e.tensor_tensor(yo[:], zo, Eb[:, c % 2], ALU.mult))
                        e.tensor_tensor(zc, yo[:], yd, ALU.add).then_inc(s["combined"], 1)

                def skips(k, par):
                    e.wait_ge(s["combined"], k * NCH)
                    e.wait_ge(s["dgn_in"], k * 16)
                    for i in range(GT):
                        e.scalar_tensor_tensor(z[:, i, :], hid[:, par, i, :], dgn[:, i, 0:1], z[:, i, :],
                                               ALU.mult, ALU.add).then_inc(s["dskip"], 1)

                def time_scalars(st):
                    if not st.first:
                        e.wait_ge(s["hcw_ready"], st.k * 3)
                    src = TS[:, st.b * NCH:(st.b + 1) * NCH, :,
                             st.grp * HPG:(st.grp + 1) * HPG] if isinstance(st.grp, int) else \
                        TS[:, st.b * NCH:(st.b + 1) * NCH, :, bass.ds(st.grp * HPG, HPG)]
                    ch.link(e.tensor_copy(ts[:], src))

                def decay_arguments(st, c):
                    e.wait_ge(L_in[c % 2], st.k * 32 + 16 * (c // 2 + 1))
                    if c in (1, 2):
                        e.wait_ge(s["eL_ready"], st.k * 2 + c)
                    for h in range(HPG):
                        last = e.tensor_scalar(L[:, c % 2, h, :], L[:, c % 2, h, :], ts[:, c, 1, h:h + 1], 0.0,
                                               ALU.subtract, ALU.min)
                    last.then_inc(s["subbed"], 1)

                def hidden_by_token(st, c):
                    k, q = st.k, st.k * NCH
                    e.wait_ge(s["turned"], q + c + 1)
                    if not (st.first and c == 0):
                        e.wait_ge(s["ssd"], q + c)
                    e.tensor_tensor(hc[:, :].rearrange("p (h n) -> p h n", h=HPG),
                                    psum[:, 2:4, :].rearrange("p b (h n) -> p (b h) n", n=HD),
                                    ts[:, c, 0, :].unsqueeze(2).to_broadcast([P, HPG, HD]),
                                    ALU.mult).then_inc(s["hc_ready"], 1)

                def decayed_products(st, c):
                    q = st.k * NCH
                    e.wait_ge(s["exped"], q + c + 1)
                    e.wait_ge(*freed(st, CBT))
                    e.tensor_tensor(L[:, c % 2], L[:, c % 2], cb[:, c, :].unsqueeze(1).to_broadcast([P, HPG, P]),
                                    ALU.mult).then_inc(s["m_ready"], 1)

                def next_state(st, c):
                    k = st.k
                    e.wait_ge(s["ssd"], k * NCH + (c + 1))
                    S = psum[:, 2:4, :].rearrange("p b n -> p (b n)")
                    if c == 0:
                        e.tensor_copy(prev[:], S).then_inc(s["prev_ready"], 1)
                    else:
                        p3 = prev[:, :].rearrange("p (h n) -> p h n", h=HPG)
                        ch.link(e.tensor_tensor(p3, p3, eL[:, c - 1, :].unsqueeze(2).to_broadcast([P, HPG, HD]),
                                                ALU.mult))
                        e.tensor_tensor(prev[:], prev[:], S, ALU.add).then_inc(s["prev_ready"], 1)

                def sums(k):
                    e.wait_ge(s["sum_mm"], k)
                    e.tensor_scalar(sv[:], psum[:, 6, 0:4], 1.0 / GW, EPS, ALU.mult, ALU.add
                                    ).then_inc(s["sum_ready"], 1)

                def outputs(k, b, where):
                    e.wait_ge(s["rstd_ready"], k)
                    for t in range(4):
                        n, bank = where(t)
                        e.wait_ge(s["ring_full"], n + 1)
                        xt = x[:, b * 4 + t, :]
                        ins = e.scalar_tensor_tensor(xt, ps[bank], rstd[:, t:t + 1], xt, ALU.mult, ALU.add)
                        ins.then_inc(ring_free[bank], 1)

                ch = Chain(e, s["dve"])
                e.wait_ge(s["const_in"], CONST_IN)
                for i in range(NB):
                    convolve(0, i, i % 2, 0)
                total = {"first": None}
                PER = NB * 2 + 1 + 3 + 2

                def body(st):
                    nonlocal ch
                    k, par, q = st.k, st.par, st.k * NCH
                    if not st.first:
                        ch = Chain(e, s["dve"], (k - 1) * PER + total["first"])

                    def conv(i):
                        if not st.last:
                            n, bank = use(st, HB0 + i if i < 5 else HB1 + i - 5)
                            convolve(1 - par, i, bank, k + 1)

                    masked_products(st)
                    if not st.first:
                        combine(False, (k - 1) * NCH, k - 1, 3)
                    conv(0)
                    if not st.first:
                        skips(k, 1 - par)
                    time_scalars(st)
                    decay_arguments(st, 0)
                    conv(1)
                    hidden_by_token(st, 0)
                    conv(2)
                    conv(3)
                    decayed_products(st, 0)
                    conv(4)
                    if not st.first:
                        sums(k)
                        outputs(k, 1 - par, lambda t: use(st, OUT + t))
                    for c in (1, 2, 3):
                        next_state(st, c - 1)
                        combine(st.first, q, k, c - 1, filled(st, OUT + 3))
                        decay_arguments(st, c)
                        hidden_by_token(st, c)
                        if c == 1:
                            for i in (5, 6, 7, 8, 9):
                                conv(i)
                                if i == 6:
                                    decayed_products(st, c)
                        else:
                            decayed_products(st, c)
                    if st.first:
                        total["first"] = ch.n
                    elif not st.last:
                        assert ch.n == PER, ch.n

                run(e, body)
                ch = Chain(e, s["dve"], (STEPS - 2) * PER + total["first"] + ch.n)
                combine(False, (STEPS - 1) * NCH, STEPS - 1, 3)
                skips(STEPS, 1)
                sums(STEPS)
                outputs(STEPS, 1, lambda t: (END + t, (END + t) % 2))


def time_steps(nc, g, c_, hT, TS, a_dram, e_dram):
    ps, psum, d, ident = g["ps"], g["psum"], g["dram"], g["ident"]
    w = c_.sb("w", [P, DT, HEADS])
    hp = c_.sb("hp", [P, 2])
    A = c_.sb("A", [P, 1])
    zz, az, ez, w1 = (c_.sb(n, [P, TOK]) for n in ("zz", "az", "ez", "w1"))
    dt, acs, dec, E = (c_.sb(n, [P, TOK]) for n in ("dt", "acs", "dec", "E"))
    one = c_.sb("one", [P, P])
    w_in, mm, zz_ready, az_ready, ez_ready, w1_ready, ln_ready, a_ready, acs_ready, e_ready, dif, dec_ready, turned, \
        copied, stored, dve, init = (
            c_.sem(n) for n in ("w_in", "mm", "zz_ready", "az_ready", "ez_ready", "w1_ready", "ln_ready", "a_ready",
                                "acs_ready", "e_ready", "dif", "dec_ready", "turned", "copied", "stored", "dve",
                                "init"))
    NTC = TOK // CHUNK
    with nc.Block() as block:
        @block.sync
        def _(e):
            e.dma_start(w[:], d["win"][-1 + (2 * INNER + 2 * GROUPS * STATE + HEADS) // P]).then_inc(w_in, 16)
            e.dma_start(hp[:], d["heads"]).then_inc(w_in, 16)
            e.wait_ge(acs_ready, NTC)
            e.dma_start(a_dram, acs[:]).then_inc(stored, 16)
            e.wait_ge(e_ready, 1)
            e.dma_start(e_dram, E[:]).then_inc(stored, 16)
            e.wait_ge(stored, 32)

        @block.tensor
        def _(e):
            e.wait_ge(w_in, 32)
            for h in range(SEQS):
                for a in range(DT):
                    last = e.matmul(ps[h], w[:, a, :], hT[:, a, h * SEQ:(h + 1) * SEQ], start=a == 0,
                                    stop=a == DT - 1)
                last.then_inc(mm, 1)
            for n, (src, sem, v) in enumerate(((dt, acs_ready, NTC), (acs, acs_ready, NTC), (dec, dec_ready, 1))):
                e.wait_ge(sem, v)
                for t in range(NTC):
                    last = e.transpose(psum[:, 2 + 2 * n + t // 4, (t % 4) * P:(t % 4 + 1) * P],
                                       src[:, t * P:(t + 1) * P], ident[:])
                    if t % 4 == 3:
                        last.then_inc(turned, 1)

        @block.vector
        def _(e):
            ch = Chain(e, dve)
            e.memset(one[:], 1.0).then_inc(init, 1)
            e.wait_ge(w_in, 32)
            for h in range(SEQS):
                e.wait_ge(mm, h + 1)
                e.tensor_scalar(zz[:, h * SEQ:(h + 1) * SEQ], ps[h], hp[:, 0:1], None, ALU.add).then_inc(zz_ready, 1)
            e.wait_ge(ez_ready, 1)
            e.tensor_scalar(w1[:], ez[:], 1.0, None, ALU.add).then_inc(w1_ready, 1)
            e.wait_ge(w1_ready, 1)
            ch.link(e.scalar_tensor_tensor(ez[:], w1[:], -1.0, ez[:], ALU.add, ALU.subtract))
            ch.link(e.scalar_tensor_tensor(dt[:], zz[:], 0.0, ez[:], ALU.max, ALU.subtract))
            e.wait_ge(ln_ready, 1)
            ch.link(e.tensor_tensor(dt[:], dt[:], az[:], ALU.add))
            e.wait_ge(a_ready, 1)
            ch.link(e.tensor_scalar(A[:], A[:], -1.0, None, ALU.mult))
            ch.link(e.tensor_scalar(w1[:], dt[:], A[:, 0:1], None, ALU.mult))
            e.wait_ge(init, 1)
            for t in range(NTC):
                sl = slice(t * P, (t + 1) * P)
                e.tensor_tensor_scan(acs[:, sl], one[:], w1[:, sl], 0.0, ALU.mult, ALU.add).then_inc(acs_ready, 1)
            e.wait_ge(acs_ready, NTC)
            a3 = acs[:, :].rearrange("p (t n) -> p t n", t=NTC)
            e.tensor_tensor(dec[:, :].rearrange("p (t n) -> p t n", t=NTC),
                            a3[:, :, P - 1:P].to_broadcast([P, NTC, P]), a3, ALU.subtract).then_inc(dif, 1)
            for n in range(6):
                e.wait_ge(turned, n + 1)
                src = ps[2 + n].rearrange("p (t h) -> p t h", t=4)
                e.tensor_copy(TS[:, 4 * (n % 2):4 * (n % 2) + 4, n // 2, :], src).then_inc(copied, 1)

        @block.scalar
        def _(e):
            e.wait_ge(w_in, 32)
            e.activation(A[:], hp[:, 1:2], ACT.Exp).then_inc(a_ready, 1)
            e.wait_ge(zz_ready, SEQS)
            e.activation(az[:], zz[:], ACT.Abs).then_inc(az_ready, 1)
            e.wait_ge(az_ready, 1)
            e.activation(ez[:], az[:], ACT.Exp, scale=-1.0).then_inc(ez_ready, 1)
            e.wait_ge(w1_ready, 1)
            e.activation(az[:], w1[:], ACT.Ln).then_inc(ln_ready, 1)
            e.wait_ge(acs_ready, NTC)
            e.activation(E[:], acs[:], ACT.Exp).then_inc(e_ready, 1)
            e.wait_ge(dif, 1)
            e.activation(dec[:], dec[:], ACT.Exp).then_inc(dec_ready, 1)


def build(nc, d, out, stages):
    ctx = ExitStack()
    with ctx:
        c = Chip(nc, ctx, "s_")
        g = {"dram": d, "x": c.sb("x", [P, NT, D]), "ident": c.sb("ident", [P, P]), "ones": c.sb("ones", [P, P]),
             "nhalf": c.sb("nhalf", [P, 16]),
             "psum": ctx.enter_context(nc.psum_tensor("psum", [P, 8, 512], F32))}
        g["ps"] = [g["psum"][:, i, :] for i in range(8)]
        loaded, stored, const = c.sem("loaded"), c.sem("stored"), c.sem("const")
        xv = d["x"].rearrange("(t p) n -> p t n", p=P)
        with nc.Block() as block:
            @block.sync
            def _(e):
                e.dma_start(g["x"][:], xv).then_inc(loaded, 16)
                e.dma_start(g["ident"][:], d["ident"]).then_inc(loaded, 16)
                e.wait_ge(loaded, 32)

            @block.gpsimd
            def _(e):
                e.memset(g["ones"][:], 1.0).then_inc(const, 1)
                e.memset(g["nhalf"][:], -0.5).then_inc(const, 1)
                e.wait_ge(const, 2)
        for n, s in enumerate(stages):
            STAGES[s](nc, g, f"{s}{n}_")
        with nc.Block() as block:
            @block.sync
            def _(e):
                e.dma_start(out.rearrange("(t p) n -> p t n", p=P), g["x"][:]).then_inc(stored, 16)
                e.wait_ge(stored, 16)


STAGES = {"ffn": q4_ffn, "mamba": mamba, "routed": routed_ffn, "attn": attention}
ORDER = ["ffn", "mamba", "ffn", "routed", "attn", "routed"]


def shape_constants():
    c = {"ident": np.eye(P, dtype=np.float32)}
    c["causal01"] = np.triu(np.ones((P, P), np.float32))
    c["causal_add"] = np.where(np.tri(P, dtype=bool), 0.0, -1e30).astype(np.float32)
    hi, lo = (0, 4), (28, 28)
    sh = np.zeros((P, 5, 2), np.int32)
    for p in range(P):
        sh[p, 0] = hi if p < 64 else lo
        for k in range(4):
            sh[p, k + 1] = lo if ((k * HID + p) // 64) % 2 else hi
    for dd in range(D):
        for f in range(0, HID, 32):
            assert tuple(sh[f % P, dd % 4 + 1]) == (lo if ((dd * HID + f) // 64) % 2 else hi)
    c["shifts"] = sh
    inv = (1.0 / np.float32(10000.0) ** (np.arange(0, AHD, 2, dtype=np.float32) / np.float32(AHD))).astype(np.float32)
    fr = np.outer(np.arange(SEQ, dtype=np.float32), inv).astype(np.float32)
    emb = np.concatenate([fr, fr], -1).T
    c["cos"] = np.tile(np.cos(emb), (P // AHD, 1)).astype(np.float32)
    c["sin"] = np.tile(np.sin(emb), (P // AHD, 1)).astype(np.float32)
    rot = np.zeros((P, P), np.float32)
    for h in range(P // AHD):
        for i in range(AHD // 2):
            rot[h * AHD + i + AHD // 2, h * AHD + i] = -1.0
            rot[h * AHD + i, h * AHD + i + AHD // 2] = 1.0
    c["rot"] = rot
    par = np.zeros((P, 2), np.float32)
    par[:, 0] = (np.arange(P) // AHD) % 2 == 0
    par[:, 1] = (np.arange(P) // AHD) % 2 == 1
    c["parity"] = par
    return c


def layouts(i):
    a = {k: np.asarray(v) for k, v in i.items()}
    o = {"x": a["L0_attn_x"].reshape(TOK, D)}
    for n in ("1", "3"):
        o["w" + n] = a["L0_ffn_w" + n].reshape(HID, DT, 64).transpose(2, 1, 0)
        o["s" + n] = a["L0_ffn_s" + n].reshape(HID, DT, 2).transpose(2, 1, 0)
    w2 = a["L0_ffn_w2"]
    o["w2"] = np.repeat(w2[:, None, :], 2, axis=1).reshape(D, HID).T
    o["s2"] = np.repeat(a["L0_ffn_s2"], 2).reshape(D, HID // 32).T
    wi = a["L0_attn_in_proj_w"]
    o["win"] = wi.reshape(-1, P, DT, P).transpose(0, 3, 2, 1)
    o["wout"] = a["L0_attn_out_proj_w"].T.reshape(GROUPS, GT, P, D).transpose(0, 2, 1, 3)
    cw = np.concatenate([a["L0_attn_conv_w"], a["L0_attn_conv_b"][:, None]], axis=1)
    ct = cw.reshape(-1, P, TAPS + 1)
    o["conv"] = np.stack([np.stack([ct[GROUPS * GT + gr], ct[GROUPS * GT + GROUPS + gr],
                                    *ct[gr * GT:(gr + 1) * GT]], axis=1) for gr in range(GROUPS)])
    dp = np.repeat(a["L0_attn_Dp"], HD).reshape(GROUPS, GT, P)
    gn = a["L0_attn_gnorm_w"].reshape(GROUPS, GT, P)
    o["dgn"] = np.stack([dp, gn], axis=-1).transpose(0, 2, 1, 3)
    o["norm_w"] = a["L0_attn_norm_w"].reshape(DT, P).T
    o["heads"] = np.stack([a["L0_attn_dt_bias"], a["L0_attn_A_log"]], axis=1)
    o["wq"] = a["L1_attn_Wq"].T
    o["wk"] = np.repeat(a["L1_attn_Wk"].reshape(NKV, 1, AHD, D), NH // NKV, axis=1).reshape(NH * AHD, D).T
    o["wv"] = a["L1_attn_Wv"].T
    o["wo"] = a["L1_attn_Wo"].T
    o["rWqT"] = a["L1_ffn_Wq"].T
    o["WrT"] = a["L1_ffn_Wr"].T
    o["akT"] = a["L1_ffn_aux_keys"].T
    o["avT"] = a["L1_ffn_aux_values"].T
    o["WvdT"] = a["L1_ffn_Wvd"].T
    o["WvuT"] = a["L1_ffn_Wvu"].T
    o["Wu1T"] = a["L1_ffn_Wu1"].T
    o["bu1"] = a["L1_ffn_bu1"][:, None]
    o["Wu2"] = a["L1_ffn_Wu2"].T
    o["bu2"] = a["L1_ffn_bu2"]
    o["gate_w1"] = a["L1_ffn_gate_w1"].reshape(1)
    o["gate_bias"] = a["L1_ffn_gate_bias"].reshape(1)
    o["lrel"] = a["L1_ffn_log_rel"]
    o = {k: np.ascontiguousarray(v) for k, v in o.items()}
    o.update({k: np.ascontiguousarray(v) for k, v in shape_constants().items()})
    return o


def kernel(**inputs):
    import concourse.bacc as _bacc
    from concourse.bass_utils import run_bass_kernel_spmd as _run

    nc = _bacc.Bacc("TRN2", target_bir_lowering=False, num_devices=1)
    arrays = {f"in_{k}": v for k, v in layouts(inputs).items()}
    d = {k[3:]: nc.dram_tensor(k, v.shape, mybir.dt.from_np(v.dtype), kind="ExternalInput").ap()
         for k, v in arrays.items()}
    out = nc.dram_tensor("out_0_dram", (TOK, D), F32, kind="ExternalOutput").ap()
    build(nc, d, out, ORDER)
    r = _run(nc, [arrays], core_ids=[0])
    return r.results[0]["out_0_dram"].reshape(SEQS, SEQ, D)
```

```python
import math
from contextlib import ExitStack

import numpy as np

import concourse.bass as bass
from concourse import mybir
from concourse.alu_op_type import AluOpType as ALU

F32 = mybir.dt.float32
F32R = mybir.dt.float32r
I32 = mybir.dt.int32
ACT = mybir.ActivationFunctionType
AX = mybir.AxisListType

P = 128
SEQS, SEQ, D = 2, 512, 512
TOK = SEQS * SEQ
NT = TOK // P
DT = D // P
EPS = 1e-5
HID = 1376
FT = -(-HID // P)
HEADS, HD, GROUPS, STATE, TAPS, CHUNK = 128, 64, 8, 128, 4, 128
INNER = HEADS * HD
HPG = HEADS // GROUPS
GW = HPG * HD
GT = GW // P
NCH = SEQ // CHUNK
NH, NKV, AHD = 32, 8, 16
BOT, RDIM, NSLOT, VB, UH = 64, 48, 128, 32, 128


class Chip:

    def __init__(self, nc, ctx, prefix):
        self.nc, self.ctx, self.prefix, self.sems = nc, ctx, prefix, []
        ctx.callback(self.leave)

    def leave(self):
        self.nc.clear_and_free_semaphores(self.sems)
        self.nc.all_engine_barrier()

    def sb(self, name, shape, dtype=F32):
        return self.ctx.enter_context(self.nc.sbuf_tensor(self.prefix + name, shape, dtype))

    def pair(self, name, shape):
        return Pair(self.sb(name + "_hi", shape, F32R), self.sb(name + "_lo", shape, F32R))

    def sem(self, name):
        self.sems.append(self.nc.alloc_semaphore(name=self.prefix + name))
        return self.sems[-1]


class Pair:

    def __init__(self, hi, lo):
        self.hi, self.lo, self.hi_read = hi, lo, hi[:].bitcast(F32)


def matmul3(e, out, wh, wl, mh, ml, start, stop):
    e.matmul(out, wh, ml, start=start, stop=False)
    e.matmul(out, wh, mh, start=False, stop=False)
    return e.matmul(out, wl, mh, start=False, stop=stop)


class Chain:

    def __init__(self, eng, sem, base=0):
        self.eng, self.sem, self.base, self.n = eng, sem, base, 0

    def step(self, ins):
        ins.then_inc(self.sem, 1)
        self.n += 1

    def wait(self):
        self.eng.wait_ge(self.sem, self.base + self.n)

    def link(self, ins):
        self.step(ins)
        self.wait()


def norm_transpose(nc, g, name, dst, xn, rms_w=None, var_out=None):
    x, ps, ident, nhalf = g["x"], g["ps"], g["ident"], g["nhalf"]
    with ExitStack() as ctx:
        c = Chip(nc, ctx, name)
        st = c.sb("st", [P, NT, 6])
        mv = c.sb("mv", [P, NT, 2])
        ve = c.sb("ve", [P, NT])
        rstd = c.sb("rstd", [P, NT])
        ss = c.sb("ss", [P, NT])
        sq = c.sb("sq", [P, 2, D])
        r2 = c.sb("r2", [P, NT])
        xr = c.sb("xr", [P, NT, D]) if rms_w is not None else xn
        paired = isinstance(dst, Pair)
        xw = c.sb("xw", [P, 2, DT, P]) if rms_w is not None else None
        var_ready, rstd_ready, xn_ready, ss_ready, r2_ready, xr_ready, t_done, t_used, dve, v2, hi_ready, \
            lo_ready = (c.sem(s) for s in ("var_ready", "rstd_ready", "xn_ready", "ss_ready", "r2_ready",
                                           "xr_ready", "t_done", "t_used", "dve", "v2", "hi_ready", "lo_ready"))

        def bank(t):
            return ps[t % 2].rearrange("p (a n) -> p a n", a=DT)

        def cols(t):
            return slice(t * P, (t + 1) * P)

        with nc.Block() as block:
            @block.vector
            def _(e):
                ch = Chain(e, dve)
                for t in range(NT):
                    ch.step(e.bn_stats(st[:, t, :], x[:, t, :]))
                ch.wait()
                for t in range(NT):
                    ch.step(e.bn_aggr(mv[:, t, :], st[:, t, :]))
                ch.wait()
                e.tensor_scalar(ve[:], mv[:, :, 1], EPS, None, ALU.add).then_inc(var_ready, 1)
                e.wait_ge(rstd_ready, 1)
                for t in range(NT):
                    e.tensor_scalar(xn[:, t, :], x[:, t, :], mv[:, t, 0:1], rstd[:, t:t + 1],
                                    ALU.subtract, ALU.mult).then_inc(xn_ready, 1)
                if var_out is not None:
                    e.wait_ge(xn_ready, NT)
                    for t in range(NT):
                        ch.step(e.bn_stats(st[:, t, :], xn[:, t, :]))
                    ch.wait()
                    for t in range(NT):
                        ch.step(e.bn_aggr(mv[:, t, :], st[:, t, :]))
                    ch.wait()
                    ch.link(e.tensor_copy(var_out[:], mv[:, :, 1]))
                if rms_w is not None:
                    e.wait_ge(xn_ready, NT)
                    for t in range(NT):
                        ch.step(e.tensor_tensor(x[:, t, :], x[:, t, :], xn[:, t, :], ALU.add))
                    e.wait_ge(ss_ready, NT)
                    e.tensor_scalar(ve[:], ss[:], 1.0 / D, EPS, ALU.mult, ALU.add).then_inc(v2, 1)
                    e.wait_ge(r2_ready, 1)
                    for t in range(NT):
                        e.tensor_scalar(xr[:, t, :], xn[:, t, :], r2[:, t:t + 1], None,
                                        ALU.mult).then_inc(xr_ready, 1)
                    for t in range(NT):
                        e.wait_ge(t_done, t + 1)
                        if t >= 2:
                            e.wait_ge(lo_ready, t - 1)
                        w = rms_w[:, :].unsqueeze(2).to_broadcast([P, DT, P])
                        e.tensor_tensor(xw[:, t % 2], bank(t), w, ALU.mult).then_inc(t_used, 1)
                elif paired:
                    for t in range(NT):
                        e.wait_ge(hi_ready, t + 1)
                        e.tensor_tensor(dst.lo[:, :, cols(t)], bank(t), dst.hi_read[:, :, cols(t)],
                                        ALU.subtract).then_inc(t_used, 1)

            @block.gpsimd
            def _(e):
                e.wait_ge(var_ready, 1)
                e.tensor_tensor(rstd[:], ve[:], nhalf[:, 0:NT], ALU.pow).then_inc(rstd_ready, 1)
                if rms_w is not None:
                    e.wait_ge(v2, 1)
                    e.tensor_tensor(r2[:], ve[:], nhalf[:, 0:NT], ALU.pow).then_inc(r2_ready, 1)
                    for t in range(NT):
                        e.wait_ge(hi_ready, t + 1)
                        e.tensor_tensor(dst.lo[:, :, cols(t)], xw[:, t % 2], dst.hi_read[:, :, cols(t)],
                                        ALU.subtract).then_inc(lo_ready, 1)

            @block.scalar
            def _(e):
                if rms_w is not None:
                    for t in range(NT):
                        e.wait_ge(xn_ready, t + 1)
                        if t >= 2:
                            e.wait_ge(ss_ready, t - 1)
                        e.activation(sq[:, t % 2, :], xn[:, t, :], ACT.Square,
                                     accum_out=ss[:, t:t + 1]).then_inc(ss_ready, 1)
                    for t in range(NT):
                        e.wait_ge(t_used, t + 1)
                        e.copy(dst.hi[:, :, cols(t)], xw[:, t % 2]).then_inc(hi_ready, 1)
                else:
                    for t in range(NT):
                        e.wait_ge(t_done, t + 1)
                        if paired:
                            e.copy(dst.hi[:, :, cols(t)], bank(t)).then_inc(hi_ready, 1)
                        else:
                            e.copy(dst[:, :, cols(t)], bank(t)).then_inc(t_used, 1)

            @block.tensor
            def _(e):
                for t in range(NT):
                    e.wait_ge(xr_ready if rms_w is not None else xn_ready, t + 1)
                    if t >= 2:
                        e.wait_ge(t_used, t - 1)
                    for a in range(DT):
                        last = e.transpose(ps[t % 2][:, a * P:(a + 1) * P], xr[:, t, a * P:(a + 1) * P],
                                           ident[:])
                    last.then_inc(t_done, 1)


def q4_ffn(nc, g, name):
    x, ps, d = g["x"], g["ps"], g["dram"]
    with ExitStack() as ctx:
        c = Chip(nc, ctx, name)
        hT = c.pair("hT", [P, DT, TOK])
        with ExitStack() as pre:
            xn = pre.enter_context(nc.sbuf_tensor(name + "xn", [P, NT, D], F32))
            norm_transpose(nc, g, name + "n_", hT, xn)
        NS = 4
        raw = c.sb("raw", [P, 2, 512], I32)
        scl = c.sb("scl", [P, 2, 512])
        deq = c.sb("deq", [P, 2, 512])
        w = c.pair("w", [P, NS, 512])
        shifts = c.sb("shifts", [P, 5, 2], I32)
        hh = c.pair("hh", [P, FT, TOK])
        hf = c.sb("hf", [P, 2, SEQ])
        sil = c.sb("sil", [P, 2, SEQ])
        sh_in, shifted, deq_ready, w_hi, w_lo, a_done, b_done, silued, hf_ready, hh_hi, hh_lo, w_used, o_done, \
            x_done = (c.sem(s) for s in ("sh_in", "shifted", "deq_ready", "w_hi", "w_lo", "a_done", "b_done",
                                         "silued", "hf_ready", "hh_hi", "hh_lo", "w_used", "o_done", "x_done"))
        raw_in = [c.sem(f"raw_in{i}") for i in range(2)]
        FTAIL = HID - (FT - 1) * P
        NW = 3 * FT

        def rows(f):
            return P if f < FT - 1 else FTAIL

        def tile(u):
            return (u % 2, u // 2) if u < 2 * FT else (2, u - 2 * FT)

        def loads(u):
            m, f = tile(u)
            return 4 if m < 2 else 1 + (4 if f < FT - 1 else FTAIL // 32)

        def arrived(u):
            return 16 * sum(loads(v) for v in range(u % 2, u + 1, 2))

        def view(t, u):
            m, f = tile(u)
            if m == 2:
                return t[0:rows(f), :]
            return t[:, 0:DT * rows(f)].rearrange("p (a n) -> p a n", a=DT)

        with nc.Block() as block:
            @block.sync
            def _(e):
                e.dma_start(shifts[:], d["shifts"]).then_inc(sh_in, 16)
                for u in range(NW):
                    m, f = tile(u)
                    r, n = rows(f), u % 2
                    if u >= 2:
                        e.wait_ge(deq_ready, u - 1)
                    rv, sv = view(raw[:, n, :], u), view(scl[:, n, :], u)
                    if m < 2:
                        s = ("1", "3")[m]
                        for half in range(2):
                            hs = slice(64 * half, 64 * half + 64)
                            e.dma_start(rv[hs], d["w" + s][:, :, f * P:f * P + r]).then_inc(raw_in[n], 16)
                            e.dma_start(sv[hs], d["s" + s][half, :, f * P:f * P + r].partition_broadcast(64)
                                        ).then_inc(raw_in[n], 16)
                    else:
                        e.dma_start(rv, d["w2"][f * P:f * P + r, :]).then_inc(raw_in[n], 16)
                        for q in range(r // 32):
                            e.dma_start(sv[32 * q:32 * q + 32], d["s2"][4 * f + q].partition_broadcast(32)
                                        ).then_inc(raw_in[n], 16)

            @block.vector
            def _(e):
                e.wait_ge(sh_in, 16)
                done = [0]

                def dequantize(u):
                    m, f = tile(u)
                    r, n = (P, u % 2) if m < 2 else (rows(f), u % 2)
                    e.wait_ge(raw_in[n], arrived(u))
                    parts = [(view(raw[:, n, :], u), 0)] if m < 2 else \
                        [(raw[0:r, n, :].rearrange("p (n k) -> p n k", k=4)[:, :, k], k + 1) for k in range(4)]
                    for v, k in parts:
                        e.tensor_scalar(v, v, shifts[0:r, k, 0:1], shifts[0:r, k, 1:2],
                                        ALU.logical_shift_left, ALU.arith_shift_right).then_inc(shifted, 1)
                    done[0] += len(parts)
                    e.wait_ge(shifted, done[0])
                    if u >= 2:
                        e.wait_ge(w_lo, u - 1)
                    e.tensor_tensor(view(deq[:, n, :], u), view(raw[:, n, :], u), view(scl[:, n, :], u),
                                    ALU.mult).then_inc(deq_ready, 1)

                for u in range(4):
                    dequantize(u)
                for f in range(FT):
                    r = rows(f)
                    for u in (2 * f + 4, 2 * f + 5):
                        dequantize(u)
                    for h in range(2):
                        n = 2 * f + h
                        bank = 4 * (f % 2) + 2 + h
                        e.wait_ge(silued, n + 1)
                        e.wait_ge(b_done, n + 1)
                        e.tensor_tensor(hf[0:r, h, :], ps[bank][0:r, :], sil[0:r, h, :], ALU.mult
                                        ).then_inc(hf_ready, 1)
                        e.wait_ge(hh_hi, n + 1)
                        e.tensor_tensor(hh.lo[0:r, f, h * SEQ:(h + 1) * SEQ], hf[0:r, h, :],
                                        hh.hi_read[0:r, f, h * SEQ:(h + 1) * SEQ], ALU.subtract
                                        ).then_inc(hh_lo, 1)
                for u in range(2 * FT + 4, NW):
                    dequantize(u)
                for t in range(NT):
                    e.wait_ge(o_done, t + 1)
                    e.scalar_tensor_tensor(x[:, t, :], ps[t], 0.5, x[:, t, :], ALU.mult, ALU.add
                                           ).then_inc(x_done, 1)

            @block.gpsimd
            def _(e):
                for u in range(NW):
                    e.wait_ge(w_hi, u + 1)
                    e.tensor_tensor(view(w.lo[:, u % NS, :], u), view(deq[:, u % 2, :], u),
                                    view(w.hi_read[:, u % NS, :], u), ALU.subtract).then_inc(w_lo, 1)

            @block.scalar
            def _(e):
                def split(u):
                    e.wait_ge(deq_ready, u + 1)
                    if u >= NS:
                        m, f = tile(u - NS)
                        e.wait_ge((a_done, b_done, w_used)[m], 2 * f + 2 if m < 2 else f + 1)
                    e.copy(view(w.hi[:, u % NS, :], u), view(deq[:, u % 2, :], u)).then_inc(w_hi, 1)

                for u in range(4):
                    split(u)
                for f in range(FT):
                    r = rows(f)
                    for h in range(2):
                        n = 2 * f + h
                        e.wait_ge(a_done, n + 1)
                        if f:
                            e.wait_ge(hf_ready, n - 1)
                        e.activation(sil[0:r, h, :], ps[4 * (f % 2) + h][0:r, :], ACT.Silu).then_inc(silued, 1)
                    for h in range(2):
                        n = 2 * f + h
                        e.wait_ge(hf_ready, n + 1)
                        e.copy(hh.hi[0:r, f, h * SEQ:(h + 1) * SEQ], hf[0:r, h, :]).then_inc(hh_hi, 1)
                        split(2 * f + 4 + h)
                for u in range(2 * FT + 4, NW):
                    split(u)

            @block.tensor
            def _(e):
                for f in range(FT):
                    r = rows(f)
                    for m in range(2):
                        u = 2 * f + m
                        e.wait_ge(w_lo, u + 1)
                        wh, wl = view(w.hi[:, u % NS, :], u), view(w.lo[:, u % NS, :], u)
                        for h in range(2):
                            n = 2 * f + h
                            bank = 4 * (f % 2) + 2 * m + h
                            if f >= 2:
                                e.wait_ge(hf_ready, n - 3)
                            for a in range(DT):
                                sl = (slice(None), a, slice(h * SEQ, (h + 1) * SEQ))
                                last = matmul3(e, ps[bank][0:r, :], wh[:, a, :], wl[:, a, :], hT.hi[sl], hT.lo[sl],
                                               a == 0, a == DT - 1)
                            last.then_inc((a_done, b_done)[m], 1)
                e.wait_ge(hh_lo, 2 * FT)
                for f in range(FT):
                    r, u = rows(f), 2 * FT + f
                    e.wait_ge(w_lo, u + 1)
                    for t in range(NT):
                        sl = (slice(0, r), f, slice(t * P, (t + 1) * P))
                        last = matmul3(e, ps[t], hh.hi[sl], hh.lo[sl], w.hi[0:r, u % NS, :], w.lo[0:r, u % NS, :],
                                       f == 0, f == FT - 1)
                        if f == FT - 1:
                            last.then_inc(o_done, 1)
                        elif t == NT - 1:
                            last.then_inc(w_used, 1)


def routed_ffn(nc, g, name):
    x, ps, d, ident, ones, nhalf = g["x"], g["ps"], g["dram"], g["ident"], g["ones"], g["nhalf"]
    with ExitStack() as ctx:
        c = Chip(nc, ctx, name)
        hT = c.sb("hT", [P, DT, TOK])
        xn = c.sb("xn", [P, NT, D])
        var = c.sb("var", [P, NT])
        norm_transpose(nc, g, name + "n_", hT, xn, var_out=var)
        WqT = c.sb("WqT", [P, DT, BOT])
        Wu1T = c.sb("Wu1T", [P, DT, UH])
        WvdT = c.sb("WvdT", [P, DT, VB])
        avT = c.sb("avT", [P, DT, NSLOT])
        WrT = c.sb("WrT", [BOT, RDIM])
        akT = c.sb("akT", [BOT, NSLOT])
        WvuT = c.sb("WvuT", [VB, D])
        lrel = c.sb("lrel", [P, NSLOT])
        sc = c.sb("sc", [P, 4])
        sc2 = c.sb("sc2", [P, 3])
        qT = c.sb("qT", [BOT, TOK])
        rqT = c.sb("rqT", [RDIM, TOK])
        rkT = c.sb("rkT", [RDIM, NSLOT])
        vd = c.sb("vd", [NSLOT, VB])
        u = c.sb("u", [UH, TOK])
        u2 = c.sb("u2", [UH, TOK])
        u3 = c.sb("u3", [UH, TOK])
        rs = c.sb("rs", [P, NT, NSLOT])
        at = c.sb("at", [P, NT, NSLOT])
        rep = c.sb("rep", [P, NT, NSLOT])
        top = c.sb("top", [P, NT, 8])
        mx = c.sb("mx", [P, NT])
        den = c.sb("den", [P, NT])
        wT = c.sb("wT", [NSLOT, TOK])
        lowT = c.sb("lowT", [VB, TOK])
        lv = c.sb("lv", [P, NT])
        lvs = c.sb("lvs", [P, 1])
        s1 = c.sb("s1", [P, NT])
        s2 = c.sb("s2", [P, NT])
        gate = c.sb("gate", [P, NT])
        msk = c.sb("msk", [P, NT])
        w_in, q_mm, q_sb, rk_mm, rk_sb, rq_mm, rq_sb, vd_mm, vd_sb, u_mm, u_sb, gelu, lr_mm, sc_mm, picked, neg, \
            exped, norm, t_mm, t_sb, low_mm, low_sb, o_mm, o_used, dve, lvr, lv_mm, act, tanhed, ez, fin = (
                c.sem(s) for s in ("w_in", "q_mm", "q_sb", "rk_mm", "rk_sb", "rq_mm", "rq_sb", "vd_mm", "vd_sb",
                                   "u_mm", "u_sb", "gelu", "lr_mm", "sc_mm", "picked", "neg", "exped", "norm",
                                   "t_mm", "t_sb", "low_mm", "low_sb", "o_mm", "o_used", "dve", "lvr", "lv_mm",
                                   "act", "tanhed", "ez", "fin"))
        loads = [(WqT, "rWqT"), (Wu1T, "Wu1T"), (WvdT, "WvdT"), (avT, "avT")]
        small = [(WrT, "WrT"), (akT, "akT"), (WvuT, "WvuT")]
        NL = 16 * (len(loads) + len(small) + 3 + 3)
        BIG = 1e30
        C0 = math.sqrt(2.0 / math.pi)

        with nc.Block() as block:
            @block.sync
            def _(e):
                for dst, src in loads:
                    e.dma_start(dst[:], d[src].rearrange("(a p) n -> p a n", p=P)).then_inc(w_in, 16)
                for dst, src in small:
                    e.dma_start(dst[:], d[src]).then_inc(w_in, 16)
                e.dma_start(lrel[:], d["lrel"].partition_broadcast(P)).then_inc(w_in, 16)
                e.dma_start(sc[:, 0:1], d["bu1"]).then_inc(w_in, 16)
                e.dma_start(sc[:, 1:2], d["Wu2"]).then_inc(w_in, 16)
                for n, s in enumerate(("bu2", "gate_w1", "gate_bias")):
                    e.dma_start(sc2[:, n:n + 1], d[s].partition_broadcast(P)).then_inc(w_in, 16)

            @block.tensor
            def _(e):
                e.wait_ge(w_in, NL)
                for h in range(2):
                    for a in range(DT):
                        last = e.matmul(ps[h][0:BOT, :], WqT[:, a, :], hT[:, a, h * 512:h * 512 + 512],
                                        start=a == 0, stop=a == DT - 1)
                    last.then_inc(q_mm, 1)
                e.matmul(ps[2][0:RDIM, 0:NSLOT], WrT[:], akT[:], start=True, stop=True).then_inc(rk_mm, 1)
                for a in range(DT):
                    last = e.matmul(ps[3][:, 0:VB], avT[:, a, :], WvdT[:, a, :], start=a == 0, stop=a == DT - 1)
                last.then_inc(vd_mm, 1)
                for h in range(2):
                    for a in range(DT):
                        last = e.matmul(ps[4 + h][:, :], Wu1T[:, a, :], hT[:, a, h * 512:h * 512 + 512],
                                        start=a == 0, stop=a == DT - 1)
                    last.then_inc(u_mm, 1)
                for h in range(2):
                    e.wait_ge(q_sb, h + 1)
                    e.matmul(ps[6 + h][0:RDIM, :], WrT[:], qT[:, h * 512:h * 512 + 512],
                             start=True, stop=True).then_inc(rq_mm, 1)
                e.wait_ge(rk_sb, 1)
                for t in range(NT):
                    e.wait_ge(rq_sb, t // 4 + 1)
                    if t < 2:
                        e.wait_ge(vd_sb, 1)
                        e.wait_ge(q_sb, 2)
                    else:
                        e.wait_ge(dve, 2 * (t - 1))
                    e.matmul(ps[t % 2][:, 0:NSLOT], rqT[:, t * P:(t + 1) * P], rkT[:], start=True, stop=True)
                    e.matmul(ps[2 + t % 2][:, 0:NSLOT], qT[:, t * P:(t + 1) * P], akT[:],
                             start=True, stop=True).then_inc(sc_mm, 1)
                e.wait_ge(lvr, 1)
                e.wait_ge(u_sb, 2)
                e.matmul(ps[4][:, 0:1], ones[:], lvs[:], start=True, stop=True).then_inc(lv_mm, 1)
                e.wait_ge(gelu, 1)
                for t in range(NT):
                    last = e.matmul(ps[5][:, t:t + 1], u[:, t * P:(t + 1) * P], sc[:, 1:2], start=True, stop=True)
                last.then_inc(lr_mm, 1)
                e.wait_ge(norm, NT)
                e.wait_ge(rq_sb, 2)
                for h in range(2):
                    for t in range(4):
                        n = 4 * h + t
                        last = e.transpose(ps[6 + h][:, t * P:(t + 1) * P], at[:, n, :], ident[:])
                    last.then_inc(t_mm, 1)
                e.wait_ge(dve, 2 * NT)
                for h in range(2):
                    e.wait_ge(t_sb, h + 1)
                    e.matmul(ps[h][0:VB, :], vd[:], wT[:, h * 512:h * 512 + 512],
                             start=True, stop=True).then_inc(low_mm, 1)
                for t in range(NT):
                    e.wait_ge(low_sb, t // 4 + 1)
                    if t >= 2:
                        e.wait_ge(o_used, t - 1)
                    e.matmul(ps[2 + t % 2][:, :], lowT[:, t * P:(t + 1) * P], WvuT[:],
                             start=True, stop=True).then_inc(o_mm, 1)

            @block.scalar
            def _(e):
                for h in range(2):
                    e.wait_ge(q_mm, h + 1)
                    e.copy(qT[:, h * 512:h * 512 + 512], ps[h][0:BOT, :]).then_inc(q_sb, 1)
                e.wait_ge(rk_mm, 1)
                e.copy(rkT[:], ps[2][0:RDIM, 0:NSLOT]).then_inc(rk_sb, 1)
                e.wait_ge(vd_mm, 1)
                e.copy(vd[:], ps[3][:, 0:VB]).then_inc(vd_sb, 1)
                for h in range(2):
                    e.wait_ge(u_mm, h + 1)
                    e.activation(u[:, h * 512:h * 512 + 512], ps[4 + h][:, :], ACT.Identity,
                                 bias=sc[:, 0:1]).then_inc(u_sb, 1)
                for h in range(2):
                    e.wait_ge(rq_mm, h + 1)
                    e.copy(rqT[:, h * 512:h * 512 + 512], ps[6 + h][0:RDIM, :]).then_inc(rq_sb, 1)
                e.activation(lv[:], var[:], ACT.Ln, bias=1.0, accum_out=lvs[:]).then_inc(lvr, 1)
                e.wait_ge(act, 1)
                e.activation(u3[:], u3[:], ACT.Tanh, scale=C0).then_inc(tanhed, 1)
                for t in range(NT):
                    e.wait_ge(neg, t + 1)
                    e.activation(at[:, t, :], at[:, t, :], ACT.Exp, bias=mx[:, t:t + 1],
                                 accum_out=den[:, t:t + 1]).then_inc(exped, 1)
                e.wait_ge(act, 2)
                e.activation(s1[:], s1[:], ACT.Exp, scale=-1.0).then_inc(ez, 1)
                e.wait_ge(act, 3)
                e.activation(gate[:], gate[:], ACT.Exp, scale=-1.0).then_inc(ez, 1)
                for h in range(2):
                    e.wait_ge(t_mm, h + 1)
                    e.copy(wT[:, h * 512:h * 512 + 512], ps[6 + h][:, :]).then_inc(t_sb, 1)
                for h in range(2):
                    e.wait_ge(low_mm, h + 1)
                    e.copy(lowT[:, h * 512:h * 512 + 512], ps[h][0:VB, :]).then_inc(low_sb, 1)

            @block.vector
            def _(e):
                ch = Chain(e, fin)
                e.wait_ge(u_sb, 2)
                ch.link(e.tensor_tensor(u2[:], u[:], u[:], ALU.mult))
                ch.link(e.tensor_scalar(u2[:], u2[:], 0.044715, 1.0, ALU.mult, ALU.add))
                e.tensor_tensor(u3[:], u2[:], u[:], ALU.mult).then_inc(act, 1)
                for t in range(NT):
                    e.wait_ge(sc_mm, t + 1)
                    e.scalar_tensor_tensor(rs[:, t, :], ps[t % 2][:, 0:NSLOT], RDIM ** -0.5, lrel[:],
                                           ALU.mult, ALU.add).then_inc(dve, 1)
                    e.scalar_tensor_tensor(at[:, t, :], ps[2 + t % 2][:, 0:NSLOT], BOT ** -0.5, lrel[:],
                                           ALU.mult, ALU.add).then_inc(dve, 1)
                e.wait_ge(dve, 2 * NT)
                for t in range(NT):
                    ch.step(e.max(out=top[:, t, :], in_=rs[:, t, :]))
                ch.wait()
                for t in range(NT):
                    ch.step(e.match_replace(out=rep[:, t, :], in_to_replace=top[:, t, :], in_values=rs[:, t, :],
                                            imm_value=-3.0e38))
                ch.wait()
                for t in range(NT):
                    ch.step(e.tensor_tensor(rs[:, t, :], rs[:, t, :], rep[:, t, :], ALU.not_equal))
                ch.wait()
                for t in range(NT):
                    ch.step(e.tensor_scalar(rep[:, t, :], rs[:, t, :], -1.0, BIG, ALU.add, ALU.mult))
                    ch.step(e.tensor_tensor(at[:, t, :], at[:, t, :], rs[:, t, :], ALU.mult))
                ch.wait()
                for t in range(NT):
                    ch.step(e.tensor_tensor(at[:, t, :], at[:, t, :], rep[:, t, :], ALU.add))
                ch.wait()
                for t in range(NT):
                    ch.link(e.tensor_reduce(mx[:, t:t + 1], at[:, t, :], AX.X, ALU.max))
                    e.tensor_scalar(mx[:, t:t + 1], mx[:, t:t + 1], -1.0, None, ALU.mult).then_inc(neg, 1)
                e.wait_ge(tanhed, 1)
                ch.step(e.tensor_scalar(u3[:], u3[:], 1.0, 0.5, ALU.add, ALU.mult))
                ch.wait()
                e.tensor_tensor(u[:], u[:], u3[:], ALU.mult).then_inc(gelu, 1)
                e.wait_ge(exped, NT)
                ch.link(e.reciprocal(den[:], den[:]))
                for t in range(NT):
                    e.tensor_scalar(at[:, t, :], at[:, t, :], den[:, t:t + 1], None, ALU.mult).then_inc(norm, 1)
                e.wait_ge(lv_mm, 1)
                ch.link(e.tensor_scalar(lvs[:], ps[4][:, 0:1], 1.0 / TOK, 1e-6, ALU.mult, ALU.add))
                ch.link(e.reciprocal(lvs[:], lvs[:]))
                ch.step(e.tensor_scalar(s2[:], lv[:], lvs[:], 0.5, ALU.mult, ALU.mult))
                e.wait_ge(lr_mm, 1)
                e.tensor_scalar(s1[:], ps[5][:, 0:NT], sc2[:, 0:1], None, ALU.add).then_inc(act, 1)
                e.wait_ge(ez, 1)
                ch.link(e.tensor_scalar(s1[:], s1[:], 1.0, None, ALU.add))
                ch.link(e.reciprocal(s1[:], s1[:]))
                ch.link(e.scalar_tensor_tensor(s1[:], s1[:], 2.5, s2[:], ALU.mult, ALU.add))
                ch.link(e.tensor_scalar(s1[:], s1[:], 0.0, 5.0, ALU.max, ALU.min))
                ch.link(e.tensor_scalar(s1[:], s1[:], -0.5, 1.0 / 1.5, ALU.add, ALU.mult))
                ch.link(e.tensor_scalar(s1[:], s1[:], 0.0, 1.0, ALU.max, ALU.min))
                e.tensor_scalar(gate[:], s1[:], sc2[:, 1:2], sc2[:, 2:3], ALU.mult, ALU.add).then_inc(act, 1)
                e.wait_ge(ez, 2)
                ch.link(e.tensor_scalar(gate[:], gate[:], 1.0, None, ALU.add))
                ch.link(e.reciprocal(gate[:], gate[:]))
                ch.link(e.tensor_scalar(msk[:], gate[:], 0.05, 0.5, ALU.is_ge, ALU.mult))
                ch.link(e.tensor_tensor(gate[:], gate[:], msk[:], ALU.mult))
                for t in range(NT):
                    ch.step(e.scalar_tensor_tensor(x[:, t, :], xn[:, t, :], 0.5, x[:, t, :], ALU.mult, ALU.add))
                ch.wait()
                for t in range(NT):
                    e.wait_ge(o_mm, t + 1)
                    e.scalar_tensor_tensor(x[:, t, :], ps[2 + t % 2][:, :], gate[:, t:t + 1], x[:, t, :],
                                           ALU.mult, ALU.add).then_inc(o_used, 1)


def attention(nc, g, name):
    x, ps, psum, d, ident = g["x"], g["ps"], g["psum"], g["dram"], g["ident"]
    QT = SEQ // P
    PAIRS = NH // 2
    M = QT * PAIRS
    NP = 2 * DT
    SCALE = AHD ** -0.5
    with ExitStack() as ctx:
        c = Chip(nc, ctx, name)
        hT = c.sb("hT", [P, DT, TOK])
        with ExitStack() as pre:
            xn = pre.enter_context(nc.sbuf_tensor(name + "xn", [P, NT, D], F32))
            norm_transpose(nc, g, name + "n_", hT, xn)
        wq, wk, wo = (c.sb(n, [P, DT, D]) for n in ("wq", "wk", "wo"))
        wv = c.sb("wv", [P, DT, NKV * AHD])
        cos, sin, rot = c.sb("cos", [P, SEQ]), c.sb("sin", [P, SEQ]), c.sb("rot", [P, P])
        par, cmask = c.sb("par", [P, 2]), c.sb("cmask", [P, P])
        hb = c.sb("hb", [P, DT, SEQ])
        raw = c.sb("raw", [P, 2, SEQ])
        t0, t1 = c.sb("t0", [P, SEQ]), c.sb("t1", [P, SEQ])
        q = c.sb("q", [P, DT, SEQ])
        kk = c.sb("kk", [P, 2, DT, SEQ])
        v = c.sb("v", [P, QT, NKV * AHD])
        pr = c.sb("pr", [P, 2, 2, SEQ])
        pt = c.sb("pt", [P, 2, 2, SEQ])
        mx = c.sb("mx", [P, 2, 2])
        nm = c.sb("nm", [P, 2, 2])
        den = c.sb("den", [P, 2, NH])
        rden = c.sb("rden", [P, NH])
        on = c.sb("on", [P, D])
        oT = c.sb("oT", [P, DT, P])
        w_in, hb_ready, proj, raw_ready, rotated, roped, scores, negmax, exped, turned, pt_act, pt_dve, pv, \
            normed, o_turned, oT_ready, out_mm, x_done, dve = (
                c.sem(s) for s in ("w_in", "hb_ready", "proj", "raw_ready", "rotated", "roped", "scores",
                                   "negmax", "exped", "turned", "pt_act", "pt_dve", "pv", "normed", "o_turned",
                                   "oT_ready", "out_mm", "x_done", "dve"))
        NV = NP + QT
        CR = 2

        with nc.Block() as block:
            @block.sync
            def _(e):
                for dst, src in ((wq, "wq"), (wk, "wk"), (wv, "wv"), (wo, "wo")):
                    e.dma_start(dst[:], d[src].rearrange("(a p) n -> p a n", p=P)).then_inc(w_in, 16)
                for dst, src in ((cos, "cos"), (sin, "sin"), (rot, "rot"), (par, "parity"), (cmask, "causal_add")):
                    e.dma_start(dst[:], d[src]).then_inc(w_in, 16)

            @block.gpsimd
            def _(e):
                with e.Fori(0, SEQS) as b:
                    e.wait_ge(raw_ready, b * NV + CR)
                    e.tensor_copy(hb[:], hT[:, :, bass.ds(b * SEQ, SEQ)]).then_inc(hb_ready, 1)

            @block.tensor
            def _(e):
                e.sem_inc(pv, CR)
                e.sem_inc(turned, CR)
                e.sem_inc(o_turned, 1)
                e.sem_inc(out_mm, 1)
                e.wait_ge(w_in, 9 * 16)
                with e.Fori(0, SEQS) as b:
                    e.wait_ge(hb_ready, b + 1)

                    def project(n):
                        e.wait_ge(raw_ready, b * NV + n - 1 + CR)
                        bank = 4 + n % 2
                        if n < NP:
                            w = wq if n < DT else wk
                            for a in range(DT):
                                last = e.matmul(ps[bank], w[:, a, (n % DT) * P:(n % DT + 1) * P], hb[:, a, :],
                                                start=a == 0, stop=a == DT - 1)
                        else:
                            t = n - NP
                            for a in range(DT):
                                last = e.matmul(psum[:, bank, 0:NKV * AHD], hb[:, a, t * P:(t + 1) * P],
                                                wv[:, a, :], start=a == 0, stop=a == DT - 1)
                        last.then_inc(proj, 1)

                    def rotate(n):
                        e.wait_ge(raw_ready, b * NV + n + 1 + CR)
                        e.wait_ge(roped, b * NP + n - 1 + CR)
                        e.matmul(ps[6 + n % 2], rot[:], raw[:, n % 2, :], start=True, stop=True).then_inc(rotated, 1)

                    e.wait_ge(x_done, b * QT + 1)
                    project(0)
                    for n in range(1, NV):
                        project(n)
                        if n - 1 < NP:
                            rotate(n - 1)
                    e.wait_ge(roped, b * NP + NP + CR)
                    e.wait_ge(raw_ready, b * NV + NV + CR)

                    def score(m):
                        qt, u = divmod(m, PAIRS)
                        e.wait_ge(exped, b * M + m - 1 + CR)
                        T, r = divmod(u, 4)
                        n = P * (qt + 1)
                        for h in range(2):
                            last = e.matmul(psum[:, 2 * (m % 2) + h, 0:n],
                                            q[32 * r:32 * r + 32, T, qt * P:(qt + 1) * P],
                                            kk[32 * r:32 * r + 32, h, T, 0:n], start=True, stop=True)
                        last.then_inc(scores, 1)

                    def turn(m):
                        qt, u = divmod(m, PAIRS)
                        e.wait_ge(exped, b * M + m + 1 + CR)
                        e.wait_ge(pt_act, b * M + m + CR)
                        e.wait_ge(pt_dve, b * M + m + CR)
                        for h in range(2):
                            for t in range(qt + 1):
                                last = e.transpose(psum[:, 4 + h, t * P:(t + 1) * P],
                                                   pr[:, m % 2, h, t * P:(t + 1) * P], ident[:])
                        last.then_inc(turned, 1)

                    def weigh(m):
                        qt, u = divmod(m, PAIRS)
                        e.wait_ge(pt_act, b * M + m + 1 + CR)
                        e.wait_ge(pt_dve, b * M + m + 1 + CR)
                        if u == 0:
                            e.wait_ge(normed, b * QT + qt + CR)
                        for h in range(2):
                            kv = (2 * u + h) // (NH // NKV)
                            col = (2 * u + h) * AHD
                            for t in range(qt + 1):
                                last = e.matmul(psum[:, 6, col:col + AHD], pt[:, m % 2, h, t * P:(t + 1) * P],
                                                v[:, t, kv * AHD:(kv + 1) * AHD], start=t == 0, stop=t == qt)
                        last.then_inc(pv, 1)

                    def o_turn(qt):
                        e.wait_ge(normed, b * QT + qt + 1 + CR)
                        e.wait_ge(x_done, b * QT + qt + 1)
                        for a in range(DT):
                            last = e.transpose(psum[:, 7, a * P:(a + 1) * P], on[:, a * P:(a + 1) * P], ident[:])
                        last.then_inc(o_turned, 1)

                    def o_mul(qt):
                        e.wait_ge(oT_ready, b * QT + qt + 1 + CR)
                        for a in range(DT):
                            last = e.matmul(ps[7], oT[:, a, :], wo[:, a, :], start=a == 0, stop=a == DT - 1)
                        last.then_inc(out_mm, 1)

                    score(0)
                    score(1)
                    for m in range(M + 4):
                        if m < M:
                            turn(m)
                        if 1 <= m <= M:
                            weigh(m - 1)
                        if m + 2 < M:
                            score(m + 2)
                        if m % PAIRS == 1 and m > 1:
                            o_turn(m // PAIRS - 1)
                        if m % PAIRS == 3 and m > 3:
                            o_mul(m // PAIRS - 1)

            @block.scalar
            def _(e):
                e.sem_inc(raw_ready, CR)
                e.sem_inc(exped, CR)
                e.sem_inc(pt_act, CR)
                e.sem_inc(oT_ready, CR)
                with e.Fori(0, SEQS) as b:
                    for n in range(NV):
                        e.wait_ge(proj, b * NV + n + 1)
                        if n < NP:
                            e.wait_ge(roped, b * NP + n - 1 + CR)
                            e.copy(raw[:, n % 2, :], ps[4 + n % 2]).then_inc(raw_ready, 1)
                        else:
                            e.copy(v[:, n - NP, :], psum[:, 4 + n % 2, 0:NKV * AHD]).then_inc(raw_ready, 1)

                    def evacuate(m):
                        n = P * (m // PAIRS + 1)
                        e.wait_ge(turned, b * M + m + 1 + CR)
                        e.wait_ge(pv, b * M + m - 1 + CR)
                        e.copy(pt[:, m % 2, 0, 0:n], psum[:, 4, 0:n]).then_inc(pt_act, 1)

                    for m in range(M + 4):
                        if m < M:
                            n = P * (m // PAIRS + 1)
                            e.wait_ge(negmax, b * M + m + 1)
                            e.wait_ge(turned, b * M + m - 1 + CR)
                            if m % PAIRS == 0:
                                e.wait_ge(normed, b * QT + m // PAIRS - 1 + CR)
                            for h in range(2):
                                hd = 2 * (m % PAIRS) + h
                                last = e.activation(pr[:, m % 2, h, 0:n], psum[:, 2 * (m % 2) + h, 0:n], ACT.Exp,
                                                    bias=nm[:, m % 2, h:h + 1], scale=SCALE,
                                                    accum_out=den[:, (m // PAIRS) % 2, hd:hd + 1])
                            last.then_inc(exped, 1)
                        if 1 <= m <= M:
                            evacuate(m - 1)
                        if m % PAIRS == 2 and m > 2:
                            qt = m // PAIRS - 1
                            e.wait_ge(o_turned, b * QT + qt + 1 + 1)
                            e.wait_ge(out_mm, b * QT + qt + 1)
                            e.copy(oT[:], psum[:, 7, :].rearrange("p (a n) -> p a n", a=DT)).then_inc(oT_ready, 1)

            @block.vector
            def _(e):
                e.sem_inc(roped, CR)
                e.sem_inc(pt_dve, CR)
                e.sem_inc(normed, CR)
                e.sem_inc(x_done, 1)
                e.wait_ge(w_in, 9 * 16)
                NC = DT * 2 + DT * 4 + M * 2 + QT
                with e.Fori(0, SEQS) as b:
                    ch = Chain(e, dve, b * NC)
                    for n in range(NP):
                        T = n % DT
                        e.wait_ge(raw_ready, b * NV + n + 1 + CR)
                        ch.step(e.tensor_tensor(t0[:], raw[:, n % 2, :], cos[:], ALU.mult))
                        e.wait_ge(rotated, b * NP + n + 1)
                        ch.link(e.tensor_tensor(t1[:], ps[6 + n % 2], sin[:], ALU.mult))
                        if n < DT:
                            e.tensor_tensor(q[:, T, :], t0[:], t1[:], ALU.add).then_inc(roped, 1)
                            e.wait_ge(roped, b * NP + n + 1 + CR)
                        else:
                            ch.link(e.tensor_tensor(t0[:], t0[:], t1[:], ALU.add))
                            ch.step(e.tensor_scalar(kk[:, 0, T, :], t0[:], par[:, 0:1], None, ALU.mult))
                            e.tensor_scalar(kk[:, 1, T, :], t0[:], par[:, 1:2], None, ALU.mult).then_inc(roped, 1)
                            e.wait_ge(roped, b * NP + n + 1 + CR)

                    def peak(m):
                        n = P * (m // PAIRS + 1)
                        s = psum[:, 2 * (m % 2):2 * (m % 2) + 2, :]
                        e.wait_ge(scores, b * M + m + 1)
                        ch.link(e.tensor_tensor(s[:, :, n - P:n], s[:, :, n - P:n],
                                                cmask[:, :].unsqueeze(1).to_broadcast([P, 2, P]), ALU.add))
                        ch.link(e.tensor_reduce(mx[:, m % 2, :], s[:, :, 0:n], AX.X, ALU.max))
                        e.wait_ge(exped, b * M + m - 1 + CR)
                        e.tensor_scalar(nm[:, m % 2, :], mx[:, m % 2, :], -SCALE, None, ALU.mult).then_inc(negmax, 1)

                    def evacuate(m):
                        n = P * (m // PAIRS + 1)
                        e.wait_ge(turned, b * M + m + 1 + CR)
                        e.wait_ge(pv, b * M + m - 1 + CR)
                        e.tensor_copy(pt[:, m % 2, 1, 0:n], psum[:, 5, 0:n]).then_inc(pt_dve, 1)

                    def normalize(qt):
                        e.wait_ge(pv, b * M + PAIRS * (qt + 1) + CR)
                        e.wait_ge(o_turned, b * QT + qt + 1)
                        ch.link(e.reciprocal(rden[:], den[:, qt % 2, :]))
                        e.tensor_tensor(on[:, :].rearrange("p (h n) -> p h n", h=NH),
                                        psum[:, 6, :].rearrange("p (h n) -> p h n", h=NH),
                                        rden[:, :].unsqueeze(2).to_broadcast([P, NH, AHD]), ALU.mult
                                        ).then_inc(normed, 1)

                    peak(0)
                    for m in range(M + 5):
                        if m + 1 < M:
                            peak(m + 1)
                        if m < M:
                            evacuate(m)
                        if m % PAIRS == 0 and m > 0:
                            normalize(m // PAIRS - 1)
                        if m % PAIRS == 4 and m > 4:
                            qt = m // PAIRS - 1
                            e.wait_ge(out_mm, b * QT + qt + 1 + 1)
                            xv = x[:, bass.ds(b * QT + qt, 1), :].squeeze(1)
                            e.tensor_tensor(xv, xv, ps[7], ALU.add).then_inc(x_done, 1)
                    assert ch.n == NC


def mamba(nc, g, name):
    x, ps, psum, d, ident, ones, nhalf = (g[n] for n in ("x", "ps", "psum", "dram", "ident", "ones", "nhalf"))
    STEPS = SEQS * GROUPS
    NB = 2 + GT
    NRAW, NSPLIT = 2, 4
    HQ = [(0, 1), (2, 3, 4, 5), (6, 7, 8), (9,)]
    GQ = [(), (0,), (1, 2), (3, 4, 5, 6, 7)]
    assert sorted(sum(HQ, ())) == list(range(NB)) and sorted(sum(GQ, ())) == list(range(GT))
    tiles = [[("h", i) for i in HQ[c]] + [("g", i) for i in GQ[c]] for c in range(NCH)]
    USES = [("cbt", 0), ("btr", 0)] + tiles[0] + [("out", 0), ("out", 1)] + sum(tiles[1:], [])
    WTILES = tiles[0] + [("o", i) for i in range(GT)] + sum(tiles[1:], [])
    with ExitStack() as ctx:
        c_ = Chip(nc, ctx, name)
        hT = c_.pair("hT", [P, DT, TOK])
        t_dram = nc.dram_tensor(name + "t_dram", (P, SEQS * NCH, 3, HEADS), F32, kind="Internal").ap()
        a_dram = nc.dram_tensor(name + "a_dram", (HEADS, TOK), F32, kind="Internal").ap()
        e_dram = nc.dram_tensor(name + "e_dram", (HEADS, TOK), F32, kind="Internal").ap()
        nw = c_.sb("nw", [P, DT])
        nw_in = c_.sem("nw_in")
        with nc.Block() as block:
            @block.sync
            def _(e):
                e.dma_start(nw[:], d["norm_w"]).then_inc(nw_in, 16)
                e.wait_ge(nw_in, 16)
        with ExitStack() as pre:
            xn = pre.enter_context(nc.sbuf_tensor(name + "xn", [P, NT, D], F32))
            norm_transpose(nc, g, name + "n_", hT, xn, rms_w=nw)
        with ExitStack() as pre:
            time_steps(nc, g, Chip(nc, pre, name + "t_"), hT, t_dram, a_dram, e_dram)

        raw = c_.sb("raw", [P, NRAW, 512])
        w = c_.pair("w", [P, NSPLIT, 512])
        causal = c_.sb("causal", [P, P])
        cw = c_.sb("cw", [P, 2, NB, TAPS + 1])
        dgn = c_.sb("dgn", [P, 2, GT, 2])
        ts = c_.sb("ts", [P, 2, NCH, 3, HPG])
        hid = c_.sb("hid", [P, 2, GT, SEQ])
        bc = c_.sb("bc", [P, 2, 2, SEQ])
        gate = c_.sb("gate", [P, GT, SEQ])
        z = c_.sb("z", [P, GT, SEQ])
        zs = c_.pair("zs", [P, 2, SEQ])
        L = c_.sb("L", [P, 2, HPG, P])
        hc = c_.sb("hc", [P, GW])
        hcw = c_.sb("hcw", [P, GW])
        Eb = c_.sb("Eb", [P, 2, GT, P])
        yo = c_.sb("yo", [P, GT, P])
        prev = c_.sb("prev", [STATE, GW])
        eL = c_.sb("eL", [P, 2, HPG])
        cb = c_.sb("cb", [P, NCH, P])
        bt = c_.sb("bt", [P, NCH, STATE])
        sv, rstd = c_.sb("sv", [P, 4]), c_.sb("rstd", [P, 4])

        names = ("const_in", "ring_full", "w_hi", "w_lo", "cw_in", "dgn_in", "ts_in", "acc", "hid_ready", "turned",
                 "hc_ready", "hcw_ready", "subbed", "exped", "m_ready", "eL_ready", "ssd", "prev_ready",
                 "combined", "out_read", "dskip", "gated", "z_hi", "z_lo", "added", "out_used", "sum_mm", "sum_ready",
                 "rstd_ready", "dve")
        s = {n: c_.sem(n) for n in names}
        ring_free = [c_.sem(f"ring_free{i}") for i in range(2)]
        raw_in = [c_.sem(f"raw_in{i}") for i in range(NRAW)]
        L_in = [c_.sem(f"L_in{i}") for i in range(2)]
        E_in = [c_.sem(f"E_in{i}") for i in range(2)]
        CONST_IN = 16

        class Step:

            def __init__(self, k, grp, b, grp_next):
                self.k, self.grp, self.b, self.grp_next = k, grp, b, grp_next
                self.first = isinstance(k, int) and k == 0
                self.last = isinstance(k, int) and k == STEPS - 1
                self.par = b

        NU, NWT = len(USES), len(WTILES)
        assert NU % 2 == 0 and 2 * NWT % NSPLIT == 0

        def index(st, order, first_base, item):
            skipped = {"out", "o"}
            n0 = first_base - sum(i[0] in skipped for i in order)
            if st.first:
                return 0, first_base + [i for i in order if i[0] not in skipped].index(item)
            if st.last:
                return 0, n0 + st.k * len(order) + [i for i in order if i[0] != "h"].index(item)
            return len(order), n0 + order.index(item)

        def use(st, *item):
            f, n = index(st, USES, NB, item)
            return (st.k * f + n if f else n), n % 2

        def slot_count(st, *item):
            f, n = index(st, USES, NB, item)
            return st.k * (f // 2) + n // 2 if f else n // 2

        def wnumber(st, *item):
            f, n = index(st, WTILES, NB, item)
            return (st.k * f + n, st.par * f + n) if f else (n, n)

        def freed(st, *pos):
            return ring_free[use(st, *pos)[1]], slot_count(st, *pos) + 1

        def filled(st, *pos):
            return use(st, *pos)[0] + 1

        def freed_back(st, back, *item):
            n = NB - 2 + USES.index(item)
            return ring_free[n % 2], (st.k - back) * (NU // 2) + (n // 2 + 1)

        def raw_count(n, ns):
            return (n // NRAW + 1) * 16 if isinstance(n, int) else (n - (ns % NRAW)) * (16 // NRAW) + 16

        final = Step(STEPS - 1, GROUPS - 1, 1, None)
        END = use(final, "g", GT - 1)[0] + 1
        WEND = wnumber(final, "g", GT - 1)[0] + 1

        def run(eng, body):
            body(Step(0, 0, 0, 0))
            with eng.Fori(0, (STEPS - 2) // 2) as j:
                body(Step(j * 2 + 1, j, 1, j + 1))
                body(Step(j * 2 + 2, j + 1, 0, j + 1))
            body(Step(STEPS - 1, GROUPS - 1, 1, None))

        with nc.Block() as block:
            @block.sync
            def _(e):
                def part(name, v):
                    return d[name][bass.ds(v, 1)].squeeze(0) if not isinstance(v, int) else d[name][v]

                def load(n, ns, src):
                    if not isinstance(n, int) or n >= NRAW:
                        e.wait_ge(s["w_lo"], n - (NRAW - 1))
                    dst = raw[:, ns % NRAW, :]
                    if len(src.shape) == 3:
                        dst = dst.rearrange("p (a n) -> p a n", a=DT)
                    e.dma_start(dst, src).then_inc(raw_in[ns % NRAW], 16)

                def hidden(grp, i):
                    G = GROUPS * GT
                    return part("win", (grp + (2 * G + i * GROUPS)) if i < 2 else (grp * GT + (G + i - 2)))

                def out_weights(grp, i):
                    return part("wout", grp * GT + i)

                def load_scalars(st, grp, b, par):
                    src = bass.AP(tensor=t_dram.tensor, offset=grp * HPG + b * NCH * 3 * HEADS,
                                  ap=[[SEQS * NCH * 3 * HEADS, P], [HEADS, NCH * 3], [1, HPG]])
                    e.dma_start(ts[:, par].rearrange("p c q h -> p (c q) h"), src).then_inc(s["ts_in"], 16)

                e.dma_start(cw[:, 0], d["conv"][0]).then_inc(s["cw_in"], 16)
                load_scalars(None, 0, 0, 0)
                e.dma_start(causal[:], d["causal01"]).then_inc(s["const_in"], 16)
                for i in range(NB):
                    load(i, i, hidden(0, i))

                def body(st):
                    k = st.k
                    if not st.last:
                        if not st.first:
                            e.wait_ge(*freed_back(st, 2, "h", 9))
                        e.dma_start(cw[:, 1 - st.par], part("conv", st.grp_next)).then_inc(s["cw_in"], 16)
                    for kind, i in WTILES:
                        if (st.first and kind == "o") or (st.last and kind == "h"):
                            continue
                        n, ns = wnumber(st, kind, i)
                        if kind == "h":
                            load(n, ns, hidden(st.grp_next, i))
                        elif kind == "g":
                            load(n, ns, part("win", st.grp * GT + i))
                        else:
                            load(n, ns, out_weights(st.grp - (1 - st.b), i))
                        if (kind, i) == WTILES[len(tiles[0]) + GT - 1] or (st.first and (kind, i) == ("h", 1)):
                            if not st.first:
                                e.wait_ge(s["ssd"], k * NCH)
                            e.dma_start(dgn[:, st.par], part("dgn", st.grp)).then_inc(s["dgn_in"], 16)
                            if not st.last:
                                load_scalars(st, st.grp_next, 1 - st.b, 1 - st.par)

                run(e, body)
                for i in range(GT):
                    load(WEND + i, WEND + i, out_weights(GROUPS - 1, i))

            @block.tensor
            def _(e):
                def bank_for(st, *item):
                    bank = use(st, *item)[1]
                    e.wait_ge(ring_free[bank], slot_count(st, *item))
                    return bank

                def project(n, ns, rhs_b, bank):
                    e.wait_ge(s["w_lo"], n + 1)
                    wh, wl = (t[:, ns % NSPLIT, :].rearrange("p (a n) -> p a n", a=DT) for t in (w.hi, w.lo))
                    for a in range(DT):
                        sl = (slice(None), a, slice(rhs_b * SEQ, (rhs_b + 1) * SEQ))
                        last = matmul3(e, ps[bank], wh[:, a, :], wl[:, a, :], hT.hi[sl], hT.lo[sl],
                                       a == 0, a == DT - 1)
                    last.then_inc(s["ring_full"], 1)

                for i in range(NB):
                    if i >= 2:
                        e.wait_ge(ring_free[i % 2], i // 2)
                    project(i, i, 0, i % 2)

                def out_product(k, number, banks):
                    e.wait_ge(s["combined"], k * NCH)
                    for i in range(GT):
                        n, ns = number(i)
                        e.wait_ge(s["w_lo"], n + 1)
                        e.wait_ge(s["z_lo"], k * GT + (i - GT + 1))
                        for t in range(4):
                            sl = (slice(None), i % 2, slice(t * P, (t + 1) * P))
                            last = matmul3(e, ps[banks[t]], zs.hi[sl], zs.lo[sl], w.hi[:, ns % NSPLIT, :],
                                           w.lo[:, ns % NSPLIT, :], i == 0, i == GT - 1)
                            if i == GT - 1 and t < 2:
                                last.then_inc(s["ring_full"], 1)
                        last.then_inc(s["out_used"], 1)
                    e.wait_ge(s["added"], k)
                    for t in range(4):
                        last = e.matmul(psum[:, 2, t:t + 1], gate[:, 0, t * P:(t + 1) * P], ones[:, 0:1],
                                        start=True, stop=True)
                    last.then_inc(s["sum_mm"], 1)

                def body(st):
                    k, par = st.k, st.par
                    q = k * NCH
                    e.wait_ge(s["hid_ready"], k * NB + NB)
                    bank = bank_for(st, "cbt", 0)
                    for c in range(NCH):
                        cs = slice(c * P, (c + 1) * P)
                        last = e.matmul(psum[:, bank, cs], bc[:, par, 0, cs], bc[:, par, 1, cs], start=True, stop=True)
                    last.then_inc(s["ring_full"], 1)
                    bank = bank_for(st, "btr", 0)
                    for c in range(NCH):
                        cs = slice(c * P, (c + 1) * P)
                        last = e.transpose(psum[:, bank, cs], bc[:, par, 0, cs], ident[:])
                    last.then_inc(s["ring_full"], 1)

                    def states(c):
                        e.wait_ge(s["hcw_ready"], k * 3 + (c + 1))
                        e.wait_ge(*freed(st, "btr", 0))
                        for i in range(2):
                            last = e.matmul(ps[2 + i], bt[:, c, :], hcw[:, i * 512:i * 512 + 512],
                                            start=True, stop=True)
                        return last

                    for c in range(NCH):
                        cs = slice(c * P, (c + 1) * P)
                        if c:
                            e.wait_ge(s["prev_ready"], k * 3 + c)
                        elif not st.first:
                            e.wait_ge(s["hc_ready"], q)
                        for i in range(GT):
                            last = e.transpose(psum[:, 2 + i // 4, (i % 4) * P:(i % 4 + 1) * P],
                                               hid[:, par, i, cs], ident[:])
                        last.then_inc(s["turned"], 1)
                        for kind, i in tiles[c]:
                            if not (st.last and kind == "h"):
                                n, ns = wnumber(st, kind, i)
                                project(n, ns, 1 - par if kind == "h" else par, bank_for(st, kind, i))
                        if c == 0 and not st.first:
                            e.wait_ge(s["hc_ready"], q + 1)
                            out_product(k, lambda i: wnumber(st, "o", i),
                                        (bank_for(st, "out", 0), bank_for(st, "out", 1), 6, 7))
                        if not (st.first and c == 0):
                            e.wait_ge(s["combined"], q + c)
                        if c:
                            if c == 1 and not st.first:
                                e.wait_ge(s["out_read"], k)
                            for i in range(GT):
                                e.matmul(psum[:, 6 + i // 4, (i % 4) * P:(i % 4 + 1) * P],
                                         prev[:, i * P:(i + 1) * P], bc[:, par, 1, cs], start=True, stop=True)
                        e.wait_ge(s["hc_ready"], q + c + 1)
                        if c in (1, 2):
                            states(c)
                        e.wait_ge(s["m_ready"], q + c + 1)
                        for h in range(HPG):
                            i = h // 2
                            lo = HD * (h % 2)
                            last = e.matmul(psum[lo:lo + HD, 4 + i // 4, (i % 4) * P:(i % 4 + 1) * P],
                                            hc[:, h * HD:(h + 1) * HD], L[:, c % 2, h, :], start=True, stop=True)
                        if c == 0:
                            if not st.first:
                                e.wait_ge(s["sum_ready"], k)
                            last = states(0)
                        last.then_inc(s["ssd"], 1)

                run(e, body)
                for n in (END, END + 1):
                    e.wait_ge(ring_free[n % 2], n // 2)
                out_product(STEPS, lambda i: (WEND + i, WEND + i), (END % 2, (END + 1) % 2, 6, 7))

            @block.scalar
            def _(e):
                a3 = a_dram.rearrange("h t -> (h t)")
                e3 = e_dram.rearrange("h t -> (h t)")

                def load_decays(grp, b, c):
                    off = grp * (HPG * TOK) + (b * SEQ + c * P)
                    ap = bass.AP(tensor=a3.tensor, offset=off, ap=[[0, P], [TOK, HPG], [1, P]])
                    e.dma_start(L[:, c % 2], ap).then_inc(L_in[c % 2], 16)

                def load_starts(grp, b, c):
                    for half in range(2):
                        off = grp * (HPG * TOK) + (half * TOK + b * SEQ + c * P)
                        ap = bass.AP(tensor=e3.tensor, offset=off, ap=[[0, HD], [2 * TOK, GT], [1, P]])
                        e.dma_start(Eb[HD * half:HD * half + HD, c % 2], ap).then_inc(E_in[c % 2], 16)

                def target(par, i):
                    return bc[:, par, i, :] if i < 2 else hid[:, par, i - 2, :]

                def newest_tap(par, i, bank):
                    e.activation(target(par, i), ps[bank], ACT.Identity, bias=cw[:, par, i, TAPS:TAPS + 1],
                                 scale=cw[:, par, i, TAPS - 1:TAPS]).then_inc(s["acc"], 1)

                def silu(par, i, convolved):
                    e.wait_ge(*convolved)
                    t = target(par, i)
                    e.activation(t, t, ACT.Silu).then_inc(s["hid_ready"], 1)

                def decay(q, c):
                    e.wait_ge(s["subbed"], q + (c + 1))
                    Lc = L[:, c % 2].rearrange("p h i -> p (h i)")
                    e.activation(Lc, Lc, ACT.Exp).then_inc(s["exped"], 1)

                def split(n, ns):
                    if isinstance(n, int) and n >= WEND + GT:
                        return
                    e.wait_ge(raw_in[ns % NRAW], raw_count(n, ns))
                    e.copy(w.hi[:, ns % NSPLIT, :], raw[:, ns % NRAW, :]).then_inc(s["w_hi"], 1)

                def z_part(k, i, par):
                    e.wait_ge(s["gated"], k * GT + (i - GT + 1))
                    e.activation(gate[:, i, :], z[:, i, :], ACT.Square)
                    e.activation(zs.hi[:, i % 2, :], z[:, i, :], ACT.Copy, scale=dgn[:, par, i, 1:2]
                                 ).then_inc(s["z_hi"], 1)

                def z_parts(k, par, number, ahead):
                    for i in range(GT):
                        e.wait_ge(s["out_used"], k * GT + (i - GT + 1))
                        if i + 2 < GT:
                            z_part(k, i + 2, par)
                        split(*ahead(i))

                load_decays(0, 0, 0)
                for i in range(NSPLIT):
                    split(i, i)
                e.wait_ge(s["cw_in"], 16)
                for i in range(NB):
                    e.wait_ge(s["ring_full"], i + 1)
                    newest_tap(0, i, i % 2)
                    split(i + NSPLIT, i + NSPLIT)
                for i in range(NB):
                    silu(0, i, (ring_free[i % 2], i // 2 + 1))
                decay(0, 0)

                def body(st):
                    k, par = st.k, st.par
                    q = k * NCH

                    def ahead(*item):
                        n, ns = wnumber(st, *item)
                        return n + NSPLIT, ns + NSPLIT

                    if not st.last:
                        e.wait_ge(s["cw_in"], k * 16 + 32)
                    e.wait_ge(s["ring_full"], filled(st, "btr", 0))
                    if not st.first:
                        e.wait_ge(s["ssd"], q)
                    bank = use(st, "btr", 0)[1]
                    e.copy(bt[:, :, :].rearrange("p c n -> p (c n)"), ps[bank]).then_inc(ring_free[bank], 1)
                    for c in range(NCH):
                        if c in (1, 2):
                            e.wait_ge(L_in[c % 2], k * 32 + 16 * (c // 2 + 1))
                            if not st.first:
                                e.wait_ge(s["prev_ready"], k * 3 + (c - 2))
                            e.activation(eL[:, c - 1, :], L[:, c % 2, :, P - 1], ACT.Exp).then_inc(s["eL_ready"], 1)
                        if c:
                            decay(q, c)
                        if not (st.last and c == 3):
                            if not (st.first and c == 0):
                                e.wait_ge(s["ssd"], q + c)
                                e.wait_ge(s["combined"], q + c)
                            if c < 3:
                                load_decays(st.grp, st.b, c + 1)
                                load_starts(st.grp, st.b, c + 1)
                            else:
                                load_decays(st.grp_next, 1 - st.b, 0)
                        for kind, i in tiles[c]:
                            if kind == "h" and not st.last:
                                e.wait_ge(s["ring_full"], filled(st, "h", i))
                                if i >= 2 and not st.first:
                                    e.wait_ge(s["dskip"], k * GT + (i - 2 - GT + 1))
                                newest_tap(1 - par, i, use(st, "h", i)[1])
                                split(*ahead("h", i))
                        if c == 0 and not st.first:
                            z_part(k, 0, 1 - par)
                            z_part(k, 1, 1 - par)
                            z_parts(k, 1 - par, None, lambda i: ahead("o", i))
                        for kind, i in tiles[c]:
                            if kind == "g":
                                e.wait_ge(s["ring_full"], filled(st, "g", i))
                                if not st.first:
                                    e.wait_ge(s["sum_mm"], k)
                                bank = use(st, "g", i)[1]
                                e.activation(gate[:, i, :], ps[bank], ACT.Silu).then_inc(ring_free[bank], 1)
                                split(*ahead("g", i))
                        for kind, i in tiles[c]:
                            if kind == "h" and not st.last:
                                silu(1 - par, i, freed(st, "h", i))
                    if not st.last:
                        decay(q + NCH, 0)

                run(e, body)
                z_part(STEPS, 0, 1)
                z_part(STEPS, 1, 1)
                z_parts(STEPS, 1, None, lambda i: (WEND + i + NSPLIT, WEND + i + NSPLIT))

            @block.gpsimd
            def _(e):
                def split(n, ns):
                    if isinstance(n, int) and n >= WEND + GT:
                        return
                    e.wait_ge(s["w_hi"], n + 1)
                    sl = (slice(None), ns % NSPLIT, slice(None))
                    e.tensor_tensor(w.lo[sl], raw[:, ns % NRAW, :], w.hi_read[sl], ALU.subtract
                                    ).then_inc(s["w_lo"], 1)

                def gate_product(k, i):
                    e.wait_ge(s["dskip"], k * GT + (i - GT + 1))
                    e.tensor_tensor(z[:, i, :], z[:, i, :], gate[:, i, :], ALU.mult).then_inc(s["gated"], 1)

                def inverse_norm(k):
                    e.wait_ge(s["sum_ready"], k)
                    e.tensor_tensor(rstd[:], sv[:], nhalf[:, 0:4], ALU.pow).then_inc(s["rstd_ready"], 1)

                for i in range(NSPLIT + NB):
                    split(i, i)

                def body(st):
                    k = st.k

                    def ahead(*item):
                        n, ns = wnumber(st, *item)
                        split(n + NSPLIT, ns + NSPLIT)

                    def decayed(c):
                        e.wait_ge(s["hc_ready"], k * NCH + (c + 1))
                        if not (st.first and c == 0):
                            e.wait_ge(s["ssd"], k * NCH + c)
                        e.tensor_tensor(hcw[:, :].rearrange("p (h n) -> p h n", h=HPG),
                                        hc[:, :].rearrange("p (h n) -> p h n", h=HPG),
                                        ts[:, st.par, c, 2, :].unsqueeze(2).to_broadcast([P, HPG, HD]),
                                        ALU.mult).then_inc(s["hcw_ready"], 1)

                    if not st.first:
                        e.wait_ge(*freed_back(st, 1, "g", GT - 1))
                        for i in range(4):
                            gate_product(k, i)
                    if not st.last:
                        ahead("h", 0)
                    if not st.first:
                        for i in range(4, GT):
                            gate_product(k, i)
                    if not st.last:
                        ahead("h", 1)
                    decayed(0)
                    if not st.first:
                        for i in range(GT):
                            ahead("o", i)
                        inverse_norm(k)
                    for c in (1, 2, 3):
                        if c < 3:
                            decayed(c)
                        for kind, i in tiles[c]:
                            if not (st.last and kind == "h"):
                                ahead(kind, i)

                run(e, body)
                e.wait_ge(*freed(final, "g", GT - 1))
                for i in range(GT):
                    gate_product(STEPS, i)
                for i in range(GT):
                    split(WEND + i + NSPLIT, WEND + i + NSPLIT)
                inverse_norm(STEPS)

            @block.vector
            def _(e):
                def convolve(par, i, bank, k1):
                    t = bc[:, par, i, :] if i < 2 else hid[:, par, i - 2, :]
                    e.wait_ge(s["acc"], k1 * NB + i + 1)
                    for n in (1, 2, 3):
                        ins = e.scalar_tensor_tensor(t[:, n:], ps[bank][:, :SEQ - n], cw[:, par, i, 3 - n:4 - n],
                                                     t[:, n:], ALU.mult, ALU.add)
                        if n < 3:
                            ch.link(ins)
                    ins.then_inc(ring_free[bank], 1)

                def masked_products(st):
                    n, bank = use(st, "cbt", 0)
                    e.wait_ge(s["ring_full"], n + 1)
                    e.tensor_tensor(cb[:], ps[bank].rearrange("p (c i) -> p c i", c=NCH),
                                    causal[:, :].unsqueeze(1).to_broadcast([P, NCH, P]), ALU.mult
                                    ).then_inc(ring_free[bank], 1)

                def combine(st_first, q, k, c, z_free=None):
                    e.wait_ge(s["ssd"], q + c + 1)
                    yd = psum[:, 4:6, :].rearrange("p b (i n) -> p (b i) n", i=4)
                    zo = psum[:, 6:8, :].rearrange("p b (i n) -> p (b i) n", i=4)
                    zc = z[:, :, c * P:(c + 1) * P]
                    if c == 0:
                        e.tensor_copy(zc, yd).then_inc(s["combined"], 1)
                    else:
                        e.wait_ge(E_in[c % 2], k * (64 if c % 2 else 32) + (64 if c == 3 else 32))
                        ch.link(e.tensor_tensor(yo[:], zo, Eb[:, c % 2], ALU.mult))
                        e.tensor_tensor(zc, yo[:], yd, ALU.add).then_inc(s["combined"], 1)

                def skips(k, par):
                    e.wait_ge(s["combined"], k * NCH)
                    e.wait_ge(s["dgn_in"], k * 16)
                    for i in range(GT):
                        e.scalar_tensor_tensor(z[:, i, :], hid[:, par, i, :], dgn[:, par, i, 0:1], z[:, i, :],
                                               ALU.mult, ALU.add).then_inc(s["dskip"], 1)

                def decay_arguments(k, par, c):
                    e.wait_ge(L_in[c % 2], k * 32 + 16 * (c // 2 + 1))
                    if c == 0:
                        e.wait_ge(s["ts_in"], k * 16 + 16)
                    if c in (1, 2):
                        e.wait_ge(s["eL_ready"], k * 2 + c)
                    for h in range(HPG):
                        last = e.tensor_scalar(L[:, c % 2, h, :], L[:, c % 2, h, :], ts[:, par, c, 1, h:h + 1], 0.0,
                                               ALU.subtract, ALU.min)
                    last.then_inc(s["subbed"], 1)

                def hidden_by_token(st, c):
                    k, q = st.k, st.k * NCH
                    e.wait_ge(s["turned"], q + c + 1)
                    if not (st.first and c == 0):
                        e.wait_ge(s["ssd"], q + c)
                    e.tensor_tensor(hc[:, :].rearrange("p (h n) -> p h n", h=HPG),
                                    psum[:, 2:4, :].rearrange("p b (h n) -> p (b h) n", n=HD),
                                    ts[:, st.par, c, 0, :].unsqueeze(2).to_broadcast([P, HPG, HD]),
                                    ALU.mult).then_inc(s["hc_ready"], 1)

                def decayed_products(st, c):
                    q = st.k * NCH
                    e.wait_ge(s["exped"], q + c + 1)
                    if c == 0:
                        e.wait_ge(*freed(st, "cbt", 0))
                    e.tensor_tensor(L[:, c % 2], L[:, c % 2], cb[:, c, :].unsqueeze(1).to_broadcast([P, HPG, P]),
                                    ALU.mult).then_inc(s["m_ready"], 1)

                def next_state(st, c):
                    k = st.k
                    e.wait_ge(s["ssd"], k * NCH + (c + 1))
                    S = psum[:, 2:4, :].rearrange("p b n -> p (b n)")
                    if c == 0:
                        e.tensor_copy(prev[:], S).then_inc(s["prev_ready"], 1)
                    else:
                        p3 = prev[:, :].rearrange("p (h n) -> p h n", h=HPG)
                        ch.link(e.tensor_tensor(p3, p3, eL[:, c - 1, :].unsqueeze(2).to_broadcast([P, HPG, HD]),
                                                ALU.mult))
                        e.tensor_tensor(prev[:], prev[:], S, ALU.add).then_inc(s["prev_ready"], 1)

                def z_low(k, i, par):
                    e.wait_ge(s["z_hi"], k * GT + (i - GT + 1))
                    e.scalar_tensor_tensor(zs.lo[:, i % 2, :], z[:, i, :], dgn[:, par, i, 1:2],
                                           zs.hi_read[:, i % 2, :], ALU.mult, ALU.subtract).then_inc(s["z_lo"], 1)
                    if i:
                        ins = e.tensor_tensor(gate[:, 0, :], gate[:, 0, :], gate[:, i, :], ALU.add)
                        if i < GT - 1:
                            ch.link(ins)
                        else:
                            ins.then_inc(s["added"], 1)

                def outputs(k, b, where):
                    e.wait_ge(s["sum_mm"], k)
                    e.tensor_scalar(sv[:], psum[:, 2, 0:4], 1.0 / GW, EPS, ALU.mult, ALU.add
                                    ).then_inc(s["sum_ready"], 1)
                    e.wait_ge(s["out_used"], k * GT)
                    e.wait_ge(s["rstd_ready"], k)
                    for t in range(4):
                        bank = where[t]
                        xt = x[:, b * 4 + t, :]
                        ins = e.scalar_tensor_tensor(xt, ps[bank], rstd[:, t:t + 1], xt, ALU.mult, ALU.add)
                        if t < 2:
                            ins.then_inc(ring_free[bank], 1)
                    ins.then_inc(s["out_read"], 1)

                ch = Chain(e, s["dve"])
                e.wait_ge(s["const_in"], CONST_IN)
                e.wait_ge(s["cw_in"], 16)
                for i in range(NB):
                    convolve(0, i, i % 2, 0)
                decay_arguments(0, 0, 0)
                total = {"first": None}
                PER = NB * 2 + 3 + 2 + 6

                def body(st):
                    nonlocal ch
                    k, par, q = st.k, st.par, st.k * NCH
                    if not st.first:
                        ch = Chain(e, s["dve"], (k - 1) * PER + total["first"])

                    def conv(c):
                        for i in HQ[c] if not st.last else ():
                            convolve(1 - par, i, use(st, "h", i)[1], k + 1)

                    masked_products(st)
                    if not st.first:
                        combine(False, (k - 1) * NCH, k - 1, 3)
                        skips(k, 1 - par)
                    conv(0)
                    if not st.first:
                        z_low(k, 0, 1 - par)
                        z_low(k, 1, 1 - par)
                    hidden_by_token(st, 0)
                    decayed_products(st, 0)
                    if not st.first:
                        for i in range(2, GT):
                            z_low(k, i, 1 - par)
                        outputs(k, 1 - par, (use(st, "out", 0)[1], use(st, "out", 1)[1], 6, 7))
                    for c in (1, 2, 3):
                        next_state(st, c - 1)
                        decay_arguments(k, par, c)
                        combine(st.first, q, k, c - 1)
                        hidden_by_token(st, c)
                        if c == 3:
                            decayed_products(st, c)
                            conv(c)
                        else:
                            conv_first = HQ[c][:2]
                            for i in HQ[c] if not st.last else ():
                                convolve(1 - par, i, use(st, "h", i)[1], k + 1)
                                if i == conv_first[-1]:
                                    decayed_products(st, c)
                            if st.last:
                                decayed_products(st, c)
                    if not st.last:
                        decay_arguments(k + 1, 1 - par, 0)
                    if st.first:
                        total["first"] = ch.n
                    elif not st.last:
                        assert ch.n == PER, ch.n

                run(e, body)
                ch = Chain(e, s["dve"], (STEPS - 2) * PER + total["first"] + ch.n)
                combine(False, (STEPS - 1) * NCH, STEPS - 1, 3)
                skips(STEPS, 1)
                for i in range(GT):
                    z_low(STEPS, i, 1)
                outputs(STEPS, 1, (END % 2, (END + 1) % 2, 6, 7))


def time_steps(nc, g, c_, hT, t_dram, a_dram, e_dram):
    ps, psum, d, ident = g["ps"], g["psum"], g["dram"], g["ident"]
    w, ws = c_.sb("w", [P, DT, HEADS]), c_.pair("ws", [P, DT, HEADS])
    TS = c_.sb("TS", [P, SEQS * NCH, 3, HEADS])
    hp = c_.sb("hp", [P, 2])
    A = c_.sb("A", [P, 1])
    zz, az, ez, w1 = (c_.sb(n, [P, TOK]) for n in ("zz", "az", "ez", "w1"))
    dt, acs, dec, E = (c_.sb(n, [P, TOK]) for n in ("dt", "acs", "dec", "E"))
    one = c_.sb("one", [P, P])
    w_in, mm, zz_ready, az_ready, ez_ready, w1_ready, ln_ready, a_ready, acs_ready, e_ready, dif, dec_ready, turned, \
        copied, stored, dve, init, w_hi, w_lo = (
            c_.sem(n) for n in ("w_in", "mm", "zz_ready", "az_ready", "ez_ready", "w1_ready", "ln_ready", "a_ready",
                                "acs_ready", "e_ready", "dif", "dec_ready", "turned", "copied", "stored", "dve",
                                "init", "w_hi", "w_lo"))
    NTC = TOK // CHUNK
    with nc.Block() as block:
        @block.sync
        def _(e):
            e.dma_start(w[:], d["win"][-1 + (2 * INNER + 2 * GROUPS * STATE + HEADS) // P]).then_inc(w_in, 16)
            e.dma_start(hp[:], d["heads"]).then_inc(w_in, 16)
            e.wait_ge(acs_ready, NTC)
            e.dma_start(a_dram, acs[:]).then_inc(stored, 16)
            e.wait_ge(e_ready, 1)
            e.dma_start(e_dram, E[:]).then_inc(stored, 16)
            e.wait_ge(copied, 6)
            e.dma_start(t_dram, TS[:]).then_inc(stored, 16)
            e.wait_ge(stored, 48)

        @block.tensor
        def _(e):
            e.wait_ge(w_lo, 1)
            for h in range(SEQS):
                for a in range(DT):
                    sl = (slice(None), a, slice(h * SEQ, (h + 1) * SEQ))
                    last = matmul3(e, ps[h], ws.hi[:, a, :], ws.lo[:, a, :], hT.hi[sl], hT.lo[sl], a == 0,
                                   a == DT - 1)
                last.then_inc(mm, 1)
            for n, (src, sem, v) in enumerate(((dt, acs_ready, NTC), (acs, acs_ready, NTC), (dec, dec_ready, 1))):
                e.wait_ge(sem, v)
                for t in range(NTC):
                    last = e.transpose(psum[:, 2 + 2 * n + t // 4, (t % 4) * P:(t % 4 + 1) * P],
                                       src[:, t * P:(t + 1) * P], ident[:])
                    if t % 4 == 3:
                        last.then_inc(turned, 1)

        @block.vector
        def _(e):
            ch = Chain(e, dve)
            e.memset(one[:], 1.0).then_inc(init, 1)
            e.wait_ge(w_hi, 1)
            e.tensor_tensor(ws.lo[:], w[:], ws.hi_read, ALU.subtract).then_inc(w_lo, 1)
            for h in range(SEQS):
                e.wait_ge(mm, h + 1)
                e.tensor_scalar(zz[:, h * SEQ:(h + 1) * SEQ], ps[h], hp[:, 0:1], None, ALU.add).then_inc(zz_ready, 1)
            e.wait_ge(ez_ready, 1)
            e.tensor_scalar(w1[:], ez[:], 1.0, None, ALU.add).then_inc(w1_ready, 1)
            e.wait_ge(w1_ready, 1)
            ch.link(e.scalar_tensor_tensor(ez[:], w1[:], -1.0, ez[:], ALU.add, ALU.subtract))
            ch.link(e.scalar_tensor_tensor(dt[:], zz[:], 0.0, ez[:], ALU.max, ALU.subtract))
            e.wait_ge(ln_ready, 1)
            ch.link(e.tensor_tensor(dt[:], dt[:], az[:], ALU.add))
            e.wait_ge(a_ready, 1)
            ch.link(e.tensor_scalar(A[:], A[:], -1.0, None, ALU.mult))
            ch.link(e.tensor_scalar(w1[:], dt[:], A[:, 0:1], None, ALU.mult))
            e.wait_ge(init, 1)
            for t in range(NTC):
                sl = slice(t * P, (t + 1) * P)
                e.tensor_tensor_scan(acs[:, sl], one[:], w1[:, sl], 0.0, ALU.mult, ALU.add).then_inc(acs_ready, 1)
            e.wait_ge(acs_ready, NTC)
            a3 = acs[:, :].rearrange("p (t n) -> p t n", t=NTC)
            e.tensor_tensor(dec[:, :].rearrange("p (t n) -> p t n", t=NTC),
                            a3[:, :, P - 1:P].to_broadcast([P, NTC, P]), a3, ALU.subtract).then_inc(dif, 1)
            for n in range(6):
                e.wait_ge(turned, n + 1)
                src = ps[2 + n].rearrange("p (t h) -> p t h", t=4)
                e.tensor_copy(TS[:, 4 * (n % 2):4 * (n % 2) + 4, n // 2, :], src).then_inc(copied, 1)

        @block.scalar
        def _(e):
            e.wait_ge(w_in, 32)
            e.copy(ws.hi[:], w[:]).then_inc(w_hi, 1)
            e.activation(A[:], hp[:, 1:2], ACT.Exp).then_inc(a_ready, 1)
            e.wait_ge(zz_ready, SEQS)
            e.activation(az[:], zz[:], ACT.Abs).then_inc(az_ready, 1)
            e.wait_ge(az_ready, 1)
            e.activation(ez[:], az[:], ACT.Exp, scale=-1.0).then_inc(ez_ready, 1)
            e.wait_ge(w1_ready, 1)
            e.activation(az[:], w1[:], ACT.Ln).then_inc(ln_ready, 1)
            e.wait_ge(acs_ready, NTC)
            e.activation(E[:], acs[:], ACT.Exp).then_inc(e_ready, 1)
            e.wait_ge(dif, 1)
            e.activation(dec[:], dec[:], ACT.Exp).then_inc(dec_ready, 1)


def build(nc, d, out, stages):
    ctx = ExitStack()
    with ctx:
        c = Chip(nc, ctx, "s_")
        g = {"dram": d, "x": c.sb("x", [P, NT, D]), "ident": c.sb("ident", [P, P]), "ones": c.sb("ones", [P, P]),
             "nhalf": c.sb("nhalf", [P, 16]),
             "psum": ctx.enter_context(nc.psum_tensor("psum", [P, 8, 512], F32))}
        g["ps"] = [g["psum"][:, i, :] for i in range(8)]
        loaded, stored, const = c.sem("loaded"), c.sem("stored"), c.sem("const")
        xv = d["x"].rearrange("(t p) n -> p t n", p=P)
        with nc.Block() as block:
            @block.sync
            def _(e):
                e.dma_start(g["x"][:], xv).then_inc(loaded, 16)
                e.dma_start(g["ident"][:], d["ident"]).then_inc(loaded, 16)
                e.wait_ge(loaded, 32)

            @block.gpsimd
            def _(e):
                e.memset(g["ones"][:], 1.0).then_inc(const, 1)
                e.memset(g["nhalf"][:], -0.5).then_inc(const, 1)
                e.wait_ge(const, 2)
        for n, s in enumerate(stages):
            STAGES[s](nc, g, f"{s}{n}_")
        with nc.Block() as block:
            @block.sync
            def _(e):
                e.dma_start(out.rearrange("(t p) n -> p t n", p=P), g["x"][:]).then_inc(stored, 16)
                e.wait_ge(stored, 16)


STAGES = {"ffn": q4_ffn, "mamba": mamba, "routed": routed_ffn, "attn": attention}
ORDER = ["ffn", "mamba", "ffn", "routed", "attn", "routed"]


def shape_constants():
    c = {"ident": np.eye(P, dtype=np.float32)}
    c["causal01"] = np.triu(np.ones((P, P), np.float32))
    c["causal_add"] = np.where(np.tri(P, dtype=bool), 0.0, -1e30).astype(np.float32)
    hi, lo = (0, 4), (28, 28)
    sh = np.zeros((P, 5, 2), np.int32)
    for p in range(P):
        sh[p, 0] = hi if p < 64 else lo
        for k in range(4):
            sh[p, k + 1] = lo if ((k * HID + p) // 64) % 2 else hi
    for dd in range(D):
        for f in range(0, HID, 32):
            assert tuple(sh[f % P, dd % 4 + 1]) == (lo if ((dd * HID + f) // 64) % 2 else hi)
    c["shifts"] = sh
    inv = (1.0 / np.float32(10000.0) ** (np.arange(0, AHD, 2, dtype=np.float32) / np.float32(AHD))).astype(np.float32)
    fr = np.outer(np.arange(SEQ, dtype=np.float32), inv).astype(np.float32)
    emb = np.concatenate([fr, fr], -1).T
    c["cos"] = np.tile(np.cos(emb), (P // AHD, 1)).astype(np.float32)
    c["sin"] = np.tile(np.sin(emb), (P // AHD, 1)).astype(np.float32)
    rot = np.zeros((P, P), np.float32)
    for h in range(P // AHD):
        for i in range(AHD // 2):
            rot[h * AHD + i + AHD // 2, h * AHD + i] = -1.0
            rot[h * AHD + i, h * AHD + i + AHD // 2] = 1.0
    c["rot"] = rot
    par = np.zeros((P, 2), np.float32)
    par[:, 0] = (np.arange(P) // AHD) % 2 == 0
    par[:, 1] = (np.arange(P) // AHD) % 2 == 1
    c["parity"] = par
    return c


def layouts(i):
    a = {k: np.asarray(v) for k, v in i.items()}
    o = {"x": a["L0_attn_x"].reshape(TOK, D)}
    for n in ("1", "3"):
        o["w" + n] = a["L0_ffn_w" + n].reshape(HID, DT, 64).transpose(2, 1, 0)
        o["s" + n] = a["L0_ffn_s" + n].reshape(HID, DT, 2).transpose(2, 1, 0)
    w2 = a["L0_ffn_w2"]
    o["w2"] = np.repeat(w2[:, None, :], 2, axis=1).reshape(D, HID).T
    o["s2"] = np.repeat(a["L0_ffn_s2"], 2).reshape(D, HID // 32).T
    wi = a["L0_attn_in_proj_w"]
    o["win"] = wi.reshape(-1, P, DT, P).transpose(0, 3, 2, 1)
    o["wout"] = a["L0_attn_out_proj_w"].T.reshape(GROUPS * GT, P, D)
    cw = np.concatenate([a["L0_attn_conv_w"], a["L0_attn_conv_b"][:, None]], axis=1)
    ct = cw.reshape(-1, P, TAPS + 1)
    o["conv"] = np.stack([np.stack([ct[GROUPS * GT + gr], ct[GROUPS * GT + GROUPS + gr],
                                    *ct[gr * GT:(gr + 1) * GT]], axis=1) for gr in range(GROUPS)])
    dp = np.repeat(a["L0_attn_Dp"], HD).reshape(GROUPS, GT, P)
    gn = a["L0_attn_gnorm_w"].reshape(GROUPS, GT, P)
    o["dgn"] = np.stack([dp, gn], axis=-1).transpose(0, 2, 1, 3)
    o["norm_w"] = a["L0_attn_norm_w"].reshape(DT, P).T
    o["heads"] = np.stack([a["L0_attn_dt_bias"], a["L0_attn_A_log"]], axis=1)
    o["wq"] = a["L1_attn_Wq"].T
    o["wk"] = np.repeat(a["L1_attn_Wk"].reshape(NKV, 1, AHD, D), NH // NKV, axis=1).reshape(NH * AHD, D).T
    o["wv"] = a["L1_attn_Wv"].T
    o["wo"] = a["L1_attn_Wo"].T
    o["rWqT"] = a["L1_ffn_Wq"].T
    o["WrT"] = a["L1_ffn_Wr"].T
    o["akT"] = a["L1_ffn_aux_keys"].T
    o["avT"] = a["L1_ffn_aux_values"].T
    o["WvdT"] = a["L1_ffn_Wvd"].T
    o["WvuT"] = a["L1_ffn_Wvu"].T
    o["Wu1T"] = a["L1_ffn_Wu1"].T
    o["bu1"] = a["L1_ffn_bu1"][:, None]
    o["Wu2"] = a["L1_ffn_Wu2"].T
    o["bu2"] = a["L1_ffn_bu2"]
    o["gate_w1"] = a["L1_ffn_gate_w1"].reshape(1)
    o["gate_bias"] = a["L1_ffn_gate_bias"].reshape(1)
    o["lrel"] = a["L1_ffn_log_rel"]
    o = {k: np.ascontiguousarray(v) for k, v in o.items()}
    o.update({k: np.ascontiguousarray(v) for k, v in shape_constants().items()})
    return o


def kernel(**inputs):
    import concourse.bacc as _bacc
    from concourse.bass_utils import run_bass_kernel_spmd as _run

    nc = _bacc.Bacc("TRN2", target_bir_lowering=False, num_devices=1)
    arrays = {f"in_{k}": v for k, v in layouts(inputs).items()}
    d = {k[3:]: nc.dram_tensor(k, v.shape, mybir.dt.from_np(v.dtype), kind="ExternalInput").ap()
         for k, v in arrays.items()}
    out = nc.dram_tensor("out_0_dram", (TOK, D), F32, kind="ExternalOutput").ap()
    build(nc, d, out, ORDER)
    r = _run(nc, [arrays], core_ids=[0])
    return r.results[0]["out_0_dram"].reshape(SEQS, SEQ, D)
```

```python
import math
from contextlib import ExitStack

import numpy as np

import concourse.bass as bass
from concourse import mybir
from concourse.alu_op_type import AluOpType as ALU

F32 = mybir.dt.float32
F32R = mybir.dt.float32r
I32 = mybir.dt.int32
ACT = mybir.ActivationFunctionType
AX = mybir.AxisListType

P = 128
SEQS, SEQ, D = 2, 512, 512
TOK = SEQS * SEQ
NT = TOK // P
DT = D // P
EPS = 1e-5
HID = 1376
FT = -(-HID // P)
HEADS, HD, GROUPS, STATE, TAPS, CHUNK = 128, 64, 8, 128, 4, 128
INNER = HEADS * HD
HPG = HEADS // GROUPS
GW = HPG * HD
GT = GW // P
NCH = SEQ // CHUNK
NH, NKV, AHD = 32, 8, 16
BOT, RDIM, NSLOT, VB, UH = 64, 48, 128, 32, 128


class Chip:

    def __init__(self, nc, ctx, prefix):
        self.nc, self.ctx, self.prefix, self.sems = nc, ctx, prefix, []
        ctx.callback(self.leave)

    def leave(self):
        self.nc.clear_and_free_semaphores(self.sems)
        self.nc.all_engine_barrier()

    def sb(self, name, shape, dtype=F32):
        return self.ctx.enter_context(self.nc.sbuf_tensor(self.prefix + name, shape, dtype))

    def pair(self, name, shape):
        return Pair(self.sb(name + "_hi", shape, F32R), self.sb(name + "_lo", shape, F32R))

    def sem(self, name):
        self.sems.append(self.nc.alloc_semaphore(name=self.prefix + name))
        return self.sems[-1]


class Pair:

    def __init__(self, hi, lo):
        self.hi, self.lo, self.hi_read = hi, lo, hi[:].bitcast(F32)


def matmul3(e, out, wh, wl, mh, ml, start, stop):
    e.matmul(out, wh, ml, start=start, stop=False)
    e.matmul(out, wh, mh, start=False, stop=False)
    return e.matmul(out, wl, mh, start=False, stop=stop)


class Chain:

    def __init__(self, eng, sem, base=0):
        self.eng, self.sem, self.base, self.n = eng, sem, base, 0

    def step(self, ins):
        ins.then_inc(self.sem, 1)
        self.n += 1

    def wait(self):
        self.eng.wait_ge(self.sem, self.base + self.n)

    def link(self, ins):
        self.step(ins)
        self.wait()


def norm_transpose(nc, g, name, dst, xn, rms_w=None, var_out=None):
    x, ps, ident, nhalf = g["x"], g["ps"], g["ident"], g["nhalf"]
    with ExitStack() as ctx:
        c = Chip(nc, ctx, name)
        st = c.sb("st", [P, NT, 6])
        mv = c.sb("mv", [P, NT, 2])
        ve = c.sb("ve", [P, NT])
        rstd = c.sb("rstd", [P, NT])
        ss = c.sb("ss", [P, NT])
        sq = c.sb("sq", [P, 2, D])
        r2 = c.sb("r2", [P, NT])
        xr = c.sb("xr", [P, NT, D]) if rms_w is not None else xn
        paired = isinstance(dst, Pair)
        xw = c.sb("xw", [P, 2, DT, P]) if rms_w is not None else None
        var_ready, rstd_ready, xn_ready, ss_ready, r2_ready, xr_ready, t_done, t_used, dve, v2, hi_ready, \
            lo_ready = (c.sem(s) for s in ("var_ready", "rstd_ready", "xn_ready", "ss_ready", "r2_ready",
                                           "xr_ready", "t_done", "t_used", "dve", "v2", "hi_ready", "lo_ready"))

        def bank(t):
            return ps[t % 2].rearrange("p (a n) -> p a n", a=DT)

        def cols(t):
            return slice(t * P, (t + 1) * P)

        with nc.Block() as block:
            @block.vector
            def _(e):
                ch = Chain(e, dve)
                for t in range(NT):
                    ch.step(e.bn_stats(st[:, t, :], x[:, t, :]))
                ch.wait()
                for t in range(NT):
                    ch.step(e.bn_aggr(mv[:, t, :], st[:, t, :]))
                ch.wait()
                e.tensor_scalar(ve[:], mv[:, :, 1], EPS, None, ALU.add).then_inc(var_ready, 1)
                e.wait_ge(rstd_ready, 1)
                for t in range(NT):
                    e.tensor_scalar(xn[:, t, :], x[:, t, :], mv[:, t, 0:1], rstd[:, t:t + 1],
                                    ALU.subtract, ALU.mult).then_inc(xn_ready, 1)
                if var_out is not None:
                    e.wait_ge(xn_ready, NT)
                    for t in range(NT):
                        ch.step(e.bn_stats(st[:, t, :], xn[:, t, :]))
                    ch.wait()
                    for t in range(NT):
                        ch.step(e.bn_aggr(mv[:, t, :], st[:, t, :]))
                    ch.wait()
                    ch.link(e.tensor_copy(var_out[:], mv[:, :, 1]))
                if rms_w is not None:
                    e.wait_ge(xn_ready, NT)
                    for t in range(NT):
                        ch.step(e.tensor_tensor(x[:, t, :], x[:, t, :], xn[:, t, :], ALU.add))
                    e.wait_ge(ss_ready, NT)
                    e.tensor_scalar(ve[:], ss[:], 1.0 / D, EPS, ALU.mult, ALU.add).then_inc(v2, 1)
                    e.wait_ge(r2_ready, 1)
                    for t in range(NT):
                        e.tensor_scalar(xr[:, t, :], xn[:, t, :], r2[:, t:t + 1], None,
                                        ALU.mult).then_inc(xr_ready, 1)
                    for t in range(NT):
                        e.wait_ge(t_done, t + 1)
                        if t >= 2:
                            e.wait_ge(lo_ready, t - 1)
                        w = rms_w[:, :].unsqueeze(2).to_broadcast([P, DT, P])
                        e.tensor_tensor(xw[:, t % 2], bank(t), w, ALU.mult).then_inc(t_used, 1)
                elif paired:
                    for t in range(NT):
                        e.wait_ge(hi_ready, t + 1)
                        e.tensor_tensor(dst.lo[:, :, cols(t)], bank(t), dst.hi_read[:, :, cols(t)],
                                        ALU.subtract).then_inc(t_used, 1)

            @block.gpsimd
            def _(e):
                e.wait_ge(var_ready, 1)
                e.tensor_tensor(rstd[:], ve[:], nhalf[:, 0:NT], ALU.pow).then_inc(rstd_ready, 1)
                if rms_w is not None:
                    e.wait_ge(v2, 1)
                    e.tensor_tensor(r2[:], ve[:], nhalf[:, 0:NT], ALU.pow).then_inc(r2_ready, 1)
                    for t in range(NT):
                        e.wait_ge(hi_ready, t + 1)
                        e.tensor_tensor(dst.lo[:, :, cols(t)], xw[:, t % 2], dst.hi_read[:, :, cols(t)],
                                        ALU.subtract).then_inc(lo_ready, 1)

            @block.scalar
            def _(e):
                if rms_w is not None:
                    for t in range(NT):
                        e.wait_ge(xn_ready, t + 1)
                        if t >= 2:
                            e.wait_ge(ss_ready, t - 1)
                        e.activation(sq[:, t % 2, :], xn[:, t, :], ACT.Square,
                                     accum_out=ss[:, t:t + 1]).then_inc(ss_ready, 1)
                    for t in range(NT):
                        e.wait_ge(t_used, t + 1)
                        e.copy(dst.hi[:, :, cols(t)], xw[:, t % 2]).then_inc(hi_ready, 1)
                else:
                    for t in range(NT):
                        e.wait_ge(t_done, t + 1)
                        if paired:
                            e.copy(dst.hi[:, :, cols(t)], bank(t)).then_inc(hi_ready, 1)
                        else:
                            e.copy(dst[:, :, cols(t)], bank(t)).then_inc(t_used, 1)

            @block.tensor
            def _(e):
                for t in range(NT):
                    e.wait_ge(xr_ready if rms_w is not None else xn_ready, t + 1)
                    if t >= 2:
                        e.wait_ge(t_used, t - 1)
                    for a in range(DT):
                        last = e.transpose(ps[t % 2][:, a * P:(a + 1) * P], xr[:, t, a * P:(a + 1) * P],
                                           ident[:])
                    last.then_inc(t_done, 1)


def q4_ffn(nc, g, name):
    x, ps, d = g["x"], g["ps"], g["dram"]
    with ExitStack() as ctx:
        c = Chip(nc, ctx, name)
        hT = c.pair("hT", [P, DT, TOK])
        with ExitStack() as pre:
            xn = pre.enter_context(nc.sbuf_tensor(name + "xn", [P, NT, D], F32))
            norm_transpose(nc, g, name + "n_", hT, xn)
        NS = 4
        raw = c.sb("raw", [P, 2, 512], I32)
        scl = c.sb("scl", [P, 2, 512])
        deq = c.sb("deq", [P, 2, 512])
        w = c.pair("w", [P, NS, 512])
        shifts = c.sb("shifts", [P, 5, 2], I32)
        hh = c.pair("hh", [P, FT, TOK])
        hf = c.sb("hf", [P, 2, SEQ])
        sil = c.sb("sil", [P, 2, SEQ])
        sh_in, shifted, deq_ready, w_hi, w_lo, a_done, b_done, silued, hf_ready, hh_hi, hh_lo, w_used, o_done, \
            x_done = (c.sem(s) for s in ("sh_in", "shifted", "deq_ready", "w_hi", "w_lo", "a_done", "b_done",
                                         "silued", "hf_ready", "hh_hi", "hh_lo", "w_used", "o_done", "x_done"))
        raw_in = [c.sem(f"raw_in{i}") for i in range(2)]
        FTAIL = HID - (FT - 1) * P
        NW = 3 * FT

        def rows(f):
            return P if f < FT - 1 else FTAIL

        def tile(u):
            return (u % 2, u // 2) if u < 2 * FT else (2, u - 2 * FT)

        def loads(u):
            m, f = tile(u)
            return 4 if m < 2 else 1 + (4 if f < FT - 1 else FTAIL // 32)

        def arrived(u):
            return 16 * sum(loads(v) for v in range(u % 2, u + 1, 2))

        def view(t, u):
            m, f = tile(u)
            if m == 2:
                return t[0:rows(f), :]
            return t[:, 0:DT * rows(f)].rearrange("p (a n) -> p a n", a=DT)

        with nc.Block() as block:
            @block.sync
            def _(e):
                e.dma_start(shifts[:], d["shifts"]).then_inc(sh_in, 16)
                for u in range(NW):
                    m, f = tile(u)
                    r, n = rows(f), u % 2
                    if u >= 2:
                        e.wait_ge(deq_ready, u - 1)
                    rv, sv = view(raw[:, n, :], u), view(scl[:, n, :], u)
                    if m < 2:
                        s = ("1", "3")[m]
                        for half in range(2):
                            hs = slice(64 * half, 64 * half + 64)
                            e.dma_start(rv[hs], d["w" + s][:, :, f * P:f * P + r]).then_inc(raw_in[n], 16)
                            e.dma_start(sv[hs], d["s" + s][half, :, f * P:f * P + r].partition_broadcast(64)
                                        ).then_inc(raw_in[n], 16)
                    else:
                        e.dma_start(rv, d["w2"][f * P:f * P + r, :]).then_inc(raw_in[n], 16)
                        for q in range(r // 32):
                            e.dma_start(sv[32 * q:32 * q + 32], d["s2"][4 * f + q].partition_broadcast(32)
                                        ).then_inc(raw_in[n], 16)

            @block.vector
            def _(e):
                e.wait_ge(sh_in, 16)
                done = [0]

                def dequantize(u):
                    m, f = tile(u)
                    r, n = (P, u % 2) if m < 2 else (rows(f), u % 2)
                    e.wait_ge(raw_in[n], arrived(u))
                    parts = [(view(raw[:, n, :], u), 0)] if m < 2 else \
                        [(raw[0:r, n, :].rearrange("p (n k) -> p n k", k=4)[:, :, k], k + 1) for k in range(4)]
                    for v, k in parts:
                        e.tensor_scalar(v, v, shifts[0:r, k, 0:1], shifts[0:r, k, 1:2],
                                        ALU.logical_shift_left, ALU.arith_shift_right).then_inc(shifted, 1)
                    done[0] += len(parts)
                    e.wait_ge(shifted, done[0])
                    if u >= 2:
                        e.wait_ge(w_lo, u - 1)
                    e.tensor_tensor(view(deq[:, n, :], u), view(raw[:, n, :], u), view(scl[:, n, :], u),
                                    ALU.mult).then_inc(deq_ready, 1)

                for u in range(4):
                    dequantize(u)
                for f in range(FT):
                    r = rows(f)
                    for u in (2 * f + 4, 2 * f + 5):
                        dequantize(u)
                    for h in range(2):
                        n = 2 * f + h
                        bank = 4 * (f % 2) + 2 + h
                        e.wait_ge(silued, n + 1)
                        e.wait_ge(b_done, n + 1)
                        e.tensor_tensor(hf[0:r, h, :], ps[bank][0:r, :], sil[0:r, h, :], ALU.mult
                                        ).then_inc(hf_ready, 1)
                        e.wait_ge(hh_hi, n + 1)
                        e.tensor_tensor(hh.lo[0:r, f, h * SEQ:(h + 1) * SEQ], hf[0:r, h, :],
                                        hh.hi_read[0:r, f, h * SEQ:(h + 1) * SEQ], ALU.subtract
                                        ).then_inc(hh_lo, 1)
                for u in range(2 * FT + 4, NW):
                    dequantize(u)
                for t in range(NT):
                    e.wait_ge(o_done, t + 1)
                    e.scalar_tensor_tensor(x[:, t, :], ps[t], 0.5, x[:, t, :], ALU.mult, ALU.add
                                           ).then_inc(x_done, 1)

            @block.gpsimd
            def _(e):
                for u in range(NW):
                    e.wait_ge(w_hi, u + 1)
                    e.tensor_tensor(view(w.lo[:, u % NS, :], u), view(deq[:, u % 2, :], u),
                                    view(w.hi_read[:, u % NS, :], u), ALU.subtract).then_inc(w_lo, 1)

            @block.scalar
            def _(e):
                def split(u):
                    e.wait_ge(deq_ready, u + 1)
                    if u >= NS:
                        m, f = tile(u - NS)
                        e.wait_ge((a_done, b_done, w_used)[m], 2 * f + 2 if m < 2 else f + 1)
                    e.copy(view(w.hi[:, u % NS, :], u), view(deq[:, u % 2, :], u)).then_inc(w_hi, 1)

                for u in range(4):
                    split(u)
                for f in range(FT):
                    r = rows(f)
                    for h in range(2):
                        n = 2 * f + h
                        e.wait_ge(a_done, n + 1)
                        if f:
                            e.wait_ge(hf_ready, n - 1)
                        e.activation(sil[0:r, h, :], ps[4 * (f % 2) + h][0:r, :], ACT.Silu).then_inc(silued, 1)
                    for h in range(2):
                        n = 2 * f + h
                        e.wait_ge(hf_ready, n + 1)
                        e.copy(hh.hi[0:r, f, h * SEQ:(h + 1) * SEQ], hf[0:r, h, :]).then_inc(hh_hi, 1)
                        split(2 * f + 4 + h)
                for u in range(2 * FT + 4, NW):
                    split(u)

            @block.tensor
            def _(e):
                for f in range(FT):
                    r = rows(f)
                    for m in range(2):
                        u = 2 * f + m
                        e.wait_ge(w_lo, u + 1)
                        wh, wl = view(w.hi[:, u % NS, :], u), view(w.lo[:, u % NS, :], u)
                        for h in range(2):
                            n = 2 * f + h
                            bank = 4 * (f % 2) + 2 * m + h
                            if f >= 2:
                                e.wait_ge(hf_ready, n - 3)
                            for a in range(DT):
                                sl = (slice(None), a, slice(h * SEQ, (h + 1) * SEQ))
                                last = matmul3(e, ps[bank][0:r, :], wh[:, a, :], wl[:, a, :], hT.hi[sl], hT.lo[sl],
                                               a == 0, a == DT - 1)
                            last.then_inc((a_done, b_done)[m], 1)
                e.wait_ge(hh_lo, 2 * FT)
                for f in range(FT):
                    r, u = rows(f), 2 * FT + f
                    e.wait_ge(w_lo, u + 1)
                    for t in range(NT):
                        sl = (slice(0, r), f, slice(t * P, (t + 1) * P))
                        last = matmul3(e, ps[t], hh.hi[sl], hh.lo[sl], w.hi[0:r, u % NS, :], w.lo[0:r, u % NS, :],
                                       f == 0, f == FT - 1)
                        if f == FT - 1:
                            last.then_inc(o_done, 1)
                        elif t == NT - 1:
                            last.then_inc(w_used, 1)


def routed_ffn(nc, g, name):
    x, ps, d, ident, ones, nhalf = g["x"], g["ps"], g["dram"], g["ident"], g["ones"], g["nhalf"]
    with ExitStack() as ctx:
        c = Chip(nc, ctx, name)
        hT = c.sb("hT", [P, DT, TOK])
        xn = c.sb("xn", [P, NT, D])
        var = c.sb("var", [P, NT])
        norm_transpose(nc, g, name + "n_", hT, xn, var_out=var)
        WqT = c.sb("WqT", [P, DT, BOT])
        Wu1T = c.sb("Wu1T", [P, DT, UH])
        WvdT = c.sb("WvdT", [P, DT, VB])
        avT = c.sb("avT", [P, DT, NSLOT])
        WrT = c.sb("WrT", [BOT, RDIM])
        akT = c.sb("akT", [BOT, NSLOT])
        WvuT = c.sb("WvuT", [VB, D])
        lrel = c.sb("lrel", [P, NSLOT])
        sc = c.sb("sc", [P, 4])
        sc2 = c.sb("sc2", [P, 3])
        qT = c.sb("qT", [BOT, TOK])
        rqT = c.sb("rqT", [RDIM, TOK])
        rkT = c.sb("rkT", [RDIM, NSLOT])
        vd = c.sb("vd", [NSLOT, VB])
        u = c.sb("u", [UH, TOK])
        u2 = c.sb("u2", [UH, TOK])
        u3 = c.sb("u3", [UH, TOK])
        rs = c.sb("rs", [P, NT, NSLOT])
        at = c.sb("at", [P, NT, NSLOT])
        rep = c.sb("rep", [P, NT, NSLOT])
        top = c.sb("top", [P, NT, 8])
        mx = c.sb("mx", [P, NT])
        den = c.sb("den", [P, NT])
        wT = c.sb("wT", [NSLOT, TOK])
        lowT = c.sb("lowT", [VB, TOK])
        lv = c.sb("lv", [P, NT])
        lvs = c.sb("lvs", [P, 1])
        s1 = c.sb("s1", [P, NT])
        s2 = c.sb("s2", [P, NT])
        gate = c.sb("gate", [P, NT])
        msk = c.sb("msk", [P, NT])
        w_in, q_mm, q_sb, rk_mm, rk_sb, rq_mm, rq_sb, vd_mm, vd_sb, u_mm, u_sb, gelu, lr_mm, sc_mm, picked, neg, \
            exped, norm, t_mm, t_sb, low_mm, low_sb, o_mm, o_used, dve, lvr, lv_mm, act, tanhed, ez, fin = (
                c.sem(s) for s in ("w_in", "q_mm", "q_sb", "rk_mm", "rk_sb", "rq_mm", "rq_sb", "vd_mm", "vd_sb",
                                   "u_mm", "u_sb", "gelu", "lr_mm", "sc_mm", "picked", "neg", "exped", "norm",
                                   "t_mm", "t_sb", "low_mm", "low_sb", "o_mm", "o_used", "dve", "lvr", "lv_mm",
                                   "act", "tanhed", "ez", "fin"))
        loads = [(WqT, "rWqT"), (Wu1T, "Wu1T"), (WvdT, "WvdT"), (avT, "avT")]
        small = [(WrT, "WrT"), (akT, "akT"), (WvuT, "WvuT")]
        NL = 16 * (len(loads) + len(small) + 3 + 3)
        BIG = 1e30
        C0 = math.sqrt(2.0 / math.pi)

        with nc.Block() as block:
            @block.sync
            def _(e):
                for dst, src in loads:
                    e.dma_start(dst[:], d[src].rearrange("(a p) n -> p a n", p=P)).then_inc(w_in, 16)
                for dst, src in small:
                    e.dma_start(dst[:], d[src]).then_inc(w_in, 16)
                e.dma_start(lrel[:], d["lrel"].partition_broadcast(P)).then_inc(w_in, 16)
                e.dma_start(sc[:, 0:1], d["bu1"]).then_inc(w_in, 16)
                e.dma_start(sc[:, 1:2], d["Wu2"]).then_inc(w_in, 16)
                for n, s in enumerate(("bu2", "gate_w1", "gate_bias")):
                    e.dma_start(sc2[:, n:n + 1], d[s].partition_broadcast(P)).then_inc(w_in, 16)

            @block.tensor
            def _(e):
                e.wait_ge(w_in, NL)
                for h in range(2):
                    for a in range(DT):
                        last = e.matmul(ps[h][0:BOT, :], WqT[:, a, :], hT[:, a, h * 512:h * 512 + 512],
                                        start=a == 0, stop=a == DT - 1)
                    last.then_inc(q_mm, 1)
                e.matmul(ps[2][0:RDIM, 0:NSLOT], WrT[:], akT[:], start=True, stop=True).then_inc(rk_mm, 1)
                for a in range(DT):
                    last = e.matmul(ps[3][:, 0:VB], avT[:, a, :], WvdT[:, a, :], start=a == 0, stop=a == DT - 1)
                last.then_inc(vd_mm, 1)
                for h in range(2):
                    for a in range(DT):
                        last = e.matmul(ps[4 + h][:, :], Wu1T[:, a, :], hT[:, a, h * 512:h * 512 + 512],
                                        start=a == 0, stop=a == DT - 1)
                    last.then_inc(u_mm, 1)
                for h in range(2):
                    e.wait_ge(q_sb, h + 1)
                    e.matmul(ps[6 + h][0:RDIM, :], WrT[:], qT[:, h * 512:h * 512 + 512],
                             start=True, stop=True).then_inc(rq_mm, 1)
                e.wait_ge(rk_sb, 1)
                for t in range(NT):
                    e.wait_ge(rq_sb, t // 4 + 1)
                    if t < 2:
                        e.wait_ge(vd_sb, 1)
                        e.wait_ge(q_sb, 2)
                    else:
                        e.wait_ge(dve, 2 * (t - 1))
                    e.matmul(ps[t % 2][:, 0:NSLOT], rqT[:, t * P:(t + 1) * P], rkT[:], start=True, stop=True)
                    e.matmul(ps[2 + t % 2][:, 0:NSLOT], qT[:, t * P:(t + 1) * P], akT[:],
                             start=True, stop=True).then_inc(sc_mm, 1)
                e.wait_ge(lvr, 1)
                e.wait_ge(u_sb, 2)
                e.matmul(ps[4][:, 0:1], ones[:], lvs[:], start=True, stop=True).then_inc(lv_mm, 1)
                e.wait_ge(gelu, 1)
                for t in range(NT):
                    last = e.matmul(ps[5][:, t:t + 1], u[:, t * P:(t + 1) * P], sc[:, 1:2], start=True, stop=True)
                last.then_inc(lr_mm, 1)
                e.wait_ge(norm, NT)
                e.wait_ge(rq_sb, 2)
                for h in range(2):
                    for t in range(4):
                        n = 4 * h + t
                        last = e.transpose(ps[6 + h][:, t * P:(t + 1) * P], at[:, n, :], ident[:])
                    last.then_inc(t_mm, 1)
                e.wait_ge(dve, 2 * NT)
                for h in range(2):
                    e.wait_ge(t_sb, h + 1)
                    e.matmul(ps[h][0:VB, :], vd[:], wT[:, h * 512:h * 512 + 512],
                             start=True, stop=True).then_inc(low_mm, 1)
                for t in range(NT):
                    e.wait_ge(low_sb, t // 4 + 1)
                    if t >= 2:
                        e.wait_ge(o_used, t - 1)
                    e.matmul(ps[2 + t % 2][:, :], lowT[:, t * P:(t + 1) * P], WvuT[:],
                             start=True, stop=True).then_inc(o_mm, 1)

            @block.scalar
            def _(e):
                for h in range(2):
                    e.wait_ge(q_mm, h + 1)
                    e.copy(qT[:, h * 512:h * 512 + 512], ps[h][0:BOT, :]).then_inc(q_sb, 1)
                e.wait_ge(rk_mm, 1)
                e.copy(rkT[:], ps[2][0:RDIM, 0:NSLOT]).then_inc(rk_sb, 1)
                e.wait_ge(vd_mm, 1)
                e.copy(vd[:], ps[3][:, 0:VB]).then_inc(vd_sb, 1)
                for h in range(2):
                    e.wait_ge(u_mm, h + 1)
                    e.activation(u[:, h * 512:h * 512 + 512], ps[4 + h][:, :], ACT.Identity,
                                 bias=sc[:, 0:1]).then_inc(u_sb, 1)
                for h in range(2):
                    e.wait_ge(rq_mm, h + 1)
                    e.copy(rqT[:, h * 512:h * 512 + 512], ps[6 + h][0:RDIM, :]).then_inc(rq_sb, 1)
                e.activation(lv[:], var[:], ACT.Ln, bias=1.0, accum_out=lvs[:]).then_inc(lvr, 1)
                e.wait_ge(act, 1)
                e.activation(u3[:], u3[:], ACT.Tanh, scale=C0).then_inc(tanhed, 1)
                for t in range(NT):
                    e.wait_ge(neg, t + 1)
                    e.activation(at[:, t, :], at[:, t, :], ACT.Exp, bias=mx[:, t:t + 1],
                                 accum_out=den[:, t:t + 1]).then_inc(exped, 1)
                e.wait_ge(act, 2)
                e.activation(s1[:], s1[:], ACT.Exp, scale=-1.0).then_inc(ez, 1)
                e.wait_ge(act, 3)
                e.activation(gate[:], gate[:], ACT.Exp, scale=-1.0).then_inc(ez, 1)
                for h in range(2):
                    e.wait_ge(t_mm, h + 1)
                    e.copy(wT[:, h * 512:h * 512 + 512], ps[6 + h][:, :]).then_inc(t_sb, 1)
                for h in range(2):
                    e.wait_ge(low_mm, h + 1)
                    e.copy(lowT[:, h * 512:h * 512 + 512], ps[h][0:VB, :]).then_inc(low_sb, 1)

            @block.vector
            def _(e):
                ch = Chain(e, fin)
                e.wait_ge(u_sb, 2)
                ch.link(e.tensor_tensor(u2[:], u[:], u[:], ALU.mult))
                ch.link(e.tensor_scalar(u2[:], u2[:], 0.044715, 1.0, ALU.mult, ALU.add))
                e.tensor_tensor(u3[:], u2[:], u[:], ALU.mult).then_inc(act, 1)
                for t in range(NT):
                    e.wait_ge(sc_mm, t + 1)
                    e.scalar_tensor_tensor(rs[:, t, :], ps[t % 2][:, 0:NSLOT], RDIM ** -0.5, lrel[:],
                                           ALU.mult, ALU.add).then_inc(dve, 1)
                    e.scalar_tensor_tensor(at[:, t, :], ps[2 + t % 2][:, 0:NSLOT], BOT ** -0.5, lrel[:],
                                           ALU.mult, ALU.add).then_inc(dve, 1)
                e.wait_ge(dve, 2 * NT)
                for t in range(NT):
                    ch.step(e.max(out=top[:, t, :], in_=rs[:, t, :]))
                ch.wait()
                for t in range(NT):
                    ch.step(e.match_replace(out=rep[:, t, :], in_to_replace=top[:, t, :], in_values=rs[:, t, :],
                                            imm_value=-3.0e38))
                ch.wait()
                for t in range(NT):
                    ch.step(e.tensor_tensor(rs[:, t, :], rs[:, t, :], rep[:, t, :], ALU.not_equal))
                ch.wait()
                for t in range(NT):
                    ch.step(e.tensor_scalar(rep[:, t, :], rs[:, t, :], -1.0, BIG, ALU.add, ALU.mult))
                    ch.step(e.tensor_tensor(at[:, t, :], at[:, t, :], rs[:, t, :], ALU.mult))
                ch.wait()
                for t in range(NT):
                    ch.step(e.tensor_tensor(at[:, t, :], at[:, t, :], rep[:, t, :], ALU.add))
                ch.wait()
                for t in range(NT):
                    ch.link(e.tensor_reduce(mx[:, t:t + 1], at[:, t, :], AX.X, ALU.max))
                    e.tensor_scalar(mx[:, t:t + 1], mx[:, t:t + 1], -1.0, None, ALU.mult).then_inc(neg, 1)
                e.wait_ge(tanhed, 1)
                ch.step(e.tensor_scalar(u3[:], u3[:], 1.0, 0.5, ALU.add, ALU.mult))
                ch.wait()
                e.tensor_tensor(u[:], u[:], u3[:], ALU.mult).then_inc(gelu, 1)
                e.wait_ge(exped, NT)
                ch.link(e.reciprocal(den[:], den[:]))
                for t in range(NT):
                    e.tensor_scalar(at[:, t, :], at[:, t, :], den[:, t:t + 1], None, ALU.mult).then_inc(norm, 1)
                e.wait_ge(lv_mm, 1)
                ch.link(e.tensor_scalar(lvs[:], ps[4][:, 0:1], 1.0 / TOK, 1e-6, ALU.mult, ALU.add))
                ch.link(e.reciprocal(lvs[:], lvs[:]))
                ch.step(e.tensor_scalar(s2[:], lv[:], lvs[:], 0.5, ALU.mult, ALU.mult))
                e.wait_ge(lr_mm, 1)
                e.tensor_scalar(s1[:], ps[5][:, 0:NT], sc2[:, 0:1], None, ALU.add).then_inc(act, 1)
                e.wait_ge(ez, 1)
                ch.link(e.tensor_scalar(s1[:], s1[:], 1.0, None, ALU.add))
                ch.link(e.reciprocal(s1[:], s1[:]))
                ch.link(e.scalar_tensor_tensor(s1[:], s1[:], 2.5, s2[:], ALU.mult, ALU.add))
                ch.link(e.tensor_scalar(s1[:], s1[:], 0.0, 5.0, ALU.max, ALU.min))
                ch.link(e.tensor_scalar(s1[:], s1[:], -0.5, 1.0 / 1.5, ALU.add, ALU.mult))
                ch.link(e.tensor_scalar(s1[:], s1[:], 0.0, 1.0, ALU.max, ALU.min))
                e.tensor_scalar(gate[:], s1[:], sc2[:, 1:2], sc2[:, 2:3], ALU.mult, ALU.add).then_inc(act, 1)
                e.wait_ge(ez, 2)
                ch.link(e.tensor_scalar(gate[:], gate[:], 1.0, None, ALU.add))
                ch.link(e.reciprocal(gate[:], gate[:]))
                ch.link(e.tensor_scalar(msk[:], gate[:], 0.05, 0.5, ALU.is_ge, ALU.mult))
                ch.link(e.tensor_tensor(gate[:], gate[:], msk[:], ALU.mult))
                for t in range(NT):
                    ch.step(e.scalar_tensor_tensor(x[:, t, :], xn[:, t, :], 0.5, x[:, t, :], ALU.mult, ALU.add))
                ch.wait()
                for t in range(NT):
                    e.wait_ge(o_mm, t + 1)
                    e.scalar_tensor_tensor(x[:, t, :], ps[2 + t % 2][:, :], gate[:, t:t + 1], x[:, t, :],
                                           ALU.mult, ALU.add).then_inc(o_used, 1)


def attention(nc, g, name):
    x, ps, psum, d, ident = g["x"], g["ps"], g["psum"], g["dram"], g["ident"]
    QT = SEQ // P
    QPK = NH // NKV
    PAIRS = NH // 2
    M = QT * PAIRS
    NR = 1 + DT
    NV = NR + QT
    STACKS = NKV + DT * QPK
    ROWS = 32
    HALF = PAIRS // 2
    SCALE = AHD ** -0.5
    with ExitStack() as ctx:
        c = Chip(nc, ctx, name)
        hT = c.sb("hT", [P, DT, TOK])
        with ExitStack() as pre:
            xn = pre.enter_context(nc.sbuf_tensor(name + "xn", [P, NT, D], F32))
            norm_transpose(nc, g, name + "n_", hT, xn)
        wq, wo = (c.sb(n, [P, DT, D]) for n in ("wq", "wo"))
        wk, wv = (c.sb(n, [P, DT, NKV * AHD]) for n in ("wk", "wv"))
        cos, sin, rot = c.sb("cos", [P, SEQ]), c.sb("sin", [P, SEQ]), c.sb("rot", [P, P])
        cmask = c.sb("cmask", [P, P])
        sel = c.sb("sel", [P, 2, QPK + NKV, P], F32R)
        hb = c.sb("hb", [P, DT, SEQ])
        raw = c.sb("raw", [P, 2, SEQ])
        t0, t1 = c.sb("t0", [P, SEQ]), c.sb("t1", [P, SEQ])
        parts = c.pair("parts", [P, 2, SEQ])
        stack = c.sb("stack", [P, STACKS, SEQ], F32R)
        v = c.sb("v", [P, QT, NKV, ROWS])
        pr = c.sb("pr", [P, 2, 2, SEQ])
        pt = c.sb("pt", [P, 2, QT, QPK, P])
        mx = c.sb("mx", [P, 2, 2])
        nm = c.sb("nm", [P, 2, 2])
        den = c.sb("den", [P, 2, NH])
        rden = c.sb("rden", [P, NH // 2])
        og = c.sb("og", [P, SEQ])
        on = c.sb("on", [P, D])
        oT = c.sb("oT", [P, DT, P])
        w_in, hb_ready, proj, raw_ready, rotated, roped, hi_ready, lo_ready, placed, st_act, st_dve, sel_ready, \
            v_zero, scores, negmax, exped, turned, pt_act, pt_dve, pv, og_ready, og_turned, normed, o_turned, \
            oT_ready, out_mm, x_done, dve = (c.sem(s) for s in (
                "w_in", "hb_ready", "proj", "raw_ready", "rotated", "roped", "hi_ready", "lo_ready", "placed",
                "st_act", "st_dve", "sel_ready", "v_zero", "scores", "negmax", "exped", "turned", "pt_act",
                "pt_dve", "pv", "og_ready", "og_turned", "normed", "o_turned", "oT_ready", "out_mm", "x_done",
                "dve"))
        CR = 2
        LOADS = 9 * 16
        KV_S = QT * NKV

        def stacks_of(n):
            return range(NKV) if n == 0 else range(NKV + (n - 1) * QPK, NKV + n * QPK)

        def after_half(m, steps):
            k, r = divmod(m - steps, HALF)
            return k - 1 if r == 0 and k >= 1 else None

        with nc.Block() as block:
            @block.sync
            def _(e):
                for dst, src in ((wk, "wk"), (wq, "wq"), (wv, "wv"), (wo, "wo")):
                    e.dma_start(dst[:], d[src].rearrange("(a p) n -> p a n", p=P)).then_inc(w_in, 16)
                for dst, src in ((cos, "cos"), (sin, "sin"), (rot, "rot"), (cmask, "causal_add")):
                    e.dma_start(dst[:], d[src]).then_inc(w_in, 16)
                e.dma_start(pt[:].rearrange("p a t h q -> p (a t h q)")[:, 0:2 * (QPK + NKV) * P],
                            d["sel"]).then_inc(w_in, 16)

            @block.gpsimd
            def _(e):
                e.memset(v[:], 0.0).then_inc(v_zero, 1)
                with e.Fori(0, SEQS) as b:
                    e.wait_ge(raw_ready, b * NV + CR)
                    e.tensor_copy(hb[:], hT[:, :, bass.ds(b * SEQ, SEQ)]).then_inc(hb_ready, 1)

            @block.tensor
            def _(e):
                e.sem_inc(pv, CR)
                e.sem_inc(turned, CR)
                e.sem_inc(placed, CR)
                e.sem_inc(out_mm, 1)
                e.sem_inc(o_turned, 1)
                e.wait_ge(w_in, LOADS)
                e.wait_ge(sel_ready, 1)
                with e.Fori(0, SEQS) as b:
                    def project(n):
                        e.wait_ge(raw_ready, b * NV + n - 1 + CR)
                        bank = 4 + n % 2
                        if n < NR:
                            for a in range(DT):
                                w = wk[:, a, :] if n == 0 else wq[:, a, (n - 1) * P:n * P]
                                last = e.matmul(ps[bank], w, hb[:, a, :], start=a == 0, stop=a == DT - 1)
                        else:
                            t = n - NR
                            for a in range(DT):
                                last = e.matmul(psum[:, bank, 0:NKV * AHD], hb[:, a, t * P:(t + 1) * P],
                                                wv[:, a, :], start=a == 0, stop=a == DT - 1)
                        last.then_inc(proj, 1)

                    def rotate(n):
                        e.wait_ge(raw_ready, b * NV + n + 1 + CR)
                        e.wait_ge(roped, b * NR + n - 1 + CR)
                        e.matmul(ps[6 + n % 2], rot[:], raw[:, n % 2, :], start=True, stop=True).then_inc(rotated, 1)

                    def place(n):
                        e.wait_ge(hi_ready, b * NR + n + 1)
                        e.wait_ge(lo_ready, b * NR + n + 1)
                        for z in stacks_of(n):
                            e.wait_ge(st_act if z % 2 == 0 else st_dve, b * (STACKS // 2) + z // 2 - 1 + CR)
                            s = QPK + z if n == 0 else (z - NKV) % QPK
                            e.matmul(ps[z % 4], sel[:, 0, s, :], parts.hi[:, n % 2, :], start=True, stop=False)
                            e.matmul(ps[z % 4], sel[:, 1, s, :], parts.lo[:, n % 2, :], start=False,
                                     stop=True).then_inc(placed, 1)

                    e.wait_ge(hb_ready, b + 1)
                    e.wait_ge(exped, b * M + CR)
                    e.wait_ge(pt_act, b * M + CR)
                    e.wait_ge(pt_dve, b * M + CR)
                    e.wait_ge(og_ready, b * 2 * QT + 1)
                    e.wait_ge(x_done, b * QT + 1)
                    for i in range(NV):
                        project(i)
                        if 1 <= i <= NR:
                            rotate(i - 1)
                        if 2 <= i <= NR + 1:
                            place(i - 2)
                    e.wait_ge(st_act, (b + 1) * (STACKS // 2) + CR)
                    e.wait_ge(st_dve, (b + 1) * (STACKS // 2) + CR)
                    e.wait_ge(raw_ready, (b + 1) * NV + CR)

                    def score(m):
                        qt, u = divmod(m, PAIRS)
                        kv, first = u // 2, 2 * (u % 2)
                        e.wait_ge(exped, b * M + m - 1 + CR)
                        n = P * (qt + 1)
                        for h in range(2):
                            z = NKV + (kv // 2) * QPK + first + h
                            last = e.matmul(psum[:, 2 * (m % 2) + h, 0:n], stack[:, z, qt * P:(qt + 1) * P],
                                            stack[:, kv, 0:n], start=True, stop=True)
                        last.then_inc(scores, 1)

                    def turn(m):
                        qt, u = divmod(m, PAIRS)
                        e.wait_ge(exped, b * M + m + 1 + CR)
                        e.wait_ge(pt_act, b * M + m + CR)
                        e.wait_ge(pt_dve, b * M + m + CR)
                        for h in range(2):
                            for t in range(qt + 1):
                                last = e.transpose(psum[:, 4 + h, t * P:(t + 1) * P],
                                                   pr[:, m % 2, h, t * P:(t + 1) * P], ident[:])
                        last.then_inc(turned, 1)

                    def weigh(w):
                        qt, kv = divmod(w, NKV)
                        e.wait_ge(pt_act, b * M + 2 * w + 2 + CR)
                        e.wait_ge(pt_dve, b * M + 2 * w + 2 + CR)
                        r = ROWS * (kv % 4)
                        if r == 0:
                            e.wait_ge(og_ready, b * 2 * QT + w // 4 + 1)
                        for t in range(qt + 1):
                            last = e.matmul(psum[r:r + ROWS, 6, :], v[:, t, kv, :],
                                            pt[:, kv % 2, t, :, :].rearrange("p h q -> p (h q)"),
                                            start=t == 0, stop=t == qt)
                        last.then_inc(pv, 1)

                    def og_turn(k):
                        e.wait_ge(og_ready, b * 2 * QT + k + 1 + 1)
                        if k % 2 == 0:
                            e.wait_ge(x_done, b * QT + k // 2 + 1)
                        else:
                            e.wait_ge(normed, b * 2 * QT + k + CR)
                        for h in range(QPK):
                            last = e.transpose(psum[:, 7, h * P:(h + 1) * P], og[:, h * P:(h + 1) * P], ident[:])
                        last.then_inc(og_turned, 1)

                    def o_turn(qt):
                        e.wait_ge(normed, b * 2 * QT + 2 * qt + 2 + CR)
                        for a in range(DT):
                            last = e.transpose(psum[:, 7, a * P:(a + 1) * P], on[:, a * P:(a + 1) * P], ident[:])
                        last.then_inc(o_turned, 1)

                    def o_mul(qt):
                        e.wait_ge(oT_ready, b * QT + qt + 1)
                        for a in range(DT):
                            last = e.matmul(ps[7], oT[:, a, :], wo[:, a, :], start=a == 0, stop=a == DT - 1)
                        last.then_inc(out_mm, 1)

                    score(0)
                    score(1)
                    for m in range(M + 7):
                        if m + 2 < M:
                            score(m + 2)
                        if m < M:
                            turn(m)
                        if m % 2 == 0 and 2 <= m <= M:
                            weigh(m // 2 - 1)
                        k = after_half(m, 2)
                        if k is not None:
                            og_turn(k)
                        k = after_half(m, 4)
                        if k is not None and k % 2 == 1:
                            o_turn(k // 2)
                        k = after_half(m, 6)
                        if k is not None and k % 2 == 1:
                            o_mul(k // 2)

            @block.scalar
            def _(e):
                e.sem_inc(raw_ready, CR)
                e.sem_inc(exped, CR)
                e.sem_inc(pt_act, CR)
                e.sem_inc(st_act, CR)
                e.sem_inc(og_ready, 1)
                e.wait_ge(w_in, LOADS)
                e.copy(sel[:].rearrange("p a s n -> p (a s n)"),
                       pt[:].rearrange("p a t h q -> p (a t h q)")[:, 0:2 * (QPK + NKV) * P]).then_inc(sel_ready, 1)
                e.wait_ge(sel_ready, 1)
                e.wait_ge(v_zero, 1)
                with e.Fori(0, SEQS) as b:
                    for i in range(NV):
                        e.wait_ge(proj, b * NV + i + 1)
                        if i < NR:
                            e.wait_ge(roped, b * NR + i - 1 + CR)
                            e.copy(raw[:, i % 2, :], ps[4 + i % 2]).then_inc(raw_ready, 1)
                        else:
                            e.copy(v[:, i - NR, :, 0:AHD], psum[:, 4 + i % 2, 0:NKV * AHD].rearrange(
                                "p (h n) -> p h n", h=NKV)).then_inc(raw_ready, 1)
                        if 1 <= i <= NR:
                            n = i - 1
                            e.wait_ge(roped, b * NR + n + 1 + CR)
                            e.wait_ge(placed, b * STACKS + (stacks_of(n - 2)[-1] + 1 if n >= 2 else 0) + CR)
                            e.copy(parts.hi[:, n % 2, :], t0[:]).then_inc(hi_ready, 1)
                        if 2 <= i <= NR + 1:
                            for z in stacks_of(i - 2)[::2]:
                                e.wait_ge(placed, b * STACKS + z + 1 + CR)
                                e.copy(stack[:, z, :], ps[z % 4]).then_inc(st_act, 1)

                    def evacuate(m):
                        qt, u = divmod(m, PAIRS)
                        e.wait_ge(turned, b * M + m + 1 + CR)
                        e.wait_ge(pv, b * KV_S + m // 2 - 1 + CR)
                        e.copy(pt[:, (u // 2) % 2, 0:qt + 1, 2 * (u % 2), :],
                               psum[:, 4, 0:P * (qt + 1)].rearrange("p (t q) -> p t q", q=P)).then_inc(pt_act, 1)

                    for m in range(M + 7):
                        if m < M:
                            n = P * (m // PAIRS + 1)
                            e.wait_ge(negmax, b * M + m + 1)
                            e.wait_ge(turned, b * M + m - 1 + CR)
                            if m % PAIRS == 0:
                                e.wait_ge(normed, b * 2 * QT + 2 * (m // PAIRS) - 2 + CR)
                            for h in range(2):
                                hd = 2 * (m % PAIRS) + h
                                last = e.activation(pr[:, m % 2, h, 0:n], psum[:, 2 * (m % 2) + h, 0:n], ACT.Exp,
                                                    bias=nm[:, m % 2, h:h + 1], scale=SCALE,
                                                    accum_out=den[:, (m // PAIRS) % 2, hd:hd + 1])
                            last.then_inc(exped, 1)
                        if 1 <= m <= M:
                            evacuate(m - 1)
                        k = after_half(m, 1)
                        if k is not None:
                            e.wait_ge(pv, b * KV_S + 4 * (k + 1) + CR)
                            e.wait_ge(og_turned, b * 2 * QT + k + 1)
                            e.copy(og[:], ps[6]).then_inc(og_ready, 1)
                        k = after_half(m, 5)
                        if k is not None and k % 2 == 1:
                            qt = k // 2
                            e.wait_ge(o_turned, b * QT + qt + 1 + 1)
                            e.wait_ge(out_mm, b * QT + qt + 1)
                            e.copy(oT[:], psum[:, 7, :].rearrange("p (a n) -> p a n", a=DT)).then_inc(oT_ready, 1)

            @block.vector
            def _(e):
                e.sem_inc(roped, CR)
                e.sem_inc(pt_dve, CR)
                e.sem_inc(st_dve, CR)
                e.sem_inc(normed, CR)
                e.sem_inc(x_done, 1)
                e.sem_inc(og_turned, 1)
                e.wait_ge(w_in, LOADS)
                NC = NR * 2 + M * 2 + 2 * QT
                with e.Fori(0, SEQS) as b:
                    ch = Chain(e, dve, b * NC)
                    for i in range(1, NR + 2):
                        if i <= NR:
                            n = i - 1
                            e.wait_ge(raw_ready, b * NV + n + 1 + CR)
                            ch.step(e.tensor_tensor(t0[:], raw[:, n % 2, :], cos[:], ALU.mult))
                            e.wait_ge(rotated, b * NR + n + 1)
                            ch.link(e.tensor_tensor(t1[:], ps[6 + n % 2], sin[:], ALU.mult))
                            e.tensor_tensor(t0[:], t0[:], t1[:], ALU.add).then_inc(roped, 1)
                            e.wait_ge(hi_ready, b * NR + n + 1)
                            e.tensor_tensor(parts.lo[:, n % 2, :], t0[:], parts.hi_read[:, n % 2, :],
                                            ALU.subtract).then_inc(lo_ready, 1)
                            e.wait_ge(lo_ready, b * NR + n + 1)
                        if i >= 2:
                            for z in stacks_of(i - 2)[1::2]:
                                e.wait_ge(placed, b * STACKS + z + 1 + CR)
                                e.tensor_copy(stack[:, z, :], ps[z % 4]).then_inc(st_dve, 1)

                    def peak(m):
                        n = P * (m // PAIRS + 1)
                        s = psum[:, 2 * (m % 2):2 * (m % 2) + 2, :]
                        e.wait_ge(scores, b * M + m + 1)
                        ch.link(e.tensor_tensor(s[:, :, n - P:n], s[:, :, n - P:n],
                                                cmask[:, :].unsqueeze(1).to_broadcast([P, 2, P]), ALU.add))
                        ch.link(e.tensor_reduce(mx[:, m % 2, :], s[:, :, 0:n], AX.X, ALU.max))
                        e.wait_ge(exped, b * M + m - 1 + CR)
                        e.tensor_scalar(nm[:, m % 2, :], mx[:, m % 2, :], -SCALE, None, ALU.mult).then_inc(negmax, 1)

                    def evacuate(m):
                        qt, u = divmod(m, PAIRS)
                        e.wait_ge(turned, b * M + m + 1 + CR)
                        e.wait_ge(pv, b * KV_S + m // 2 - 1 + CR)
                        e.tensor_copy(pt[:, (u // 2) % 2, 0:qt + 1, 2 * (u % 2) + 1, :],
                                      psum[:, 5, 0:P * (qt + 1)].rearrange("p (t q) -> p t q", q=P)
                                      ).then_inc(pt_dve, 1)

                    def normalize(k):
                        qt, half = divmod(k, 2)
                        e.wait_ge(og_turned, b * 2 * QT + k + 1 + 1)
                        if half == 0:
                            e.wait_ge(o_turned, b * QT + qt + 1)
                        ch.link(e.reciprocal(rden[:], den[:, qt % 2, half * NH // 2:(half + 1) * NH // 2]))
                        e.tensor_tensor(
                            on[:, half * D // 2:(half + 1) * D // 2].rearrange("p (j h n) -> p j h n", j=4, h=QPK),
                            psum[:, 7, :].rearrange("p (h j n) -> p j h n", h=QPK, j=4)[:, :, :, 0:AHD],
                            rden[:, :].rearrange("p (j h) -> p j h", j=4).unsqueeze(3).to_broadcast(
                                [P, 4, QPK, AHD]), ALU.mult).then_inc(normed, 1)

                    peak(0)
                    for m in range(M + 8):
                        if m + 1 < M:
                            peak(m + 1)
                        if m < M:
                            evacuate(m)
                        k = after_half(m, 3)
                        if k is not None:
                            normalize(k)
                        k = after_half(m, 7)
                        if k is not None and k % 2 == 1:
                            qt = k // 2
                            e.wait_ge(out_mm, b * QT + qt + 1 + 1)
                            xv = x[:, bass.ds(b * QT + qt, 1), :].squeeze(1)
                            e.tensor_tensor(xv, xv, ps[7], ALU.add).then_inc(x_done, 1)
                    assert ch.n == NC


def mamba(nc, g, name):
    x, ps, psum, d, ident, ones, nhalf = (g[n] for n in ("x", "ps", "psum", "dram", "ident", "ones", "nhalf"))
    STEPS = SEQS * GROUPS
    NB = 2 + GT
    NRAW, NSPLIT = 4, 4
    HQ = [(0, 1), (2, 3, 4, 5), (6, 7, 8), (9,)]
    GQ = [(), (0,), (1, 2), (3, 4, 5, 6, 7)]
    assert sorted(sum(HQ, ())) == list(range(NB)) and sorted(sum(GQ, ())) == list(range(GT))
    tiles = [[("h", i) for i in HQ[c]] + [("g", i) for i in GQ[c]] for c in range(NCH)]
    USES = [("cbt", 0), ("btr", 0)] + tiles[0] + [("out", 0), ("out", 1)] + sum(tiles[1:], [])
    WTILES = tiles[0] + [("o", i) for i in range(GT)] + sum(tiles[1:], [])
    with ExitStack() as ctx:
        c_ = Chip(nc, ctx, name)
        hT = c_.pair("hT", [P, DT, TOK])
        t_dram = nc.dram_tensor(name + "t_dram", (P, SEQS * NCH, 3, HEADS), F32, kind="Internal").ap()
        a_dram = nc.dram_tensor(name + "a_dram", (HEADS, TOK), F32, kind="Internal").ap()
        e_dram = nc.dram_tensor(name + "e_dram", (HEADS, TOK), F32, kind="Internal").ap()
        nw = c_.sb("nw", [P, DT])
        nw_in = c_.sem("nw_in")
        with nc.Block() as block:
            @block.sync
            def _(e):
                e.dma_start(nw[:], d["norm_w"]).then_inc(nw_in, 16)
                e.wait_ge(nw_in, 16)
        with ExitStack() as pre:
            xn = pre.enter_context(nc.sbuf_tensor(name + "xn", [P, NT, D], F32))
            norm_transpose(nc, g, name + "n_", hT, xn, rms_w=nw)
        with ExitStack() as pre:
            time_steps(nc, g, Chip(nc, pre, name + "t_"), hT, t_dram, a_dram, e_dram)

        raw = c_.sb("raw", [P, NRAW, 512])
        w = c_.pair("w", [P, NSPLIT, 512])
        causal = c_.sb("causal", [P, P])
        cw = c_.sb("cw", [P, 2, NB, TAPS + 1])
        dgn = c_.sb("dgn", [P, 2, GT, 2])
        ts = c_.sb("ts", [P, 2, NCH, 3, HPG])
        hid = c_.sb("hid", [P, 2, GT, SEQ])
        bc = c_.sb("bc", [P, 2, 2, SEQ])
        gate = c_.sb("gate", [P, GT, SEQ])
        z = c_.sb("z", [P, GT, SEQ])
        zs = c_.pair("zs", [P, 2, SEQ])
        L = c_.sb("L", [P, 2, HPG, P])
        hc = c_.sb("hc", [P, GW])
        hcw = c_.sb("hcw", [P, GW])
        Eb = c_.sb("Eb", [P, 2, GT, P])
        yo = c_.sb("yo", [P, GT, P])
        prev = c_.sb("prev", [STATE, GW])
        eL = c_.sb("eL", [P, 2, HPG])
        cb = c_.sb("cb", [P, NCH, P])
        bt = c_.sb("bt", [P, NCH, STATE])
        sv, rstd = c_.sb("sv", [P, 4]), c_.sb("rstd", [P, 4])

        names = ("const_in", "ring_full", "w_hi", "w_lo", "cw_in", "dgn_in", "ts_in", "acc", "hid_ready", "turned",
                 "hc_ready", "hcw_ready", "subbed", "exped", "m_ready", "eL_ready", "ssd", "prev_ready",
                 "combined", "out_read", "dskip", "gated", "z_hi", "z_lo", "added", "out_used", "sum_mm", "sum_ready",
                 "rstd_ready", "dve")
        s = {n: c_.sem(n) for n in names}
        ring_free = [c_.sem(f"ring_free{i}") for i in range(2)]
        raw_in = [c_.sem(f"raw_in{i}") for i in range(NRAW)]
        L_in = [c_.sem(f"L_in{i}") for i in range(2)]
        E_in = [c_.sem(f"E_in{i}") for i in range(2)]
        CONST_IN = 16

        class Step:

            def __init__(self, k, grp, b, grp_next):
                self.k, self.grp, self.b, self.grp_next = k, grp, b, grp_next
                self.first = isinstance(k, int) and k == 0
                self.last = isinstance(k, int) and k == STEPS - 1
                self.par = b

        NU, NWT = len(USES), len(WTILES)
        assert NU % 2 == 0 and 2 * NWT % NSPLIT == 0

        def index(st, order, first_base, item):
            skipped = {"out", "o"}
            n0 = first_base - sum(i[0] in skipped for i in order)
            if st.first:
                return 0, first_base + [i for i in order if i[0] not in skipped].index(item)
            if st.last:
                return 0, n0 + st.k * len(order) + [i for i in order if i[0] != "h"].index(item)
            return len(order), n0 + order.index(item)

        def use(st, *item):
            f, n = index(st, USES, NB, item)
            return (st.k * f + n if f else n), n % 2

        def slot_count(st, *item):
            f, n = index(st, USES, NB, item)
            return st.k * (f // 2) + n // 2 if f else n // 2

        def wnumber(st, *item):
            f, n = index(st, WTILES, NB, item)
            return (st.k * f + n, st.par * f + n) if f else (n, n)

        def freed(st, *pos):
            return ring_free[use(st, *pos)[1]], slot_count(st, *pos) + 1

        def filled(st, *pos):
            return use(st, *pos)[0] + 1

        def freed_back(st, back, *item):
            n = NB - 2 + USES.index(item)
            return ring_free[n % 2], (st.k - back) * (NU // 2) + (n // 2 + 1)

        def raw_count(n, ns):
            return (n // NRAW + 1) * 16 if isinstance(n, int) else (n - (ns % NRAW)) * (16 // NRAW) + 16

        final = Step(STEPS - 1, GROUPS - 1, 1, None)
        END = use(final, "g", GT - 1)[0] + 1
        WEND = wnumber(final, "g", GT - 1)[0] + 1

        def run(eng, body):
            body(Step(0, 0, 0, 0))
            with eng.Fori(0, (STEPS - 2) // 2) as j:
                body(Step(j * 2 + 1, j, 1, j + 1))
                body(Step(j * 2 + 2, j + 1, 0, j + 1))
            body(Step(STEPS - 1, GROUPS - 1, 1, None))

        with nc.Block() as block:
            @block.sync
            def _(e):
                def part(name, v):
                    return d[name][bass.ds(v, 1)].squeeze(0) if not isinstance(v, int) else d[name][v]

                def load(n, ns, src):
                    if not isinstance(n, int) or n >= NRAW:
                        e.wait_ge(s["w_lo"], n - (NRAW - 1))
                    dst = raw[:, ns % NRAW, :]
                    if len(src.shape) == 3:
                        dst = dst.rearrange("p (a n) -> p a n", a=DT)
                    e.dma_start(dst, src).then_inc(raw_in[ns % NRAW], 16)

                def hidden(grp, i):
                    G = GROUPS * GT
                    return part("win", (grp + (2 * G + i * GROUPS)) if i < 2 else (grp * GT + (G + i - 2)))

                def out_weights(grp, i):
                    return part("wout", grp * GT + i)

                def load_scalars(st, grp, b, par):
                    src = bass.AP(tensor=t_dram.tensor, offset=grp * HPG + b * NCH * 3 * HEADS,
                                  ap=[[SEQS * NCH * 3 * HEADS, P], [HEADS, NCH * 3], [1, HPG]])
                    e.dma_start(ts[:, par].rearrange("p c q h -> p (c q) h"), src).then_inc(s["ts_in"], 16)

                e.dma_start(cw[:, 0], d["conv"][0]).then_inc(s["cw_in"], 16)
                load_scalars(None, 0, 0, 0)
                e.dma_start(causal[:], d["causal01"]).then_inc(s["const_in"], 16)
                for i in range(NB):
                    load(i, i, hidden(0, i))

                def body(st):
                    k = st.k
                    if not st.last:
                        if not st.first:
                            e.wait_ge(*freed_back(st, 2, "h", 9))
                        e.dma_start(cw[:, 1 - st.par], part("conv", st.grp_next)).then_inc(s["cw_in"], 16)
                    for kind, i in WTILES:
                        if (st.first and kind == "o") or (st.last and kind == "h"):
                            continue
                        n, ns = wnumber(st, kind, i)
                        if kind == "h":
                            load(n, ns, hidden(st.grp_next, i))
                        elif kind == "g":
                            load(n, ns, part("win", st.grp * GT + i))
                        else:
                            load(n, ns, out_weights(st.grp - (1 - st.b), i))
                        if (kind, i) == WTILES[len(tiles[0]) + GT - 1] or (st.first and (kind, i) == ("h", 1)):
                            if not st.first:
                                e.wait_ge(s["ssd"], k * NCH)
                            e.dma_start(dgn[:, st.par], part("dgn", st.grp)).then_inc(s["dgn_in"], 16)
                            if not st.last:
                                load_scalars(st, st.grp_next, 1 - st.b, 1 - st.par)

                run(e, body)
                for i in range(GT):
                    load(WEND + i, WEND + i, out_weights(GROUPS - 1, i))

            @block.tensor
            def _(e):
                def bank_for(st, *item):
                    bank = use(st, *item)[1]
                    e.wait_ge(ring_free[bank], slot_count(st, *item))
                    return bank

                def project(n, ns, rhs_b, bank):
                    e.wait_ge(s["w_lo"], n + 1)
                    wh, wl = (t[:, ns % NSPLIT, :].rearrange("p (a n) -> p a n", a=DT) for t in (w.hi, w.lo))
                    for a in range(DT):
                        sl = (slice(None), a, slice(rhs_b * SEQ, (rhs_b + 1) * SEQ))
                        last = matmul3(e, ps[bank], wh[:, a, :], wl[:, a, :], hT.hi[sl], hT.lo[sl],
                                       a == 0, a == DT - 1)
                    last.then_inc(s["ring_full"], 1)

                for i in range(NB):
                    if i >= 2:
                        e.wait_ge(ring_free[i % 2], i // 2)
                    project(i, i, 0, i % 2)

                def sums(k):
                    e.wait_ge(s["added"], k)
                    if k is not STEPS:
                        e.wait_ge(s["prev_ready"], k * 3 + 1)
                    for t in range(4):
                        last = e.matmul(psum[:, 2, t:t + 1], gate[:, 0, t * P:(t + 1) * P], ones[:, 0:1],
                                        start=True, stop=True)
                    last.then_inc(s["sum_mm"], 1)

                def out_product(k, number, banks):
                    e.wait_ge(s["combined"], k * NCH)
                    for i in range(GT):
                        n, ns = number(i)
                        e.wait_ge(s["w_lo"], n + 1)
                        e.wait_ge(s["z_lo"], k * GT + (i - GT + 1))
                        if i == GT - 1:
                            sums(k)
                        for t in range(4):
                            sl = (slice(None), i % 2, slice(t * P, (t + 1) * P))
                            last = matmul3(e, ps[banks[t]], zs.hi[sl], zs.lo[sl], w.hi[:, ns % NSPLIT, :],
                                           w.lo[:, ns % NSPLIT, :], i == 0, i == GT - 1)
                            if i == GT - 1 and t < 2:
                                last.then_inc(s["ring_full"], 1)
                        last.then_inc(s["out_used"], 1)

                def body(st):
                    k, par = st.k, st.par
                    q = k * NCH
                    e.wait_ge(s["hid_ready"], k * NB + NB)
                    bank = bank_for(st, "cbt", 0)
                    for c in range(NCH):
                        cs = slice(c * P, (c + 1) * P)
                        last = e.matmul(psum[:, bank, cs], bc[:, par, 0, cs], bc[:, par, 1, cs], start=True, stop=True)
                    last.then_inc(s["ring_full"], 1)
                    bank = bank_for(st, "btr", 0)
                    for c in range(NCH):
                        cs = slice(c * P, (c + 1) * P)
                        last = e.transpose(psum[:, bank, cs], bc[:, par, 0, cs], ident[:])
                    last.then_inc(s["ring_full"], 1)

                    def states(c):
                        e.wait_ge(s["hcw_ready"], k * 3 + (c + 1))
                        e.wait_ge(*freed(st, "btr", 0))
                        for i in range(2):
                            last = e.matmul(ps[2 + i], bt[:, c, :], hcw[:, i * 512:i * 512 + 512],
                                            start=True, stop=True)
                        return last

                    def project_tile(kind, i):
                        n, ns = wnumber(st, kind, i)
                        project(n, ns, 1 - par if kind == "h" else par, bank_for(st, kind, i))

                    for c in range(NCH):
                        cs = slice(c * P, (c + 1) * P)
                        early = [t for t in tiles[c] if not (st.last and t[0] == "h")][:1] if c > 1 else []
                        for t in early:
                            project_tile(*t)
                        if c:
                            e.wait_ge(s["prev_ready"], k * 3 + c)
                            if c == 1 and not st.first:
                                e.wait_ge(s["sum_ready"], k)
                        elif not st.first:
                            e.wait_ge(s["hc_ready"], q)
                        for i in range(GT):
                            last = e.transpose(psum[:, 2 + i // 4, (i % 4) * P:(i % 4 + 1) * P],
                                               hid[:, par, i, cs], ident[:])
                        last.then_inc(s["turned"], 1)
                        for t in tiles[c]:
                            if t not in early and not (st.last and t[0] == "h"):
                                project_tile(*t)
                        if not (st.first and c == 0):
                            e.wait_ge(s["combined"], q + c)
                        if c:
                            if c == 1 and not st.first:
                                e.wait_ge(s["out_read"], k)
                            for i in range(GT):
                                e.matmul(psum[:, 6 + i // 4, (i % 4) * P:(i % 4 + 1) * P],
                                         prev[:, i * P:(i + 1) * P], bc[:, par, 1, cs], start=True, stop=True)
                        e.wait_ge(s["hc_ready"], q + c + 1)
                        if c in (1, 2):
                            states(c)
                        e.wait_ge(s["m_ready"], q + c + 1)
                        for h in range(HPG):
                            i = h // 2
                            lo = HD * (h % 2)
                            last = e.matmul(psum[lo:lo + HD, 4 + i // 4, (i % 4) * P:(i % 4 + 1) * P],
                                            hc[:, h * HD:(h + 1) * HD], L[:, c % 2, h, :], start=True, stop=True)
                        if c == 0:
                            last = states(0)
                        last.then_inc(s["ssd"], 1)
                        if c == 0 and not st.first:
                            out_product(k, lambda i: wnumber(st, "o", i),
                                        (bank_for(st, "out", 0), bank_for(st, "out", 1), 6, 7))

                run(e, body)
                for n in (END, END + 1):
                    e.wait_ge(ring_free[n % 2], n // 2)
                out_product(STEPS, lambda i: (WEND + i, WEND + i), (END % 2, (END + 1) % 2, 6, 7))

            @block.scalar
            def _(e):
                a3 = a_dram.rearrange("h t -> (h t)")
                e3 = e_dram.rearrange("h t -> (h t)")

                def load_decays(grp, b, c):
                    off = grp * (HPG * TOK) + (b * SEQ + c * P)
                    ap = bass.AP(tensor=a3.tensor, offset=off, ap=[[0, P], [TOK, HPG], [1, P]])
                    e.dma_start(L[:, c % 2], ap).then_inc(L_in[c % 2], 16)

                def load_starts(grp, b, c):
                    for half in range(2):
                        off = grp * (HPG * TOK) + (half * TOK + b * SEQ + c * P)
                        ap = bass.AP(tensor=e3.tensor, offset=off, ap=[[0, HD], [2 * TOK, GT], [1, P]])
                        e.dma_start(Eb[HD * half:HD * half + HD, c % 2], ap).then_inc(E_in[c % 2], 16)

                def target(par, i):
                    return bc[:, par, i, :] if i < 2 else hid[:, par, i - 2, :]

                def newest_tap(par, i, bank):
                    e.activation(target(par, i), ps[bank], ACT.Identity, bias=cw[:, par, i, TAPS:TAPS + 1],
                                 scale=cw[:, par, i, TAPS - 1:TAPS]).then_inc(s["acc"], 1)

                def silu(par, i, convolved):
                    e.wait_ge(*convolved)
                    t = target(par, i)
                    e.activation(t, t, ACT.Silu).then_inc(s["hid_ready"], 1)

                def decay(q, c):
                    e.wait_ge(s["subbed"], q + (c + 1))
                    Lc = L[:, c % 2].rearrange("p h i -> p (h i)")
                    e.activation(Lc, Lc, ACT.Exp).then_inc(s["exped"], 1)

                def split(n, ns):
                    if isinstance(n, int) and n >= WEND + GT:
                        return
                    e.wait_ge(raw_in[ns % NRAW], raw_count(n, ns))
                    e.copy(w.hi[:, ns % NSPLIT, :], raw[:, ns % NRAW, :]).then_inc(s["w_hi"], 1)

                def z_part(k, i, par):
                    e.wait_ge(s["gated"], k * GT + (i - GT + 1))
                    e.activation(gate[:, i, :], z[:, i, :], ACT.Square)
                    e.activation(zs.hi[:, i % 2, :], z[:, i, :], ACT.Copy, scale=dgn[:, par, i, 1:2]
                                 ).then_inc(s["z_hi"], 1)

                def z_parts(k, par, ahead):
                    for i in range(GT):
                        e.wait_ge(s["out_used"], k * GT + (i - GT + 1))
                        if i + 2 < GT:
                            z_part(k, i + 2, par)
                        split(*ahead(i))

                load_decays(0, 0, 0)
                for i in range(NSPLIT):
                    split(i, i)
                e.wait_ge(s["cw_in"], 16)
                for i in range(NB):
                    e.wait_ge(s["ring_full"], i + 1)
                    newest_tap(0, i, i % 2)
                    split(i + NSPLIT, i + NSPLIT)
                for i in range(NB):
                    silu(0, i, (ring_free[i % 2], i // 2 + 1))
                decay(0, 0)

                def body(st):
                    k, par = st.k, st.par
                    q = k * NCH

                    def ahead(*item):
                        n, ns = wnumber(st, *item)
                        return n + NSPLIT, ns + NSPLIT

                    if not st.last:
                        e.wait_ge(s["cw_in"], k * 16 + 32)
                    e.wait_ge(s["ring_full"], filled(st, "btr", 0))
                    if not st.first:
                        e.wait_ge(s["ssd"], q)
                    bank = use(st, "btr", 0)[1]
                    e.copy(bt[:, :, :].rearrange("p c n -> p (c n)"), ps[bank]).then_inc(ring_free[bank], 1)
                    def tap(i):
                        e.wait_ge(s["ring_full"], filled(st, "h", i))
                        if i >= 2 and not st.first:
                            e.wait_ge(s["dskip"], k * GT + (i - 2 - GT + 1))
                        newest_tap(1 - par, i, use(st, "h", i)[1])
                        split(*ahead("h", i))

                    def load_next(c):
                        if st.last and c == 3:
                            return
                        if not (st.first and c == 0):
                            e.wait_ge(s["ssd"], q + c)
                            e.wait_ge(s["combined"], q + c)
                        if c < 3:
                            load_decays(st.grp, st.b, c + 1)
                            load_starts(st.grp, st.b, c + 1)
                        else:
                            load_decays(st.grp_next, 1 - st.b, 0)

                    def whole_decay(c):
                        e.wait_ge(L_in[c % 2], k * 32 + 16 * (c // 2 + 1))
                        if not st.first:
                            e.wait_ge(s["prev_ready"], k * 3 + (c - 2))
                        e.activation(eL[:, c - 1, :], L[:, c % 2, :, P - 1], ACT.Exp).then_inc(s["eL_ready"], 1)

                    for c in range(NCH):
                        h_tiles = [i for kind, i in tiles[c] if kind == "h" and not st.last]
                        if c == 0:
                            load_next(0)
                        for i in h_tiles[:1]:
                            tap(i)
                        if c:
                            load_next(c)
                        for i in h_tiles[1:2]:
                            tap(i)
                        if c == 1:
                            decay(q, 1)
                        for i in h_tiles[2:]:
                            tap(i)
                        if c == 0 and not st.first:
                            z_part(k, 0, 1 - par)
                            z_part(k, 1, 1 - par)
                        if c < 2:
                            whole_decay(c + 1)
                        if c == 0 and not st.first:
                            z_parts(k, 1 - par, lambda i: ahead("o", i))
                        for kind, i in tiles[c]:
                            if kind == "g":
                                e.wait_ge(s["ring_full"], filled(st, "g", i))
                                if not st.first:
                                    e.wait_ge(s["sum_mm"], k)
                                bank = use(st, "g", i)[1]
                                e.activation(gate[:, i, :], ps[bank], ACT.Silu).then_inc(ring_free[bank], 1)
                                split(*ahead("g", i))
                        for i in (h_tiles if c > 1 else range(max(HQ[1]) + 1) if c == 1 and not st.last else ()):
                            silu(1 - par, i, freed(st, "h", i))
                        if c in (1, 2):
                            decay(q, c + 1)
                    if not st.last:
                        decay(q + NCH, 0)

                run(e, body)
                z_part(STEPS, 0, 1)
                z_part(STEPS, 1, 1)
                z_parts(STEPS, 1, lambda i: (WEND + i + NSPLIT, WEND + i + NSPLIT))

            @block.gpsimd
            def _(e):
                def split(n, ns):
                    if isinstance(n, int) and n >= WEND + GT:
                        return
                    e.wait_ge(s["w_hi"], n + 1)
                    sl = (slice(None), ns % NSPLIT, slice(None))
                    e.tensor_tensor(w.lo[sl], raw[:, ns % NRAW, :], w.hi_read[sl], ALU.subtract
                                    ).then_inc(s["w_lo"], 1)

                def gate_product(k, i):
                    e.wait_ge(s["dskip"], k * GT + (i - GT + 1))
                    e.tensor_tensor(z[:, i, :], z[:, i, :], gate[:, i, :], ALU.mult).then_inc(s["gated"], 1)

                def inverse_norm(k):
                    e.wait_ge(s["sum_ready"], k)
                    e.tensor_tensor(rstd[:], sv[:], nhalf[:, 0:4], ALU.pow).then_inc(s["rstd_ready"], 1)

                for i in range(NSPLIT + NB):
                    split(i, i)

                def body(st):
                    k = st.k

                    def ahead(*item):
                        n, ns = wnumber(st, *item)
                        split(n + NSPLIT, ns + NSPLIT)

                    def decayed(c):
                        e.wait_ge(s["hc_ready"], k * NCH + (c + 1))
                        if not (st.first and c == 0):
                            e.wait_ge(s["ssd"], k * NCH + c)
                        e.tensor_tensor(hcw[:, :].rearrange("p (h n) -> p h n", h=HPG),
                                        hc[:, :].rearrange("p (h n) -> p h n", h=HPG),
                                        ts[:, st.par, c, 2, :].unsqueeze(2).to_broadcast([P, HPG, HD]),
                                        ALU.mult).then_inc(s["hcw_ready"], 1)

                    decayed(0)
                    if not st.first:
                        e.wait_ge(*freed_back(st, 1, "g", GT - 1))
                        gate_product(k, 0)
                        gate_product(k, 1)
                    if not st.last:
                        ahead("h", 0)
                    if not st.first:
                        gate_product(k, 2)
                    if not st.last:
                        ahead("h", 1)
                    if not st.first:
                        gate_product(k, 3)
                        for i in range(GT - 1):
                            if i + 4 < GT:
                                gate_product(k, i + 4)
                            ahead("o", i)
                        inverse_norm(k)
                        ahead("o", GT - 1)
                    for c in (1, 2, 3):
                        todo = [t for t in tiles[c] if not (st.last and t[0] == "h")]
                        for t in todo[:2]:
                            ahead(*t)
                        if c < 3:
                            decayed(c)
                        for t in todo[2:]:
                            ahead(*t)

                run(e, body)
                e.wait_ge(*freed(final, "g", GT - 1))
                for i in range(GT):
                    gate_product(STEPS, i)
                for i in range(GT):
                    split(WEND + i + NSPLIT, WEND + i + NSPLIT)
                inverse_norm(STEPS)

            @block.vector
            def _(e):
                def convolve(par, i, bank, k1):
                    t = bc[:, par, i, :] if i < 2 else hid[:, par, i - 2, :]
                    e.wait_ge(s["acc"], k1 * NB + i + 1)
                    for n in (1, 2, 3):
                        ins = e.scalar_tensor_tensor(t[:, n:], ps[bank][:, :SEQ - n], cw[:, par, i, 3 - n:4 - n],
                                                     t[:, n:], ALU.mult, ALU.add)
                        if n < 3:
                            ch.link(ins)
                    ins.then_inc(ring_free[bank], 1)

                def masked_products(st):
                    n, bank = use(st, "cbt", 0)
                    e.wait_ge(s["ring_full"], n + 1)
                    e.tensor_tensor(cb[:], ps[bank].rearrange("p (c i) -> p c i", c=NCH),
                                    causal[:, :].unsqueeze(1).to_broadcast([P, NCH, P]), ALU.mult
                                    ).then_inc(ring_free[bank], 1)

                def combine(q, k, c):
                    e.wait_ge(s["ssd"], q + c + 1)
                    yd = psum[:, 4:6, :].rearrange("p b (i n) -> p (b i) n", i=4)
                    zo = psum[:, 6:8, :].rearrange("p b (i n) -> p (b i) n", i=4)
                    zc = z[:, :, c * P:(c + 1) * P]
                    if c == 0:
                        e.tensor_copy(zc, yd).then_inc(s["combined"], 1)
                    else:
                        e.wait_ge(E_in[c % 2], k * (64 if c % 2 else 32) + (64 if c == 3 else 32))
                        ch.link(e.tensor_tensor(yo[:], zo, Eb[:, c % 2], ALU.mult))
                        e.tensor_tensor(zc, yo[:], yd, ALU.add).then_inc(s["combined"], 1)

                def skips(k, par, which):
                    e.wait_ge(s["combined"], k * NCH)
                    e.wait_ge(s["dgn_in"], k * 16)
                    for i in which:
                        e.scalar_tensor_tensor(z[:, i, :], hid[:, par, i, :], dgn[:, par, i, 0:1], z[:, i, :],
                                               ALU.mult, ALU.add).then_inc(s["dskip"], 1)

                def decay_arguments(k, par, c):
                    e.wait_ge(L_in[c % 2], k * 32 + 16 * (c // 2 + 1))
                    if c == 0:
                        e.wait_ge(s["ts_in"], k * 16 + 16)
                    if c in (1, 2):
                        e.wait_ge(s["eL_ready"], k * 2 + c)
                    for h in range(HPG):
                        last = e.tensor_scalar(L[:, c % 2, h, :], L[:, c % 2, h, :], ts[:, par, c, 1, h:h + 1], 0.0,
                                               ALU.subtract, ALU.min)
                    last.then_inc(s["subbed"], 1)

                def hidden_by_token(st, c):
                    k, q = st.k, st.k * NCH
                    e.wait_ge(s["turned"], q + c + 1)
                    if not (st.first and c == 0):
                        e.wait_ge(s["ssd"], q + c)
                    e.tensor_tensor(hc[:, :].rearrange("p (h n) -> p h n", h=HPG),
                                    psum[:, 2:4, :].rearrange("p b (h n) -> p (b h) n", n=HD),
                                    ts[:, st.par, c, 0, :].unsqueeze(2).to_broadcast([P, HPG, HD]),
                                    ALU.mult).then_inc(s["hc_ready"], 1)

                def decayed_products(st, c):
                    q = st.k * NCH
                    e.wait_ge(s["exped"], q + c + 1)
                    if c == 0:
                        e.wait_ge(*freed(st, "cbt", 0))
                    e.tensor_tensor(L[:, c % 2], L[:, c % 2], cb[:, c, :].unsqueeze(1).to_broadcast([P, HPG, P]),
                                    ALU.mult).then_inc(s["m_ready"], 1)

                def next_state(st, c):
                    k = st.k
                    e.wait_ge(s["ssd"], k * NCH + (c + 1))
                    S = psum[:, 2:4, :].rearrange("p b n -> p (b n)")
                    if c == 0:
                        e.tensor_copy(prev[:], S).then_inc(s["prev_ready"], 1)
                    else:
                        p3 = prev[:, :].rearrange("p (h n) -> p h n", h=HPG)
                        ch.link(e.tensor_tensor(p3, p3, eL[:, c - 1, :].unsqueeze(2).to_broadcast([P, HPG, HD]),
                                                ALU.mult))
                        e.tensor_tensor(prev[:], prev[:], S, ALU.add).then_inc(s["prev_ready"], 1)

                def z_low(k, i, par):
                    e.wait_ge(s["z_hi"], k * GT + (i - GT + 1))
                    e.scalar_tensor_tensor(zs.lo[:, i % 2, :], z[:, i, :], dgn[:, par, i, 1:2],
                                           zs.hi_read[:, i % 2, :], ALU.mult, ALU.subtract).then_inc(s["z_lo"], 1)
                    if i:
                        ins = e.tensor_tensor(gate[:, 0, :], gate[:, 0, :], gate[:, i, :], ALU.add)
                        if i < GT - 1:
                            ch.link(ins)
                        else:
                            ins.then_inc(s["added"], 1)

                def outputs(k, b, where):
                    e.wait_ge(s["sum_mm"], k)
                    e.tensor_scalar(sv[:], psum[:, 2, 0:4], 1.0 / GW, EPS, ALU.mult, ALU.add
                                    ).then_inc(s["sum_ready"], 1)
                    e.wait_ge(s["out_used"], k * GT)
                    e.wait_ge(s["rstd_ready"], k)
                    for t in range(4):
                        bank = where[t]
                        xt = x[:, b * 4 + t, :]
                        ins = e.scalar_tensor_tensor(xt, ps[bank], rstd[:, t:t + 1], xt, ALU.mult, ALU.add)
                        if t < 2:
                            ins.then_inc(ring_free[bank], 1)
                    ins.then_inc(s["out_read"], 1)

                ch = Chain(e, s["dve"])
                e.wait_ge(s["const_in"], CONST_IN)
                e.wait_ge(s["cw_in"], 16)
                for i in range(NB):
                    convolve(0, i, i % 2, 0)
                decay_arguments(0, 0, 0)
                total = {"first": None}
                PER = NB * 2 + 3 + 2 + 6

                def body(st):
                    nonlocal ch
                    k, par, q = st.k, st.par, st.k * NCH
                    if not st.first:
                        ch = Chain(e, s["dve"], (k - 1) * PER + total["first"])

                    def conv(c, which=slice(None)):
                        for i in HQ[c][which] if not st.last else ():
                            convolve(1 - par, i, use(st, "h", i)[1], k + 1)

                    masked_products(st)
                    if not st.first:
                        combine((k - 1) * NCH, k - 1, 3)
                    hidden_by_token(st, 0)
                    decayed_products(st, 0)
                    if not st.first:
                        skips(k, 1 - par, (0, 1))
                    conv(0)
                    if st.first:
                        next_state(st, 0)
                    else:
                        z_low(k, 0, 1 - par)
                        z_low(k, 1, 1 - par)
                        skips(k, 1 - par, (2, 3))
                        z_low(k, 2, 1 - par)
                        skips(k, 1 - par, (4,))
                        z_low(k, 3, 1 - par)
                        skips(k, 1 - par, (5, 6, 7))
                        z_low(k, 4, 1 - par)
                        z_low(k, 5, 1 - par)
                        next_state(st, 0)
                        z_low(k, 6, 1 - par)
                        z_low(k, 7, 1 - par)
                        outputs(k, 1 - par, (use(st, "out", 0)[1], use(st, "out", 1)[1], 6, 7))
                    for c in (1, 2, 3):
                        if c > 1:
                            next_state(st, c - 1)
                        combine(q, k, c - 1)
                        hidden_by_token(st, c)
                        if c == 1:
                            decay_arguments(k, par, 1)
                        conv(c, slice(0, 2))
                        decayed_products(st, c)
                        conv(c, slice(2, None))
                        if c < 3:
                            decay_arguments(k, par, c + 1)
                    if not st.last:
                        decay_arguments(k + 1, 1 - par, 0)
                    if st.first:
                        total["first"] = ch.n
                    elif not st.last:
                        assert ch.n == PER, ch.n

                run(e, body)
                ch = Chain(e, s["dve"], (STEPS - 2) * PER + total["first"] + ch.n)
                combine((STEPS - 1) * NCH, STEPS - 1, 3)
                skips(STEPS, 1, range(GT))
                for i in range(GT):
                    z_low(STEPS, i, 1)
                outputs(STEPS, 1, (END % 2, (END + 1) % 2, 6, 7))


def time_steps(nc, g, c_, hT, t_dram, a_dram, e_dram):
    ps, psum, d, ident = g["ps"], g["psum"], g["dram"], g["ident"]
    w, ws = c_.sb("w", [P, DT, HEADS]), c_.pair("ws", [P, DT, HEADS])
    TS = c_.sb("TS", [P, SEQS * NCH, 3, HEADS])
    hp = c_.sb("hp", [P, 2])
    A = c_.sb("A", [P, 1])
    zz, az, ez, w1 = (c_.sb(n, [P, TOK]) for n in ("zz", "az", "ez", "w1"))
    dt, acs, dec, E = (c_.sb(n, [P, TOK]) for n in ("dt", "acs", "dec", "E"))
    one = c_.sb("one", [P, P])
    w_in, mm, zz_ready, az_ready, ez_ready, w1_ready, ln_ready, a_ready, acs_ready, e_ready, dif, dec_ready, turned, \
        copied, stored, dve, init, w_hi, w_lo = (
            c_.sem(n) for n in ("w_in", "mm", "zz_ready", "az_ready", "ez_ready", "w1_ready", "ln_ready", "a_ready",
                                "acs_ready", "e_ready", "dif", "dec_ready", "turned", "copied", "stored", "dve",
                                "init", "w_hi", "w_lo"))
    NTC = TOK // CHUNK
    with nc.Block() as block:
        @block.sync
        def _(e):
            e.dma_start(w[:], d["win"][-1 + (2 * INNER + 2 * GROUPS * STATE + HEADS) // P]).then_inc(w_in, 16)
            e.dma_start(hp[:], d["heads"]).then_inc(w_in, 16)
            e.wait_ge(acs_ready, NTC)
            e.dma_start(a_dram, acs[:]).then_inc(stored, 16)
            e.wait_ge(e_ready, 1)
            e.dma_start(e_dram, E[:]).then_inc(stored, 16)
            e.wait_ge(copied, 6)
            e.dma_start(t_dram, TS[:]).then_inc(stored, 16)
            e.wait_ge(stored, 48)

        @block.tensor
        def _(e):
            e.wait_ge(w_lo, 1)
            for h in range(SEQS):
                for a in range(DT):
                    sl = (slice(None), a, slice(h * SEQ, (h + 1) * SEQ))
                    last = matmul3(e, ps[h], ws.hi[:, a, :], ws.lo[:, a, :], hT.hi[sl], hT.lo[sl], a == 0,
                                   a == DT - 1)
                last.then_inc(mm, 1)
            for n, (src, sem, v) in enumerate(((dt, acs_ready, NTC), (acs, acs_ready, NTC), (dec, dec_ready, 1))):
                e.wait_ge(sem, v)
                for t in range(NTC):
                    last = e.transpose(psum[:, 2 + 2 * n + t // 4, (t % 4) * P:(t % 4 + 1) * P],
                                       src[:, t * P:(t + 1) * P], ident[:])
                    if t % 4 == 3:
                        last.then_inc(turned, 1)

        @block.vector
        def _(e):
            ch = Chain(e, dve)
            e.memset(one[:], 1.0).then_inc(init, 1)
            e.wait_ge(w_hi, 1)
            e.tensor_tensor(ws.lo[:], w[:], ws.hi_read, ALU.subtract).then_inc(w_lo, 1)
            for h in range(SEQS):
                e.wait_ge(mm, h + 1)
                e.tensor_scalar(zz[:, h * SEQ:(h + 1) * SEQ], ps[h], hp[:, 0:1], None, ALU.add).then_inc(zz_ready, 1)
            e.wait_ge(ez_ready, 1)
            e.tensor_scalar(w1[:], ez[:], 1.0, None, ALU.add).then_inc(w1_ready, 1)
            e.wait_ge(w1_ready, 1)
            ch.link(e.scalar_tensor_tensor(ez[:], w1[:], -1.0, ez[:], ALU.add, ALU.subtract))
            ch.link(e.scalar_tensor_tensor(dt[:], zz[:], 0.0, ez[:], ALU.max, ALU.subtract))
            e.wait_ge(ln_ready, 1)
            ch.link(e.tensor_tensor(dt[:], dt[:], az[:], ALU.add))
            e.wait_ge(a_ready, 1)
            ch.link(e.tensor_scalar(A[:], A[:], -1.0, None, ALU.mult))
            ch.link(e.tensor_scalar(w1[:], dt[:], A[:, 0:1], None, ALU.mult))
            e.wait_ge(init, 1)
            for t in range(NTC):
                sl = slice(t * P, (t + 1) * P)
                e.tensor_tensor_scan(acs[:, sl], one[:], w1[:, sl], 0.0, ALU.mult, ALU.add).then_inc(acs_ready, 1)
            e.wait_ge(acs_ready, NTC)
            a3 = acs[:, :].rearrange("p (t n) -> p t n", t=NTC)
            e.tensor_tensor(dec[:, :].rearrange("p (t n) -> p t n", t=NTC),
                            a3[:, :, P - 1:P].to_broadcast([P, NTC, P]), a3, ALU.subtract).then_inc(dif, 1)
            for n in range(6):
                e.wait_ge(turned, n + 1)
                src = ps[2 + n].rearrange("p (t h) -> p t h", t=4)
                e.tensor_copy(TS[:, 4 * (n % 2):4 * (n % 2) + 4, n // 2, :], src).then_inc(copied, 1)

        @block.scalar
        def _(e):
            e.wait_ge(w_in, 32)
            e.copy(ws.hi[:], w[:]).then_inc(w_hi, 1)
            e.activation(A[:], hp[:, 1:2], ACT.Exp).then_inc(a_ready, 1)
            e.wait_ge(zz_ready, SEQS)
            e.activation(az[:], zz[:], ACT.Abs).then_inc(az_ready, 1)
            e.wait_ge(az_ready, 1)
            e.activation(ez[:], az[:], ACT.Exp, scale=-1.0).then_inc(ez_ready, 1)
            e.wait_ge(w1_ready, 1)
            e.activation(az[:], w1[:], ACT.Ln).then_inc(ln_ready, 1)
            e.wait_ge(acs_ready, NTC)
            e.activation(E[:], acs[:], ACT.Exp).then_inc(e_ready, 1)
            e.wait_ge(dif, 1)
            e.activation(dec[:], dec[:], ACT.Exp).then_inc(dec_ready, 1)


def build(nc, d, out, stages):
    ctx = ExitStack()
    with ctx:
        c = Chip(nc, ctx, "s_")
        g = {"dram": d, "x": c.sb("x", [P, NT, D]), "ident": c.sb("ident", [P, P]), "ones": c.sb("ones", [P, P]),
             "nhalf": c.sb("nhalf", [P, 16]),
             "psum": ctx.enter_context(nc.psum_tensor("psum", [P, 8, 512], F32))}
        g["ps"] = [g["psum"][:, i, :] for i in range(8)]
        loaded, stored, const = c.sem("loaded"), c.sem("stored"), c.sem("const")
        xv = d["x"].rearrange("(t p) n -> p t n", p=P)
        with nc.Block() as block:
            @block.sync
            def _(e):
                e.dma_start(g["x"][:], xv).then_inc(loaded, 16)
                e.dma_start(g["ident"][:], d["ident"]).then_inc(loaded, 16)
                e.wait_ge(loaded, 32)

            @block.gpsimd
            def _(e):
                e.memset(g["ones"][:], 1.0).then_inc(const, 1)
                e.memset(g["nhalf"][:], -0.5).then_inc(const, 1)
                e.wait_ge(const, 2)
        for n, s in enumerate(stages):
            STAGES[s](nc, g, f"{s}{n}_")
        with nc.Block() as block:
            @block.sync
            def _(e):
                e.dma_start(out.rearrange("(t p) n -> p t n", p=P), g["x"][:]).then_inc(stored, 16)
                e.wait_ge(stored, 16)


STAGES = {"ffn": q4_ffn, "mamba": mamba, "routed": routed_ffn, "attn": attention}
ORDER = ["ffn", "mamba", "ffn", "routed", "attn", "routed"]


def shape_constants():
    c = {"ident": np.eye(P, dtype=np.float32)}
    c["causal01"] = np.triu(np.ones((P, P), np.float32))
    c["causal_add"] = np.where(np.tri(P, dtype=bool), 0.0, -1e30).astype(np.float32)
    hi, lo = (0, 4), (28, 28)
    sh = np.zeros((P, 5, 2), np.int32)
    for p in range(P):
        sh[p, 0] = hi if p < 64 else lo
        for k in range(4):
            sh[p, k + 1] = lo if ((k * HID + p) // 64) % 2 else hi
    for dd in range(D):
        for f in range(0, HID, 32):
            assert tuple(sh[f % P, dd % 4 + 1]) == (lo if ((dd * HID + f) // 64) % 2 else hi)
    c["shifts"] = sh
    inv = (1.0 / np.float32(10000.0) ** (np.arange(0, AHD, 2, dtype=np.float32) / np.float32(AHD))).astype(np.float32)
    fr = np.outer(np.arange(SEQ, dtype=np.float32), inv).astype(np.float32)
    emb = np.concatenate([fr, fr], -1).T
    c["cos"] = np.tile(np.cos(emb), (P // AHD, 1)).astype(np.float32)
    c["sin"] = np.tile(np.sin(emb), (P // AHD, 1)).astype(np.float32)
    rot = np.zeros((P, P), np.float32)
    for h in range(P // AHD):
        for i in range(AHD // 2):
            rot[h * AHD + i + AHD // 2, h * AHD + i] = -1.0
            rot[h * AHD + i, h * AHD + i + AHD // 2] = 1.0
    c["rot"] = rot
    qpk = NH // NKV
    sel = np.zeros((P, 2, qpk + NKV, P), np.float32)
    for r in range(AHD):
        for half in range(2):
            for i in range(qpk):
                for part in range(2):
                    for dup in range(2):
                        sel[(half * qpk + i) * AHD + r, part, i, 64 * half + 32 * part + 16 * dup + r] = 1.0
        for kv in range(NKV):
            for part in range(2):
                for dup in range(2):
                    sel[kv * AHD + r, part, qpk + kv, 64 * (kv % 2) + 32 * dup + 16 * part + r] = 1.0
    c["sel"] = sel.reshape(P, -1)
    return c


def layouts(i):
    a = {k: np.asarray(v) for k, v in i.items()}
    o = {"x": a["L0_attn_x"].reshape(TOK, D)}
    for n in ("1", "3"):
        o["w" + n] = a["L0_ffn_w" + n].reshape(HID, DT, 64).transpose(2, 1, 0)
        o["s" + n] = a["L0_ffn_s" + n].reshape(HID, DT, 2).transpose(2, 1, 0)
    w2 = a["L0_ffn_w2"]
    o["w2"] = np.repeat(w2[:, None, :], 2, axis=1).reshape(D, HID).T
    o["s2"] = np.repeat(a["L0_ffn_s2"], 2).reshape(D, HID // 32).T
    wi = a["L0_attn_in_proj_w"]
    o["win"] = wi.reshape(-1, P, DT, P).transpose(0, 3, 2, 1)
    o["wout"] = a["L0_attn_out_proj_w"].T.reshape(GROUPS * GT, P, D)
    cw = np.concatenate([a["L0_attn_conv_w"], a["L0_attn_conv_b"][:, None]], axis=1)
    ct = cw.reshape(-1, P, TAPS + 1)
    o["conv"] = np.stack([np.stack([ct[GROUPS * GT + gr], ct[GROUPS * GT + GROUPS + gr],
                                    *ct[gr * GT:(gr + 1) * GT]], axis=1) for gr in range(GROUPS)])
    dp = np.repeat(a["L0_attn_Dp"], HD).reshape(GROUPS, GT, P)
    gn = a["L0_attn_gnorm_w"].reshape(GROUPS, GT, P)
    o["dgn"] = np.stack([dp, gn], axis=-1).transpose(0, 2, 1, 3)
    o["norm_w"] = a["L0_attn_norm_w"].reshape(DT, P).T
    o["heads"] = np.stack([a["L0_attn_dt_bias"], a["L0_attn_A_log"]], axis=1)
    o["wq"] = a["L1_attn_Wq"].T
    o["wk"] = a["L1_attn_Wk"].T
    o["wv"] = a["L1_attn_Wv"].T
    o["wo"] = a["L1_attn_Wo"].T
    o["rWqT"] = a["L1_ffn_Wq"].T
    o["WrT"] = a["L1_ffn_Wr"].T
    o["akT"] = a["L1_ffn_aux_keys"].T
    o["avT"] = a["L1_ffn_aux_values"].T
    o["WvdT"] = a["L1_ffn_Wvd"].T
    o["WvuT"] = a["L1_ffn_Wvu"].T
    o["Wu1T"] = a["L1_ffn_Wu1"].T
    o["bu1"] = a["L1_ffn_bu1"][:, None]
    o["Wu2"] = a["L1_ffn_Wu2"].T
    o["bu2"] = a["L1_ffn_bu2"]
    o["gate_w1"] = a["L1_ffn_gate_w1"].reshape(1)
    o["gate_bias"] = a["L1_ffn_gate_bias"].reshape(1)
    o["lrel"] = a["L1_ffn_log_rel"]
    o = {k: np.ascontiguousarray(v) for k, v in o.items()}
    o.update({k: np.ascontiguousarray(v) for k, v in shape_constants().items()})
    return o


def kernel(**inputs):
    import concourse.bacc as _bacc
    from concourse.bass_utils import run_bass_kernel_spmd as _run

    nc = _bacc.Bacc("TRN2", target_bir_lowering=False, num_devices=1)
    arrays = {f"in_{k}": v for k, v in layouts(inputs).items()}
    d = {k[3:]: nc.dram_tensor(k, v.shape, mybir.dt.from_np(v.dtype), kind="ExternalInput").ap()
         for k, v in arrays.items()}
    out = nc.dram_tensor("out_0_dram", (TOK, D), F32, kind="ExternalOutput").ap()
    build(nc, d, out, ORDER)
    r = _run(nc, [arrays], core_ids=[0])
    return r.results[0]["out_0_dram"].reshape(SEQS, SEQ, D)
```
